# Optimizing a Trainium2 kernel written in Bass

```python
import numpy as np
import jax
import jax.numpy as jnp

def _softmax(x, axis=-1):
    return jax.nn.softmax(x, axis=axis)

def _gelu(x):
    return jax.nn.gelu(x, approximate=True)

def _silu(x):
    return jax.nn.silu(x)

def _sigmoid(x):
    return jax.nn.sigmoid(x)

def _layernorm(x, axis=-1, eps=1e-05):
    m = jnp.mean(x, axis=axis, keepdims=True)
    v = jnp.var(x, axis=axis, keepdims=True)
    return (x - m) / jnp.sqrt(v + eps)

def _scatter_add(tgt, idx, src, axis=0):
    return tgt.at[idx].add(src)

def _segment_sum(src, seg, n):
    return jax.ops.segment_sum(src, seg, n)
kernel_name = 'mk_flamingo_gated_d2_seqx_r4_9627af'

def setup_inputs(seed: int=0):
    np.random.seed(seed)
    _w = jnp.asarray

    def _rec_inputs():
        import jax
        import jax.numpy as jnp
        _rk = jax.random.key(seed)
        x = -0.000125 + 0.9999 * jax.random.normal(jax.random.fold_in(_rk, 1), (2, 1024, 256), jnp.float32)
        _lenS = 1024 - jax.random.randint(jax.random.fold_in(_rk, 7), (2,), 0, max(1, 1024 // 4) + 1, jnp.int32)
        _lenS2 = 77 - jax.random.randint(jax.random.fold_in(_rk, 8), (2,), 0, max(1, 77 // 4) + 1, jnp.int32)
        _ctx_1024P = jax.random.normal(jax.random.fold_in(_rk, 11), (2, 16, 256), jnp.float32)
        _ctx_1024c = jax.random.dirichlet(jax.random.fold_in(_rk, 511), 0.3 * jnp.ones((16,), jnp.float32), (2, 77))
        _ctx_1024t = jnp.einsum('bsk,bkd->bsd', _ctx_1024c, _ctx_1024P)
        _ctx_1024t = _ctx_1024t * jax.lax.rsqrt(jnp.mean(jnp.square(_ctx_1024t)) + 1e-12) * 0.953939
        ctx_1024 = -1.52775e-05 + 0.999936 * (_ctx_1024t + 0.3 * jax.random.normal(jax.random.fold_in(_rk, 611), (2, 77, 256), jnp.float32))
        _g = jax.random.normal(jax.random.fold_in(_rk, 9001), (2, 2), jnp.float32)
        _g = jnp.sign(_g) * jnp.maximum(jnp.abs(_g), 1.0) + (_g == 0) * 1.0
        g_xattn = _g[0]
        g_ffn = _g[1]
        return (x, ctx_1024, g_xattn, g_ffn)
    x, ctx_1024, g_xattn, g_ffn = _rec_inputs()

    def _L0_xattn_setup():
        import jax, jax.numpy as jnp
        import numpy as np
        B, LP, LQ, H = (16, 512, 512, 256)
        key = jax.random.key(seed)
        k1, k2, k3 = jax.random.split(key, 3)
        proj_p = jax.random.normal(k1, (B, LP, H), dtype=jnp.float32)
        proj_q = jax.random.normal(k2, (B, LQ, H), dtype=jnp.float32)
        W = jax.random.normal(k3, (H, H), dtype=jnp.float32) * (1.0 / np.sqrt(H))
        b = jnp.zeros((H,), dtype=jnp.float32)
        return {'proj_p': proj_p, 'proj_q': proj_q, 'W': W, 'b': b}
    _L0_xattn_all = _L0_xattn_setup()
    _L0_xattn_in = {k: v for k, v in _L0_xattn_all.items() if k in ('W', 'b')}
    del _L0_xattn_all

    def _L0_ffn_setup():
        import jax, jax.numpy as jnp
        import numpy as np
        LN_EPS = 1e-05

        def layernorm(x, g, b):
            mu = jnp.mean(x, axis=-1, keepdims=True)
            var = jnp.mean((x - mu) ** 2, axis=-1, keepdims=True)
            return (x - mu) * jax.lax.rsqrt(var + LN_EPS) * g + b

        def act_quant_fake(x):
            scale = 127.0 / jnp.clip(jnp.max(jnp.abs(x), axis=-1, keepdims=True), 1e-05)
            return jnp.clip(jnp.round(x * scale), -128.0, 127.0) / scale

        def weight_quant_fake(w):
            scale = 1.0 / jnp.clip(jnp.mean(jnp.abs(w)), 1e-05)
            return jnp.clip(jnp.round(w * scale), -1.0, 1.0) / scale

        def bitlinear(x, w, b):
            dqx = act_quant_fake(x)
            dqw = weight_quant_fake(w)
            return jnp.einsum('btd,hd->bth', dqx, dqw) + b
        key = jax.random.key(seed)
        ks = jax.random.split(key, 5)
        B, T, D, H = (8, 1024, 256, 1024)
        return {'x': jax.random.normal(ks[0], (B, T, D), dtype=jnp.float32), 'ln1_g': jnp.ones((D,), jnp.float32), 'ln1_b': jnp.zeros((D,), jnp.float32), 'w1': jax.random.normal(ks[1], (H, D), dtype=jnp.float32) * (1.0 / np.sqrt(D)), 'b1': jax.random.normal(ks[2], (H,), dtype=jnp.float32) * 0.02, 'ln2_g': jnp.ones((H,), jnp.float32), 'ln2_b': jnp.zeros((H,), jnp.float32), 'w2': jax.random.normal(ks[3], (D, H), dtype=jnp.float32) * (1.0 / np.sqrt(H)), 'b2': jax.random.normal(ks[4], (D,), jnp.float32) * 0.02}
    _L0_ffn_all = _L0_ffn_setup()
    _L0_ffn_in = {k: v for k, v in _L0_ffn_all.items() if k in ('ln1_g', 'ln1_b', 'w1', 'b1', 'ln2_g', 'ln2_b', 'w2', 'b2')}
    del _L0_ffn_all

    def _L1_xattn_setup():
        import jax, jax.numpy as jnp
        import numpy as np
        EPS = 0.001
        LEAKY_ALPHA = 0.2

        def layer_norm(x, gamma, beta):
            mu = jnp.mean(x, axis=-1, keepdims=True)
            var = jnp.mean(jnp.square(x - mu), axis=-1, keepdims=True)
            return (x - mu) * jax.lax.rsqrt(var + EPS) * gamma + beta

        def attention_head(x_k, x_v, x_q, Wk, Wq, Wv, use_mask):
            K = x_k @ Wk
            V = x_v @ Wv
            Q = x_q @ Wq
            Lq, Lk = (Q.shape[1], K.shape[1])
            score = jnp.einsum('bqd,bkd->bqk', Q, K) / jnp.sqrt(jnp.float32(Lk))
            if use_mask:
                mask = jnp.triu(jnp.full((Lq, Lk), -jnp.inf, dtype=score.dtype), k=1)
                score = score + mask
            return jax.nn.softmax(score, axis=-1) @ V
        key = jax.random.key(seed)
        ks = jax.random.split(key, 12)
        B, S, D = (8, 512, 256)
        inp = {'inputs': jax.random.normal(ks[0], (B, S, D), jnp.float32), 'context_sequence': jax.random.normal(ks[1], (B, S, D), jnp.float32), 'Wk1': jax.random.normal(ks[2], (D, D), jnp.float32) * 0.01, 'Wq1': jax.random.normal(ks[3], (D, D), jnp.float32) * 0.01, 'Wv1': jax.random.normal(ks[4], (D, D), jnp.float32) * 0.01, 'Wk2': jax.random.normal(ks[5], (D, D), jnp.float32) * 0.01, 'Wq2': jax.random.normal(ks[6], (D, D), jnp.float32) * 0.01, 'Wv2': jax.random.normal(ks[7], (D, D), jnp.float32) * 0.01, 'W1': jax.random.normal(ks[8], (D, D), jnp.float32) * (1.0 / np.sqrt(D)), 'b1': jnp.zeros((D,), jnp.float32), 'W2': jax.random.normal(ks[9], (D, D), jnp.float32) * (1.0 / np.sqrt(D)), 'b2': jnp.zeros((D,), jnp.float32), 'gamma': jnp.ones((D,), jnp.float32), 'beta': jnp.zeros((D,), jnp.float32)}
        return inp
    _L1_xattn_all = _L1_xattn_setup()
    _L1_xattn_in = {k: v for k, v in _L1_xattn_all.items() if k in ('Wk1', 'Wq1', 'Wv1', 'Wk2', 'Wq2', 'Wv2', 'W1', 'b1', 'W2', 'b2', 'gamma', 'beta')}
    del _L1_xattn_all

    def _L1_ffn_setup():
        import jax, jax.numpy as jnp
        import numpy as np
        N_EMBED = 256
        FFN_HIDDEN = 1024
        NUM_EXPERTS = 8
        TOP_K = 2
        key = jax.random.key(seed)
        ks = jax.random.split(key, 8)
        d, f, E = (N_EMBED, FFN_HIDDEN, NUM_EXPERTS)
        s_d = 1.0 / np.sqrt(d)
        s_f = 1.0 / np.sqrt(f)
        return {'x': jax.random.normal(ks[0], (2, 512, d), dtype=jnp.float32), 'Wg': jax.random.uniform(ks[1], (d, E), jnp.float32, -s_d, s_d), 'bg': jax.random.uniform(ks[2], (E,), jnp.float32, -s_d, s_d), 'W1': jax.random.uniform(ks[3], (E, d, f), jnp.float32, -s_d, s_d), 'b1': jax.random.uniform(ks[4], (E, f), jnp.float32, -s_d, s_d), 'W2': jax.random.uniform(ks[5], (E, f, d), jnp.float32, -s_f, s_f), 'b2': jax.random.uniform(ks[6], (E, d), jnp.float32, -s_f, s_f)}
    _L1_ffn_all = _L1_ffn_setup()
    _L1_ffn_in = {k: v for k, v in _L1_ffn_all.items() if k in ('Wg', 'bg', 'W1', 'b1', 'W2', 'b2')}
    del _L1_ffn_all
    return {'x': x, 'ctx_1024': ctx_1024, 'g_xattn': g_xattn, 'g_ffn': g_ffn, 'L0_xattn_W': _L0_xattn_in['W'], 'L0_xattn_b': _L0_xattn_in['b'], 'L0_ffn_ln1_g': _L0_ffn_in['ln1_g'], 'L0_ffn_ln1_b': _L0_ffn_in['ln1_b'], 'L0_ffn_w1': _L0_ffn_in['w1'], 'L0_ffn_b1': _L0_ffn_in['b1'], 'L0_ffn_ln2_g': _L0_ffn_in['ln2_g'], 'L0_ffn_ln2_b': _L0_ffn_in['ln2_b'], 'L0_ffn_w2': _L0_ffn_in['w2'], 'L0_ffn_b2': _L0_ffn_in['b2'], 'L1_xattn_Wk1': _L1_xattn_in['Wk1'], 'L1_xattn_Wq1': _L1_xattn_in['Wq1'], 'L1_xattn_Wv1': _L1_xattn_in['Wv1'], 'L1_xattn_Wk2': _L1_xattn_in['Wk2'], 'L1_xattn_Wq2': _L1_xattn_in['Wq2'], 'L1_xattn_Wv2': _L1_xattn_in['Wv2'], 'L1_xattn_W1': _L1_xattn_in['W1'], 'L1_xattn_b1': _L1_xattn_in['b1'], 'L1_xattn_W2': _L1_xattn_in['W2'], 'L1_xattn_b2': _L1_xattn_in['b2'], 'L1_xattn_gamma': _L1_xattn_in['gamma'], 'L1_xattn_beta': _L1_xattn_in['beta'], 'L1_ffn_Wg': _L1_ffn_in['Wg'], 'L1_ffn_bg': _L1_ffn_in['bg'], 'L1_ffn_W1': _L1_ffn_in['W1'], 'L1_ffn_b1': _L1_ffn_in['b1'], 'L1_ffn_W2': _L1_ffn_in['W2'], 'L1_ffn_b2': _L1_ffn_in['b2']}

def reference(x, ctx_1024, g_xattn, g_ffn, L0_xattn_W, L0_xattn_b, L0_ffn_ln1_g, L0_ffn_ln1_b, L0_ffn_w1, L0_ffn_b1, L0_ffn_ln2_g, L0_ffn_ln2_b, L0_ffn_w2, L0_ffn_b2, L1_xattn_Wk1, L1_xattn_Wq1, L1_xattn_Wv1, L1_xattn_Wk2, L1_xattn_Wq2, L1_xattn_Wv2, L1_xattn_W1, L1_xattn_b1, L1_xattn_W2, L1_xattn_b2, L1_xattn_gamma, L1_xattn_beta, L1_ffn_Wg, L1_ffn_bg, L1_ffn_W1, L1_ffn_b1, L1_ffn_W2, L1_ffn_b2):
    import jax
    import jax.numpy as jnp

    def _L0_xattn_ref(proj_p, proj_q, W, b):
        import jax, jax.numpy as jnp
        import numpy as np
        B, LP, LQ, H = (16, 512, 512, 256)
        trans_q = jnp.einsum('bqh,oh->bqo', proj_q, W) + b
        att_weights = jnp.einsum('bph,bqh->bpq', proj_p, trans_q)
        att_norm = jax.nn.softmax(att_weights, axis=-1)
        att_vec = jnp.einsum('bpq,bqh->bph', att_norm, proj_q)
        out = jax.nn.relu(jnp.einsum('bph,oh->bpo', att_vec, W) + b)
        return out

    def _L0_ffn_ref(x, ln1_g, ln1_b, w1, b1, ln2_g, ln2_b, w2, b2):
        import jax, jax.numpy as jnp
        import numpy as np
        LN_EPS = 1e-05

        def layernorm(x, g, b):
            mu = jnp.mean(x, axis=-1, keepdims=True)
            var = jnp.mean((x - mu) ** 2, axis=-1, keepdims=True)
            return (x - mu) * jax.lax.rsqrt(var + LN_EPS) * g + b

        def act_quant_fake(x):
            scale = 127.0 / jnp.clip(jnp.max(jnp.abs(x), axis=-1, keepdims=True), 1e-05)
            return jnp.clip(jnp.round(x * scale), -128.0, 127.0) / scale

        def weight_quant_fake(w):
            scale = 1.0 / jnp.clip(jnp.mean(jnp.abs(w)), 1e-05)
            return jnp.clip(jnp.round(w * scale), -1.0, 1.0) / scale

        def bitlinear(x, w, b):
            dqx = act_quant_fake(x)
            dqw = weight_quant_fake(w)
            return jnp.einsum('btd,hd->bth', dqx, dqw) + b
        h = layernorm(x, ln1_g, ln1_b)
        h = bitlinear(h, w1, b1)
        h = jax.nn.gelu(h, approximate=False)
        h = layernorm(h, ln2_g, ln2_b)
        h = bitlinear(h, w2, b2)
        return h

    def _L1_xattn_ref(inputs, context_sequence, Wk1, Wq1, Wv1, Wk2, Wq2, Wv2, W1, b1, W2, b2, gamma, beta):
        import jax, jax.numpy as jnp
        import numpy as np
        EPS = 0.001
        LEAKY_ALPHA = 0.2

        def layer_norm(x, gamma, beta):
            mu = jnp.mean(x, axis=-1, keepdims=True)
            var = jnp.mean(jnp.square(x - mu), axis=-1, keepdims=True)
            return (x - mu) * jax.lax.rsqrt(var + EPS) * gamma + beta

        def attention_head(x_k, x_v, x_q, Wk, Wq, Wv, use_mask):
            K = x_k @ Wk
            V = x_v @ Wv
            Q = x_q @ Wq
            Lq, Lk = (Q.shape[1], K.shape[1])
            score = jnp.einsum('bqd,bkd->bqk', Q, K) / jnp.sqrt(jnp.float32(Lk))
            if use_mask:
                mask = jnp.triu(jnp.full((Lq, Lk), -jnp.inf, dtype=score.dtype), k=1)
                score = score + mask
            return jax.nn.softmax(score, axis=-1) @ V
        att = attention_head(inputs, inputs, inputs, Wk1, Wq1, Wv1, use_mask=True)
        norm = layer_norm(att + inputs, gamma, beta)
        att2 = attention_head(context_sequence, context_sequence, att, Wk2, Wq2, Wv2, use_mask=False)
        norm2 = layer_norm(att2 + norm, gamma, beta)
        h = jax.nn.leaky_relu(norm2 @ W1 + b1, negative_slope=LEAKY_ALPHA)
        ff = h @ W2 + b2
        norm3 = layer_norm(ff + norm2, gamma, beta)
        return jax.nn.relu(norm3)

    def _L1_ffn_ref(x, Wg, bg, W1, b1, W2, b2):
        import jax, jax.numpy as jnp
        import numpy as np
        N_EMBED = 256
        FFN_HIDDEN = 1024
        NUM_EXPERTS = 8
        TOP_K = 2
        gate_scores = jax.nn.softmax(x @ Wg + bg, axis=-1)
        topk_scores, topk_idx = jax.lax.top_k(gate_scores, TOP_K)
        topk_scores = topk_scores / (jnp.sum(topk_scores, axis=-1, keepdims=True) + 1e-08)
        onehot = jax.nn.one_hot(topk_idx, NUM_EXPERTS, dtype=x.dtype)
        combine_w = jnp.einsum('bsk,bske->bse', topk_scores, onehot)
        output = jnp.zeros_like(x)
        for e in range(NUM_EXPERTS):
            h = jax.nn.gelu(x @ W1[e] + b1[e])
            y = h @ W2[e] + b2[e]
            output = output + y * combine_w[..., e:e + 1]
        return output
    x = x + jnp.tanh(g_xattn[0]) * _L0_xattn_ref(_layernorm(x, axis=-1), ctx_1024, L0_xattn_W, L0_xattn_b)
    x = x + jnp.tanh(g_ffn[0]) * _L0_ffn_ref(_layernorm(x, axis=-1), L0_ffn_ln1_g, L0_ffn_ln1_b, L0_ffn_w1, L0_ffn_b1, L0_ffn_ln2_g, L0_ffn_ln2_b, L0_ffn_w2, L0_ffn_b2)
    x = x + jnp.tanh(g_xattn[1]) * _L1_xattn_ref(_layernorm(x, axis=-1), ctx_1024, L1_xattn_Wk1, L1_xattn_Wq1, L1_xattn_Wv1, L1_xattn_Wk2, L1_xattn_Wq2, L1_xattn_Wv2, L1_xattn_W1, L1_xattn_b1, L1_xattn_W2, L1_xattn_b2, L1_xattn_gamma, L1_xattn_beta)
    x = x + jnp.tanh(g_ffn[1]) * _L1_ffn_ref(_layernorm(x, axis=-1), L1_ffn_Wg, L1_ffn_bg, L1_ffn_W1, L1_ffn_b1, L1_ffn_W2, L1_ffn_b2)
    return x

_drawn_inputs = setup_inputs


def setup_inputs(seed=0):
    import zlib

    import numpy as np

    out = dict(_drawn_inputs(seed))
    spreads = {'g_ffn': (-1.0, 0.6),
     'L0_xattn_b': (0.0, 0.1),
     'L0_ffn_ln1_g': (1.0, 0.2),
     'L0_ffn_ln1_b': (0.0, 0.1),
     'L0_ffn_ln2_g': (1.0, 0.2),
     'L0_ffn_ln2_b': (0.0, 0.1),
     'L1_xattn_b1': (0.0, 0.1),
     'L1_xattn_b2': (0.0, 0.1),
     'L1_xattn_gamma': (1.0, 0.2),
     'L1_xattn_beta': (0.0, 0.1)}
    factors = {'L0_ffn_b1': 2.668,
     'L0_ffn_b2': 3.513,
     'L1_xattn_Wk1': 25.128,
     'L1_xattn_Wq1': 22.068,
     'L1_xattn_Wk2': 64.0,
     'L1_xattn_Wq2': 64.0,
     'L1_ffn_b1': 7.707,
     'L1_ffn_b2': 5.454}
    for name, (base, spread) in spreads.items():
        noise = np.random.default_rng([zlib.crc32(name.encode()), seed]).standard_normal(out[name].shape)
        drawn = base * np.exp(spread * noise) if base else spread * noise
        out[name] = jnp.asarray(drawn.astype(out[name].dtype))
    for name, factor in factors.items():
        out[name] = (out[name] * factor).astype(out[name].dtype)
    return out
```

```python
from contextlib import ExitStack

import concourse.bass as bass
from concourse import mybir

F32 = mybir.dt.float32
BF16 = mybir.dt.bfloat16
I32 = mybir.dt.int32
U32 = mybir.dt.uint32
ALU = mybir.AluOpType
ACT = mybir.ActivationFunctionType
X = mybir.AxisListType.X

P = 128
MAGIC = 1.5 * 2.0 ** 23
LN_EPS = 1e-5
L1_EPS = 1e-3
MASKED = -1e30


def gated_blocks_kernel(
    nc: bass.Bass, x, ctx_in, g_xattn, g_ffn,
    W, Wb, ln1_g, ln1_b, w1, b1, ln2_g, ln2_b, w2, b2,
    Wk1, Wq1, Wv1, Wk2, Wq2, Wv2, F1, f1b, F2, f2b, gamma, beta,
    Wg, bg, E1, e1b, E2, e2b, out,
):
    B, S, D = x.shape
    C = ctx_in.shape[1]
    H = w1.shape[0]
    E = Wg.shape[1]
    DC, HC = D // P, H // P
    NT = B * S // P
    TB = S // P
    G = 4
    GB = TB // G
    DV = D + C
    K = 2
    SLOTS = B * S * K
    TILES = (SLOTS + E * (P - 1)) // P
    U = 3
    TURN = 2 * U
    assert D == 256 and S == 1024 and H == 1024 and TILES % U == 0 and TB == GB * G
    EW = 2 * DC * H + 2 * HC * D
    BLK = 1024
    EBLK = EW // 2 // BLK
    EARLY = 6

    split_rows = nc.dram_tensor("split_rows", (B * S, 2 * D), BF16, kind="Internal").ap()
    choice_rows = nc.dram_tensor("choice_rows", (SLOTS + P, D), F32, kind="Internal").ap()

    x_tiles = x.rearrange("b (t p) d -> p (b t) d", p=P)
    out_tiles = out.rearrange("b (t p) d -> p (b t) d", p=P)

    with ExitStack() as stack:
        def sem(name):
            return stack.enter_context(nc.semaphore(name))

        def keep(name, shape, dt=F32):
            return stack.enter_context(nc.sbuf_tensor(name, shape, dt))

        ps = stack.enter_context(nc.psum_tensor("ps", [P, 8, 512], F32))

        def bank(k):
            return ps[:, k, :]

        def bank16(k):
            return ps[:, k, :].bitcast(BF16)

        res = keep("res", [P, NT, D])
        EWS = keep("EWS", [P, E, EW], BF16)
        stage_in = keep("stage_in", [P, 2, BLK])
        ident = keep("ident", [P, P])
        ident16 = keep("ident16", [P, P], BF16)
        causal = keep("causal", [P, P])
        gates = keep("gates", [P, 4])
        minus_half = keep("minus_half", [P, G])
        stats = keep("stats", [P, G, 6])
        moments = keep("moments", [P, 2, G, 2])
        rstd = keep("rstd", [P, 2, G])
        expert_b1 = keep("expert_b1", [P, E * HC])
        logits = keep("logits", [P, NT, E])
        Wg_s = keep("Wg_s", [P, DC, E])
        bg_s = keep("bg_s", [P, E])
        e2b_s = keep("e2b_s", [E, D])
        zero_col = keep("zero_col", [P, 1])

        def expert_w1(e, part):
            return EWS[:, e, part * DC * H:(part + 1) * DC * H].rearrange("p (c h) -> p c h", c=DC)

        def expert_w2(e, part):
            base = 2 * DC * H + part * HC * D
            return EWS[:, e, base:base + HC * D].rearrange("p (m d) -> p m d", m=HC)

        def block_parts(e, k):
            if k < EBLK // 2:
                return expert_w1(e, 0)[:, k, :], expert_w1(e, 1)[:, k, :]
            m = (k - EBLK // 2) * (HC // 2)
            return tuple(expert_w2(e, part)[:, m:m + HC // 2, :].rearrange("p m d -> p (m d)")
                         for part in range(2))

        spare = EWS[:, EARLY:E, :].rearrange("p e n -> p (e n)").bitcast(F32)
        spare_size = (E - EARLY) * EW // 2

        def carve(sizes):
            at, views = 0, []
            for n in sizes:
                views.append(spare[:, at:at + n])
                at += n
            assert at <= spare_size
            return views

        early3 = ExitStack()
        stack.enter_context(early3)

        def sb3(name, shape, dt=F32):
            return early3.enter_context(nc.sbuf_tensor(name, shape, dt))

        M1 = sb3("M1", [P, DC, D])
        WVA = sb3("WVA", [P, B, DC, DV])
        V2 = sb3("V2", [C, B, D])
        F1_s = sb3("F1_s", [P, DC, D])
        F2_s = sb3("F2_s", [P, DC, D])
        f1b_s = sb3("f1b_s", [P, DC])
        f2b_s = sb3("f2b_s", [P, D])
        gamma_s = sb3("gamma_s", [P, D])
        beta_s = sb3("beta_s", [P, D])

        st12 = ExitStack()

        def sb12(name, shape, dt=F32):
            return st12.enter_context(nc.sbuf_tensor(name, shape, dt))

        T1 = sb12("T1", [P, DC, H], BF16)
        T2 = sb12("T2", [P, HC, D], BF16)
        wscale = sb12("wscale", [P, 2])
        wscale_inv = sb12("wscale_inv", [P, 2])
        wscale_127 = sb12("wscale_127", [P, 2])
        q1T = sb12("q1T", [P, NT // G, DC, G * P], BF16)
        scale1 = sb12("scale1", [P, NT])
        inverse1 = sb12("inverse1", [P, NT])
        tq = sb12("tq", [C, B, D])
        tqT = sb12("tqT", [P, B, DC, C])

        setup = ExitStack()

        def sbs(name, shape, dt=F32):
            return setup.enter_context(nc.sbuf_tensor(name, shape, dt))

        ctx_s = sbs("ctx_s", [C, B, D])
        ctxT = sbs("ctxT", [P, DC, B, C])
        raw = {n: v for n, v in zip(
            ["W", "Wq1", "Wk1", "Wq2", "Wv1", "Wk2", "Wv2", "WT", "Wq1T", "Wk1T", "Wq2T", "Wv1T"],
            [v.rearrange("p (c d) -> p c d", c=DC) for v in carve([DC * D] * 12)])}
        Wb_s = sbs("Wb_s", [P, D])
        K2T = sbs("K2T", [P, DC, B * C])
        A2 = sbs("A2", [P, DC, B * C])
        bias_rows = sbs("bias_rows", [E * HC + DC, P])
        ones = sbs("ones", [P, P])
        w_abs = sbs("w_abs", [P, 2])
        borrowed = EWS[:, EARLY - 1, :]
        w1_s = borrowed[:, 0:2 * HC * D].bitcast(F32).rearrange("p (c d) -> p c d", c=HC)
        t1_s = borrowed[:, 2 * HC * D:3 * HC * D].rearrange("p (c d) -> p c d", c=HC)
        t2_s = borrowed[:, 3 * HC * D:4 * HC * D].rearrange("p (c d) -> p c d", c=DC)
        w2_s = stage_in[:]
        graw = sbs("graw", [P, 4])
        setup.close()

        s1 = ExitStack()

        def sb1(name, shape, dt=F32):
            return s1.enter_context(nc.sbuf_tensor(name, shape, dt))

        h_v, u_v, hT_v, pT_v = carve([GB * G * D, GB * G * D, GB * DC * G * P, GB * G * P])
        h1 = h_v.rearrange("p (g j d) -> p g j d", g=GB, j=G)
        u1 = u_v.rearrange("p (g j d) -> p g j d", g=GB, j=G)
        hT = hT_v.rearrange("p (g c n) -> p g c n", g=GB, c=DC)
        probsT = pT_v[0:C, :].rearrange("p (g n) -> p g n", g=GB)
        shifted = sb1("shifted", [P, GB, G, C])
        probs = sb1("probs", [P, GB, G, C])
        q1 = sb1("q1", [P, GB, G, D], BF16)
        top = sb1("top", [P, GB, G])
        total = sb1("total", [P, GB, G])
        ln1_g_s = sb1("ln1_g_s", [P, D])
        ln1_b_s = sb1("ln1_b_s", [P, D])
        b2_s = sb1("b2_s", [P, D])
        sx1 = sb1("sx1", [P, GB, G])
        s1.close()

        y2_v, v2_v, g2_v, bb2_v, b1_v = carve([2 * H, 2 * H, H, H, H])
        y2 = y2_v.rearrange("p (u h) -> p u h", u=2)
        v2 = v2_v.rearrange("p (u h) -> p u h", u=2)
        ln2_g_s, ln2_b_s, b1_s = g2_v, bb2_v, b1_v
        s2 = ExitStack()

        def sb2(name, shape, dt=F32):
            return s2.enter_context(nc.sbuf_tensor(name, shape, dt))

        q2 = sb2("q2", [P, 2, H], BF16)
        q2T = sb2("q2T", [P, 2, HC, P], BF16)
        diag = sb2("diag", [P, 2, P])
        act_scale = sb2("act_scale", [P, 2])
        ysum = sb2("ysum", [P, 2])
        ysq = sb2("ysq", [P, 2])
        neg_mean = sb2("neg_mean", [P, 2])
        rstd2 = sb2("rstd2", [P, 2])
        vmax = sb2("vmax", [P, 2])
        sx2 = sb2("sx2", [P, 2])
        outscale = sb2("outscale", [P, 2])
        square_out = sb2("square_out", [P, 2, H], BF16)
        s2.close()
        st12.close()

        nT_v, QmT_v, n_v, P_v, PT_v = carve([DC * S, DC * S, TB * D, S, S])
        nT = nT_v.rearrange("p (c s) -> p c s", c=DC)
        QmT = QmT_v.rearrange("p (c s) -> p c s", c=DC)
        n3 = n_v.rearrange("p (t d) -> p t d", t=TB)
        Pr, PT = P_v, PT_v
        s3 = ExitStack()

        def sb3o(name, shape, dt=F32):
            return s3.enter_context(nc.sbuf_tensor(name, shape, dt))

        VP = sb3o("VP", [P, TB, DV])
        acc = sb3o("acc", [P, GB, G, D])
        s2raw = sb3o("s2raw", [P, GB, G, C])
        negmax = sb3o("negmax", [P, TB])
        rowsum = sb3o("rowsum", [P, TB])
        rowinv = sb3o("rowinv", [P, TB])
        top3 = sb3o("top3", [P, G])
        total3 = sb3o("total3", [P, G])
        p2T = sb3o("p2T", [C, G * P])
        s3.close()
        n2T = QmT_v[:, 0:DC * G * P].rearrange("p (c s) -> p c s", c=DC)
        f_pre = QmT_v[:, DC * G * P:2 * DC * G * P].rearrange("p (c s) -> p c s", c=DC)
        f_hT = P_v[:, 0:DC * G * P].rearrange("p (c s) -> p c s", c=DC)
        split3 = PT_v.bitcast(BF16).rearrange("p (j n) -> p j n", j=G)
        early3.close()

        s5 = ExitStack()

        def sb5(name, shape, dt=F32):
            return s5.enter_context(nc.sbuf_tensor(name, shape, dt))

        NTK = NT * K
        weight = sb5("weight", [P, NT, K])
        src_row = sb5("src_row", [P, TILES], I32)
        dst_row = sb5("dst_row", [P, TILES], I32)
        tile_expert = sb5("tile_expert", [P, TILES], I32)
        s4 = ExitStack()

        def sb4(name, shape, dt=F32):
            return s4.enter_context(nc.sbuf_tensor(name, shape, dt))

        pe_exp = sb4("pe_exp", [P, NT, E])
        gsum = sb4("gsum", [P, NT])
        gtop = sb4("gtop", [P, NT, 8])
        gidx = sb4("gidx", [P, NT, 8], U32)
        gidx_f = sb4("gidx_f", [P, NT, K])
        onehot = sb4("onehot", [P, NT, K, E])
        count = sb4("count", [P, NT, E])
        tiles_upto = sb4("tiles_upto", [P, 2, NT, E])
        denom = sb4("denom", [P, NT])
        combine = sb4("combine", [P, NT, E])
        combineT = sb4("combineT", [E, NT, P])
        strictly_lower = sb4("strictly_lower", [P, P])
        ones5 = sb4("ones5", [P, P])
        iota_e = sb4("iota_e", [P, E])
        iota_p = sb4("iota_p", [P, P])
        iota_j = sb4("iota_j", [P, TILES])
        token_code = sb4("token_code", [P, NT, K])
        etiles = sb4("etiles", [P, E])
        eend = sb4("eend", [P, 2, E])
        prefix = sb4("prefix", [P, NT, E])
        place = sb4("place", [P, NT, K])
        picked = sb4("picked", [P, NT, K, E])
        place_hi = sb4("place_hi", [P, NT, K])
        place_lo = sb4("place_lo", [P, NT, K])
        hot_lo = sb4("hot_lo", [P, 2, 8, P])
        hot_hi = sb4("hot_hi", [P, NTK, TILES])
        code = sb4("code", [P, TILES])
        pad_row = sb4("pad_row", [P, 1])
        src_f = sb4("src_f", [P, TILES])
        dst_f = sb4("dst_f", [P, TILES])
        ended = sb4("ended", [P, TILES, E])
        tile_expert_f = sb4("tile_expert_f", [P, TILES])
        s4.close()
        src_now = sb5("src_now", [P, U], I32)
        dst_now = sb5("dst_now", [P, U], I32)
        rows_in = sb5("rows_in", [P, U, 2 * D], BF16)
        xT = sb5("xT", [P, U, 2, DC, P], BF16)
        hid = sb5("hid", [P, 2, HC * P])
        hid16 = sb5("hid16", [P, 2, 2, HC, P], BF16)
        rows_out = sb5("rows_out", [P, U, D])
        s5.close()
        both = EWS[:, 0, :].bitcast(F32).rearrange("p (g j k d) -> p g j k d", g=2, j=G, k=K)

        stage_done, waited_alone = sem("stage_done"), sem("waited_alone")
        in_x, in_w = sem("in_x"), sem("in_w")
        in_vec, in_vec2, in_late = sem("in_vec"), sem("in_vec2"), sem("in_late")
        block_in = [sem("block_in0"), sem("block_in1")]
        block_high, block_split = sem("block_high"), sem("block_split")
        const_made, ident_made = sem("const_made"), sem("ident_made")
        gates_made = sem("gates_made")
        su_psum, su_copied, su_tern, su_abs = sem("su_psum"), sem("su_copied"), sem("su_tern"), sem("su_abs")
        a_moments, a_rstd, a_h, a_hT_psum, a_hT = (sem(n) for n in (
            "a_moments", "a_rstd", "a_h", "a_hT_psum", "a_hT"))
        a_scores, a_shifted, a_probs, a_pT_psum, a_pT, a_vec = (sem(n) for n in (
            "a_scores", "a_shifted", "a_probs", "a_pT_psum", "a_pT", "a_vec"))
        a_q, a_qT_psum, a_qT = sem("a_q"), sem("a_qT_psum"), sem("a_qT")
        f_diag, f_hidden, f_gelu, f_mean, f_sq, f_rstd = (sem(n) for n in (
            "f_diag", "f_hidden", "f_gelu", "f_mean", "f_sq", "f_rstd"))
        f_scaled, f_q, f_qT_psum, f_qT, f_y = (sem(n) for n in (
            "f_scaled", "f_q", "f_qT_psum", "f_qT", "f_y"))
        c_moments, c_rstd, c_n, c_nT_psum, c_nT = (sem(n) for n in (
            "c_moments", "c_rstd", "c_n", "c_nT_psum", "c_nT"))
        c_qm_psum, c_qm, c_vp_psum, c_vp = (sem(n) for n in ("c_qm_psum", "c_qm", "c_vp_psum", "c_vp"))
        c_scores, c_max, c_exp, c_pT_psum, c_pT, c_att, c_acc = (sem(n) for n in (
            "c_scores", "c_max", "c_exp", "c_pT_psum", "c_pT", "c_att", "c_acc"))
        d_shift, d_exp, d_pT_psum, d_pT, d_att, d_norm2, d_nT_psum, d_nT = (sem(n) for n in (
            "d_shift", "d_exp", "d_pT_psum", "d_pT", "d_att", "d_norm2", "d_nT_psum", "d_nT"))
        d_f1_psum, d_f1, d_hT, d_ff, d_n4, d_n4T_psum, d_n4T, d_logits, d_stored, d_logits_in = (
            sem(n) for n in ("d_f1_psum", "d_f1", "d_hT", "d_ff", "d_n4", "d_n4T_psum", "d_n4T",
                             "d_logits", "d_stored", "d_logits_in"))
        r_const, r_exp, r_count, r_prefix, r_hot, r_hot_used, r_code, r_rows, r_expert = (
            sem(n) for n in ("r_const", "r_exp", "r_count", "r_prefix", "r_hot", "r_hot_used",
                             "r_code", "r_rows", "r_expert"))
        r_shift, r_combine, r_cT_psum, r_cT, r_b2, r_b2_in = (sem(n) for n in (
            "r_shift", "r_combine", "r_cT_psum", "r_cT", "r_b2", "r_b2_in"))
        m_rows = [sem(f"m_rows{u}") for u in range(U)]
        m_out = [sem(f"m_out{u}") for u in range(U)]
        m_src = sem("m_src")
        m_xT_psum, m_xT, m_hid_psum, m_hid, m_hid16, m_y_psum, m_y = (sem(n) for n in (
            "m_xT_psum", "m_xT", "m_hid_psum", "m_hid", "m_hid16", "m_y_psum", "m_y"))
        z_in = [sem("z_in0"), sem("z_in1")]
        z_sum, z_out = sem("z_sum"), sem("z_out")

        def wait_alone(eng, s, n):
            eng.wait_ge(s, n)
            eng.sem_inc(waited_alone, 1)

        def stage_end(eng, n):
            eng.drain().then_inc(stage_done, 1)
            wait_alone(eng, stage_done, 5 * n)

        END_SETUP, END_1, END_2, END_3, END_4, END_5 = 1, 1 + B, 2 + B, 2 + 2 * B, 3 + 2 * B, 4 + 2 * B

        def cols(ap, n):
            return ap.unsqueeze(len(ap.shape)).to_broadcast(list(ap.shape) + [n])

        def rows4(ap):
            return ap.unsqueeze(1).to_broadcast([P, G, ap.shape[-1]])

        block = stack.enter_context(nc.Block())

        SPLIT_2, SPLIT_3 = NT, EARLY * EBLK - NT

        @block.sync
        def _(sp):
            def vec(dst, src, s=in_vec):
                sp.dma_start(dst, src.partition_broadcast(P)).then_inc(s, 16)

            def mat(dst, src):
                sp.dma_start(dst, src.rearrange("(c p) n -> p c n", p=P)).then_inc(in_w, 16)

            sp.dma_start(ctx_s[:], ctx_in.rearrange("b c d -> c b d")).then_inc(in_w, 16)
            for name, src in (("W", W), ("Wq1", Wq1), ("Wk1", Wk1), ("Wq2", Wq2), ("Wv1", Wv1),
                              ("Wk2", Wk2), ("Wv2", Wv2)):
                mat(raw[name], src)
            sp.dma_start(bias_rows[0:E * HC, :], e1b.rearrange("e (m p) -> (e m) p", p=P)).then_inc(in_w, 16)
            sp.dma_start(bias_rows[E * HC:E * HC + DC, :], f1b.rearrange("(c p) -> c p", p=P)).then_inc(in_w, 16)
            vec(Wb_s[:], Wb)
            vec(graw[:, 0:2], g_xattn)
            vec(graw[:, 2:4], g_ffn)
            sp.dma_start(w1_s, w1.rearrange("(c p) n -> p c n", p=P)).then_inc(in_x, 16)
            sp.dma_start(w2_s, w2.rearrange("(c p) n -> p c n", p=P)).then_inc(in_x, 16)
            sp.dma_start(res[:], x_tiles).then_inc(in_x, 16)
            for dst, src in ((F1_s, F1), (F2_s, F2), (Wg_s, Wg)):
                sp.dma_start(dst[:], src.rearrange("(c p) n -> p c n", p=P)).then_inc(in_late, 16)
            sp.dma_start(e2b_s[:], e2b).then_inc(in_late, 16)
            for dst, src in ((f2b_s, f2b), (gamma_s, gamma), (beta_s, beta), (bg_s, bg)):
                vec(dst[:], src, in_late)
            stage_end(sp, END_SETUP)
            vec(ln1_g_s[:], ln1_g, in_vec)
            vec(ln1_b_s[:], ln1_b, in_vec)
            vec(b2_s[:], b2, in_vec)
            with sp.Fori(0, B) as b:
                stage_end(sp, END_SETUP + 1 + b)
            vec(ln2_g_s, ln2_g, in_vec2)
            vec(ln2_b_s, ln2_b, in_vec2)
            vec(b1_s, b1, in_vec2)

            def load_block(e, k):
                s = k % 2
                if k < EBLK // 2:
                    sp.dma_start(stage_in[:, s, :], E1[e, k * P:(k + 1) * P, :]).then_inc(block_in[s], 16)
                else:
                    f0 = (k - EBLK // 2) * (HC // 2) * P
                    sp.dma_start(stage_in[:, s, :].rearrange("p (m d) -> p m d", m=HC // 2),
                                 E2[e, f0:f0 + HC // 2 * P, :].rearrange("(m p) d -> p m d", p=P)
                                 ).then_inc(block_in[s], 16)

            load_block(0, 0)
            load_block(0, 1)
            for k in range(2, EBLK):
                sp.wait_ge(block_split, k - 1)
                load_block(0, k)
            with sp.Fori(1, NT // EBLK) as e:
                for k in range(EBLK):
                    wait_alone(sp, block_split, EBLK * e + k - 1)
                    load_block(e, k)
            stage_end(sp, END_2)
            with sp.Fori(0, B) as b:
                for k in range(EBLK):
                    e = b + NT // EBLK
                    wait_alone(sp, block_split, EBLK * e + k - 1)
                    load_block(e, k)
                for g in range(GB):
                    wait_alone(sp, d_n4, GB * b + g + 1)
                    sp.dma_start(split_rows[bass.ds((TB * b + G * g) * P, G * P), :].rearrange(
                        "(j p) n -> p j n", p=P), split3[:]).then_inc(d_stored, 16)
                wait_alone(sp, d_stored, 16 * GB * (b + 1))
                stage_end(sp, END_2 + 1 + b)
            with sp.Fori(EARLY, E) as e:
                for k in range(EBLK):
                    wait_alone(sp, block_split, EBLK * e + k - 1)
                    load_block(e, k)
            stage_end(sp, END_4)
            stage_end(sp, END_5)
            for g in range(2):
                sp.dma_start(both[:, g, :, :, :].rearrange("p j k d -> p j (k d)"),
                             choice_rows[g * G * P * K:(g + 1) * G * P * K, :].rearrange(
                                 "(j p k) d -> p j (k d)", p=P, k=K)).then_inc(z_in[g], 16)
            for g in range(2, NT // G):
                sp.wait_ge(z_sum, g - 1)
                sp.dma_start(both[:, g % 2, :, :, :].rearrange("p j k d -> p j (k d)"),
                             choice_rows[g * G * P * K:(g + 1) * G * P * K, :].rearrange(
                                 "(j p k) d -> p j (k d)", p=P, k=K)).then_inc(z_in[g % 2], 16)
            for g in range(NT // G):
                sp.wait_ge(z_sum, g + 1)
                sp.dma_start(out_tiles[:, g * G:(g + 1) * G, :], res[:, g * G:(g + 1) * G, :]).then_inc(z_out, 16)
            sp.wait_ge(z_out, 16 * (NT // G))

        @block.gpsimd
        def _(pool):
            pool.memset(ident[:], 0.0)
            pool.memset(ident16[:], 0.0)
            pool.memset(causal[:], 0.0)
            pool.memset(minus_half[:], -0.5)
            pool.memset(zero_col[:], 0.0)
            pool.memset(ones[:], 1.0)
            pool.drain()
            pool.affine_select(out=ident[:], in_=ident[:], compare_op=ALU.not_equal, fill=1.0,
                               base=0, pattern=[[-1, P]], channel_multiplier=1)
            pool.affine_select(out=ident16[:], in_=ident16[:], compare_op=ALU.not_equal, fill=1.0,
                               base=0, pattern=[[-1, P]], channel_multiplier=1)
            pool.affine_select(out=causal[:], in_=causal[:], compare_op=ALU.is_ge, fill=MASKED,
                               base=0, pattern=[[-1, P]], channel_multiplier=1)
            pool.drain().then_inc(const_made, 1)

            def rsqrt(dst, var, a, c, half, done):
                pool.tensor_scalar(dst, var, a, c, ALU.mult, ALU.add)
                pool.drain()
                pool.tensor_tensor(dst, dst, half, ALU.pow).then_inc(done, 1)

            def split_block(e, k):
                hi, lo = block_parts(e, k)
                pool.wait_ge(block_high, EBLK * e + k + 1)
                pool.tensor_tensor(lo, stage_in[:, k % 2, :], hi, ALU.subtract).then_inc(block_split, 1)

            stage_end(pool, END_SETUP)
            with pool.Fori(0, B) as b:
                for k in range(2 * GB):
                    wait_alone(pool, a_moments, 2 * GB * b + k + 1)
                    if k < GB:
                        rsqrt(rstd[:, k % 2, :], moments[:, k % 2, :, 1], 1.0, LN_EPS, minus_half[:], a_rstd)
                    else:
                        rsqrt(rstd[:, k % 2, :], moments[:, k % 2, :, 1], 1.0 + LN_EPS, LN_EPS ** 2,
                              minus_half[:], a_rstd)
                stage_end(pool, END_SETUP + 1 + b)

            def hidden_rstd(t, u):
                wait_alone(pool, f_sq, t + 1)
                rsqrt(rstd2[:, u:u + 1], ysq[:, u:u + 1], 1.0 / H, LN_EPS, minus_half[:, 0:1], f_rstd)

            def stage2_tile(t, u, following, e, k):
                wait_alone(pool, f_scaled, t + 1)
                pool.tensor_scalar(q2[:, u, :], v2[:, u, :], -MAGIC, 1.0, ALU.add, ALU.mult).then_inc(f_q, 1)
                if following:
                    hidden_rstd(t + 2, u)
                split_block(e, k)

            hidden_rstd(0, 0)
            hidden_rstd(1, 1)
            with pool.Fori(0, NT // EBLK - 1) as e:
                for k in range(EBLK):
                    stage2_tile(EBLK * e + k, k % 2, True, e, k)
            for k in range(EBLK):
                t = NT - EBLK + k
                stage2_tile(t, k % 2, t + 2 < NT, NT // EBLK - 1, k)
            stage_end(pool, END_2)
            with pool.Fori(0, B) as b:
                def c_rsqrt(n, eps):
                    wait_alone(pool, c_moments, 10 * b + n + 1)
                    rsqrt(rstd[:, n % 2, :], moments[:, n % 2, :, 1], 1.0, eps, minus_half[:], c_rstd)
                c_rsqrt(0, LN_EPS)
                c_rsqrt(1, LN_EPS)
                for k in range(EBLK):
                    split_block(b + NT // EBLK, k)
                for g in range(GB):
                    for k in range(3):
                        c_rsqrt(2 + 4 * g + k, L1_EPS)
                    c_rsqrt(2 + 4 * g + 3, LN_EPS)
                stage_end(pool, END_2 + 1 + b)

            pool.memset(strictly_lower[:], 1.0)
            pool.memset(ones5[:], 1.0)
            pool.iota(iota_e[:], pattern=[[1, E]], base=0, channel_multiplier=0,
                      allow_small_or_imprecise_dtypes=True)
            pool.iota(iota_p[:], pattern=[[1, P]], base=0, channel_multiplier=0,
                      allow_small_or_imprecise_dtypes=True)
            pool.iota(iota_j[:], pattern=[[1, TILES]], base=0, channel_multiplier=0,
                      allow_small_or_imprecise_dtypes=True)
            pool.iota(token_code[:], pattern=[[K * P, NT], [1, K]], base=1, channel_multiplier=K,
                      allow_small_or_imprecise_dtypes=True)
            pool.iota(pad_row[:], pattern=[[0, 1]], base=SLOTS + 1, channel_multiplier=1,
                      allow_small_or_imprecise_dtypes=True)
            pool.drain()
            pool.affine_select(out=strictly_lower[:], in_=strictly_lower[:], compare_op=ALU.is_gt, fill=0.0,
                               base=0, pattern=[[1, P]], channel_multiplier=-1)
            pool.drain().then_inc(r_const, 1)
            with pool.Fori(EARLY, E) as e:
                for k in range(EBLK):
                    split_block(e, k)
            stage_end(pool, END_4)

            def gather(j, u):
                wait_alone(pool, m_src, j + 1)
                pool.indirect_dma_start(
                    out=rows_in[:, u, :], out_offset=None, in_=split_rows,
                    in_offset=bass.IndirectOffsetOnAxis(ap=src_now[:, u:u + 1], axis=0)).then_inc(m_rows[u], 16)

            def scatter(j, u, turn):
                wait_alone(pool, m_y, j + 1)
                wait_alone(pool, m_out[u - 1], 16 * (turn + 1 if u else turn))
                pool.indirect_dma_start(
                    out=choice_rows, out_offset=bass.IndirectOffsetOnAxis(ap=dst_now[:, u:u + 1], axis=0),
                    in_=rows_out[:, u, :], in_offset=None).then_inc(m_out[u], 16)

            for u in range(U):
                gather(u, u)
            with pool.Fori(0, TILES // U - 1) as i:
                for u in range(U):
                    gather(U * (i + 1) + u, u)
                    scatter(U * i + u, u, i)
            for u in range(U):
                scatter(TILES - U + u, u, TILES // U - 1)
            for u in range(U):
                pool.wait_ge(m_out[u], 16 * (TILES // U))
            stage_end(pool, END_5)

        @block.scalar
        def _(act):
            def high_block(e, k):
                act.wait_ge(block_in[k % 2], 16 * ((EBLK // 2) * e + k // 2 + 1))
                act.activation(block_parts(e, k)[0], stage_in[:, k % 2, :], ACT.Copy).then_inc(block_high, 1)

            act.wait_ge(in_vec, 48)
            act.activation(gates[:], graw[:], ACT.Tanh).then_inc(gates_made, 1)
            stage_end(act, END_SETUP)
            with act.Fori(0, B) as b:
                for g in range(GB):
                    act.wait_ge(a_hT_psum, GB * b + g + 1)
                    for c in range(DC):
                        last = act.activation(hT[:, g, c, :], bank(DC * g + c), ACT.Copy)
                    last.then_inc(a_hT, 1)
                for g in range(GB):
                    act.wait_ge(a_shifted, GB * b + g + 1)
                    act.activation(probs[:, g, :, :], shifted[:, g, :, :], ACT.Exp).then_inc(a_probs, 1)
                for g in range(GB):
                    act.wait_ge(a_pT_psum, GB * b + g + 1)
                    act.activation(probsT[:, g, :], ps[0:C, 6 + g, :], ACT.Copy).then_inc(a_pT, 1)
                for g in range(GB):
                    act.wait_ge(a_qT_psum, GB * b + g + 1)
                    act.activation(q1T[:, bass.ds(GB * b + g, 1), :, :].rearrange("p o c n -> p (o c n)"),
                                   bank16(4 + g), ACT.Copy).then_inc(a_qT, 1)
                stage_end(act, END_SETUP + 1 + b)

            def gelu(t, u):
                act.wait_ge(f_hidden, t + 1)
                act.activation(y2[:, u, :], ps[:, 2 * u:2 * u + 2, :].rearrange("p a n -> p (a n)"),
                               ACT.Gelu, scale=act_scale[:, u:u + 1],
                               accum_out=ysum[:, u:u + 1]).then_inc(f_gelu, 1)

            def square(t, u):
                act.wait_ge(f_mean, t + 1)
                act.activation(square_out[:, u, :], y2[:, u, :], ACT.Square, bias=neg_mean[:, u:u + 1],
                               accum_out=ysq[:, u:u + 1]).then_inc(f_sq, 1)

            def stage2_tile(t, u, ahead, e, k):
                if ahead >= 2:
                    square(t + 2, u)
                act.wait_ge(f_qT_psum, t + 1)
                act.activation(q2T[:, u, :, :].rearrange("p m n -> p (m n)"), bank16(4 + u),
                               ACT.Copy).then_inc(f_qT, 1)
                high_block(e, k)
                if ahead >= 3:
                    gelu(t + 3, 1 - u)

            gelu(0, 0)
            gelu(1, 1)
            square(0, 0)
            square(1, 1)
            act.drain()
            gelu(2, 0)
            with act.Fori(0, NT // EBLK - 1) as e:
                for k in range(EBLK):
                    stage2_tile(EBLK * e + k, k % 2, 3, e, k)
            for k in range(EBLK):
                t = NT - EBLK + k
                stage2_tile(t, k % 2, NT - 1 - t, NT // EBLK - 1, k)
            stage_end(act, END_2)

            with act.Fori(0, B) as b:
                for g in range(GB):
                    act.wait_ge(c_nT_psum, GB * b + g + 1)
                    for c in range(DC):
                        last = act.activation(nT[:, c, g * 512:(g + 1) * 512], bank(DC * g + c), ACT.Copy)
                    last.then_inc(c_nT, 1)
                for k in range(2 * GB):
                    o, g = k % DC, k // DC
                    act.wait_ge(c_qm_psum, 2 * GB * b + k + 1)
                    act.activation(QmT[:, o, g * 512:(g + 1) * 512], bank(4 + k), ACT.Copy,
                                   scale=float(S) ** -0.5).then_inc(c_qm, 1)
                for i in range(TB):
                    L = (i + 1) * P
                    if i % 2:
                        high_block(b + NT // EBLK, i // 2)
                    act.wait_ge(c_max, TB * b + i + 1)
                    if i:
                        act.wait_ge(c_pT_psum, TB * b + i)
                    act.activation(Pr[:, 0:L], ps[:, 2 * (i % 2):2 * (i % 2) + 2, :].rearrange(
                        "p a n -> p (a n)")[:, 0:L], ACT.Exp, bias=negmax[:, i:i + 1],
                        accum_out=rowsum[:, i:i + 1]).then_inc(c_exp, 1)
                    act.wait_ge(c_pT_psum, TB * b + i + 1)
                    act.activation(PT[:, 0:L], ps[:, 4:6, :].rearrange("p a n -> p (a n)")[:, 0:L],
                                   ACT.Copy).then_inc(c_pT, 1)
                for g in range(GB):
                    act.wait_ge(d_shift, GB * b + g + 1)
                    act.activation(s2raw[:, g, :, :], s2raw[:, g, :, :], ACT.Exp).then_inc(d_exp, 1)
                    act.wait_ge(d_pT_psum, GB * b + g + 1)
                    act.activation(p2T[:], ps[0:C, 0, :], ACT.Copy).then_inc(d_pT, 1)
                    act.wait_ge(d_nT_psum, GB * b + g + 1)
                    for c in range(DC):
                        last = act.activation(n2T[:, c, :], bank(c), ACT.Copy)
                    last.then_inc(d_nT, 1)
                    act.wait_ge(d_f1_psum, GB * b + g + 1)
                    for c in range(DC):
                        last = act.activation(f_pre[:, c, :], bank(2 + c), ACT.Identity,
                                              bias=f1b_s[:, c:c + 1])
                    last.then_inc(d_f1, 1)
                    act.wait_ge(d_n4T_psum, GB * b + g + 1)
                    for c in range(DC):
                        last = act.activation(n2T[:, c, :], bank(c), ACT.Copy)
                    last.then_inc(d_n4T, 1)
                stage_end(act, END_2 + 1 + b)

            act.wait_ge(r_shift, 1)
            act.activation(pe_exp[:], pe_exp[:], ACT.Exp).then_inc(r_exp, 1)
            with act.Fori(EARLY, E) as e:
                for k in range(EBLK):
                    high_block(e, k)
            stage_end(act, END_4)

            def hidden(j, v, e):
                act.wait_ge(m_hid_psum, j + 1)
                for m in range(HC):
                    last = act.activation(hid[:, v, m * P:(m + 1) * P],
                                          bank(2 + 2 * v + m // 4)[:, (m % 4) * P:(m % 4 + 1) * P],
                                          ACT.Gelu_apprx_tanh, bias=expert_b1[:, bass.ds(e * HC + m, 1)])
                last.then_inc(m_hid, 1)

            def expert_of(j):
                return act.value_load(tile_expert[0:1, bass.ds(j, 1)], min_val=0, max_val=E - 1)

            act.wait_ge(r_expert, 1)
            with act.Fori(0, TILES // TURN) as i:
                for q in range(TURN):
                    hidden(TURN * i + q, q % 2, expert_of(TURN * i + q))
            for j in range(TILES // TURN * TURN, TILES):
                hidden(j, j % 2, expert_of(j))
            stage_end(act, END_5)

        @block.vector
        def _(dve):
            def copied(n=1):
                dve.drain().then_inc(su_copied, n)

            def step(n):
                dve.wait_ge(su_psum, n)

            dve.wait_ge(in_x, 48)
            dve.tensor_reduce(w_abs[:, 0:1], w1_s.rearrange("p a b -> p (a b)"), X, ALU.add,
                              apply_absolute_value=True)
            dve.tensor_reduce(w_abs[:, 1:2], w2_s.rearrange("p a b -> p (a b)"), X, ALU.add,
                              apply_absolute_value=True)
            dve.drain().then_inc(su_abs, 1)
            step(1)
            dve.tensor_copy(ctxT[:].rearrange("p c b k -> p (c b k)"), bank(0)[:, 0:DC * B * C])
            for n, name in enumerate(("WT", "Wq1T", "Wk1T", "Wq2T", "Wv1T")):
                step(2 + n)
                dve.tensor_copy(raw[name].rearrange("p c d -> p (c d)"), bank(1 + n))
            step(7)
            dve.tensor_copy(expert_b1[:], bank(6)[:, 0:E * HC])
            dve.tensor_copy(f1b_s[:], bank(6)[:, E * HC:E * HC + DC])
            copied()
            step(8)
            dve.wait_ge(in_vec, 48)
            dve.tensor_tensor(tq[:], ps[0:C, 0, :].rearrange("p (b d) -> p b d", b=B),
                              Wb_s[0:C, :].unsqueeze(1).to_broadcast([C, B, D]), ALU.add)
            step(9)
            dve.tensor_copy(M1[:].rearrange("p c d -> p (c d)"), bank(1))
            step(10)
            dve.tensor_copy(K2T[:].rearrange("p c d -> p (c d)"), bank(2)[:, 0:DC * B * C])
            step(11)
            dve.tensor_copy(V2[:].rearrange("p c d -> p (c d)"), ps[0:C, 3, :])
            copied()
            step(12)
            dve.tensor_copy(tqT[:].rearrange("p b c k -> p (b c k)"), bank(4)[:, 0:DC * B * C])
            step(13)
            dve.tensor_scalar(A2[:].rearrange("p c d -> p (c d)"), bank(5)[:, 0:DC * B * C],
                              float(C) ** -0.5, None, ALU.mult)
            copied()
            step(14)
            for b in range(B):
                dve.tensor_copy(WVA[:, b, :, D:DV],
                                bank(6)[:, 0:DC * B * C].rearrange("p (c b k) -> p c b k", c=DC, b=B)[:, :, b, :])
                dve.tensor_copy(WVA[:, b, :, 0:D], raw["Wv1"])
            step(15)
            dve.tensor_scalar(wscale[:], bank(7)[:, 0:2], 1.0 / (H * D), 1e-5, ALU.mult, ALU.max)
            dve.drain()
            dve.reciprocal(wscale_inv[:], wscale[:])
            dve.tensor_scalar(wscale_127[:], wscale[:], 1.0 / 127.0, None, ALU.mult)
            dve.drain()
            for n, (w_s, t_s) in enumerate(((w1_s, t1_s), (w2_s, t2_s))):
                flat = w_s.rearrange("p a b -> p (a b)")
                dve.tensor_scalar(flat, flat, wscale_inv[:, n:n + 1], MAGIC, ALU.mult, ALU.add)
                dve.drain()
                dve.tensor_scalar(flat, flat, -MAGIC, 1.0, ALU.add, ALU.min)
                dve.drain()
                dve.tensor_scalar(t_s.rearrange("p a b -> p (a b)"), flat, -1.0, None, ALU.max)
                dve.drain().then_inc(su_tern, 1)
            for n in range(DC):
                step(16 + n)
                dve.tensor_copy(T1[:, n, :], bank16(n))
            for n in range(2):
                step(18 + n)
                dve.tensor_copy(T2[:, 4 * n:4 * n + 4, :].rearrange("p m d -> p (m d)"), bank16(2 + n))
            dve.wait_ge(gates_made, 1)
            stage_end(dve, END_SETUP)

            def group_moments(tile_of, k, done):
                for j in range(G):
                    dve.bn_stats(stats[:, j, :], tile_of(j))
                dve.drain()
                for j in range(G):
                    dve.bn_aggr(moments[:, k, j, :], stats[:, j, :])
                dve.drain().then_inc(done, 1)

            def normalise(out_of, tile_of, k):
                for j in range(G):
                    dve.tensor_scalar(out_of(j), tile_of(j), moments[:, k, j, 0:1], rstd[:, k, j:j + 1],
                                      ALU.subtract, ALU.mult)
                dve.drain()

            dve.wait_ge(in_vec, 96)
            with dve.Fori(0, B) as b:
                def res_tile(g):
                    return lambda j: res[:, bass.ds(TB * b + G * g + j, 1), :].rearrange("p o d -> p (o d)")

                def res_group(g):
                    return res[:, bass.ds(TB * b + G * g, G), :]

                for g in range(GB):
                    group_moments(res_tile(g), g, a_moments)
                for g in range(GB):
                    dve.wait_ge(a_rstd, 2 * GB * b + g + 1)
                    normalise(lambda j: h1[:, g, j, :], res_tile(g), g)
                    dve.drain().then_inc(a_h, 1)
                for g in range(GB):
                    dve.wait_ge(a_scores, GB * b + g + 1)
                    sc = bank(4 + g)[:, 0:G * C].rearrange("p (j k) -> p j k", j=G)
                    dve.tensor_reduce(top[:, g, :], sc, X, ALU.max)
                    dve.drain()
                    dve.tensor_tensor(shifted[:, g, :, :], sc, cols(top[:, g, :], C), ALU.subtract
                                      ).then_inc(a_shifted, 1)
                for g in range(GB):
                    dve.wait_ge(a_probs, GB * b + g + 1)
                    dve.tensor_reduce(total[:, g, :], probs[:, g, :, :], X, ALU.add)
                    dve.drain()
                    dve.reciprocal(total[:, g, :], total[:, g, :])
                    dve.drain()
                    dve.wait_ge(a_vec, GB * b + g + 1)
                    for j in range(G):
                        dve.tensor_scalar(h1[:, g, j, :], bank(2 * g + j // 2)[:, (j % 2) * D:(j % 2 + 1) * D],
                                          total[:, g, j:j + 1], 0.0, ALU.mult, ALU.max)
                    dve.drain()
                    dve.scalar_tensor_tensor(res_group(g), h1[:, g, :, :], gates[:, 0:1], res_group(g),
                                             ALU.mult, ALU.add)
                    dve.drain()
                    group_moments(res_tile(g), g, a_moments)
                for g in range(GB):
                    dve.wait_ge(a_rstd, 2 * GB * b + GB + g + 1)
                    normalise(lambda j: u1[:, g, j, :], res_tile(g), g)
                    u = u1[:, g, :, :]
                    dve.tensor_tensor(u, u, rows4(ln1_g_s[:]), ALU.mult)
                    dve.scalar_tensor_tensor(res_group(g), rows4(b2_s[:]), gates[:, 2:3], res_group(g),
                                             ALU.mult, ALU.add)
                    dve.drain()
                    dve.tensor_tensor(u, u, rows4(ln1_b_s[:]), ALU.add)
                    dve.drain()
                    dve.tensor_reduce(top[:, g, :], u, X, ALU.max, apply_absolute_value=True)
                    dve.drain()
                    dve.tensor_scalar(top[:, g, :], top[:, g, :], 1e-5, None, ALU.max)
                    dve.drain()
                    dve.reciprocal(sx1[:, g, :], top[:, g, :])
                    dve.drain()
                    dve.tensor_scalar(sx1[:, g, :], sx1[:, g, :], 127.0, None, ALU.mult)
                    dve.tensor_scalar(scale1[:, bass.ds(TB * b + G * g, G)], top[:, g, :],
                                      wscale_127[:, 0:1], None, ALU.mult)
                    dve.drain()
                    dve.tensor_scalar(inverse1[:, bass.ds(TB * b + G * g, G)], sx1[:, g, :],
                                      wscale_inv[:, 0:1], None, ALU.mult)
                    for j in range(G):
                        dve.tensor_scalar(u1[:, g, j, :], u1[:, g, j, :], sx1[:, g, j:j + 1], MAGIC,
                                          ALU.mult, ALU.add)
                    dve.drain()
                    dve.tensor_scalar(q1[:, g, :, :], u, -MAGIC, None, ALU.add).then_inc(a_q, 1)
                stage_end(dve, END_SETUP + 1 + b)

            dve.wait_ge(in_vec2, 48)

            def make_diag(t, u):
                dve.tensor_scalar(diag[:, u, :], ident[:], inverse1[:, bass.ds(t, 1)], None, ALU.mult)
                dve.tensor_copy(act_scale[:, u:u + 1], scale1[:, bass.ds(t, 1)])
                dve.drain().then_inc(f_diag, 1)

            def finish(t, u):
                dve.wait_ge(f_y, t + 1)
                r = res[:, bass.ds(t, 1), :].rearrange("p o d -> p (o d)")
                dve.scalar_tensor_tensor(r, bank(6 + u)[:, 0:D], outscale[:, u:u + 1], r, ALU.mult, ALU.add)

            def start_row(t, u, ahead):
                dve.wait_ge(f_gelu, t + 1)
                dve.tensor_scalar(neg_mean[:, u:u + 1], ysum[:, u:u + 1], -1.0 / H, None, ALU.mult
                                  ).then_inc(f_mean, 1)
                if ahead >= 2:
                    make_diag(t + 2, u)

            def centre(t, u, reused):
                if reused:
                    dve.wait_ge(f_q, t - 1)
                dve.scalar_tensor_tensor(v2[:, u, :], y2[:, u, :], neg_mean[:, u:u + 1], ln2_g_s,
                                         ALU.add, ALU.mult)

            def hidden_row(t, u, ahead, reused, before):
                if ahead >= 1:
                    start_row(t + 1, 1 - u, ahead - 1)
                v = v2[:, u, :]
                dve.drain()
                dve.wait_ge(f_rstd, t + 1)
                dve.scalar_tensor_tensor(v, v, rstd2[:, u:u + 1], ln2_b_s, ALU.mult, ALU.add)
                if ahead >= 1:
                    centre(t + 1, 1 - u, reused)
                dve.drain()
                dve.tensor_reduce(vmax[:, u:u + 1], v, X, ALU.max, apply_absolute_value=True)
                dve.drain()
                dve.tensor_scalar(vmax[:, u:u + 1], vmax[:, u:u + 1], 1e-5, 1.0 / 127.0, ALU.max, ALU.mult)
                dve.drain()
                dve.reciprocal(sx2[:, u:u + 1], vmax[:, u:u + 1])
                dve.tensor_scalar(outscale[:, u:u + 1], vmax[:, u:u + 1], wscale[:, 1:2], gates[:, 2:3],
                                  ALU.mult, ALU.mult)
                dve.drain()
                dve.tensor_scalar(v, v, sx2[:, u:u + 1], MAGIC, ALU.mult, ALU.add).then_inc(f_scaled, 1)
                if before:
                    finish(t - 1, 1 - u)

            make_diag(0, 0)
            make_diag(1, 1)
            start_row(0, 0, 2)
            dve.drain()
            centre(0, 0, False)
            dve.drain()
            hidden_row(0, 0, 3, False, False)
            with dve.Fori(0, (NT - G) // 2) as i:
                hidden_row(2 * i + 1, 1, 3, True, True)
                hidden_row(2 * i + 2, 0, 3, True, True)
            for t in range(NT - G + 1, NT):
                hidden_row(t, t % 2, NT - 1 - t, True, True)
            finish(NT - 1, 1)
            stage_end(dve, END_2)

            dve.wait_ge(in_late, 16 * 8)
            with dve.Fori(0, B) as b:
                def res_tile(g):
                    return lambda j: res[:, bass.ds(TB * b + G * g + j, 1), :].rearrange("p o d -> p (o d)")

                def res_group(g):
                    return res[:, bass.ds(TB * b + G * g, G), :]

                for g in range(GB):
                    group_moments(res_tile(g), g, c_moments)
                for g in range(GB):
                    dve.wait_ge(c_rstd, 10 * b + g + 1)
                    normalise(lambda j: n3[:, G * g + j, :], res_tile(g), g)
                    dve.drain().then_inc(c_n, 1)
                for i in range(TB):
                    dve.wait_ge(c_vp_psum, TB * b + i + 1)
                    dve.tensor_copy(VP[:, i, :], bank(i % 4)[:, 0:DV]).then_inc(c_vp, 1)

                def attended(i):
                    g, j = i // G, i % G
                    dve.wait_ge(c_att, TB * b + i + 1)
                    dve.reciprocal(rowinv[:, i:i + 1], rowsum[:, i:i + 1])
                    dve.drain()
                    o = bank(6 + i % 2)
                    dve.scalar_tensor_tensor(acc[:, g, j, :], o[:, 0:D], rowinv[:, i:i + 1], n3[:, i, :],
                                             ALU.mult, ALU.add)
                    dve.tensor_scalar(s2raw[:, g, j, :], o[:, D:DV], rowinv[:, i:i + 1], None, ALU.mult
                                      ).then_inc(c_acc, 1)

                for i in range(TB):
                    L = (i + 1) * P
                    dve.wait_ge(c_scores, TB * b + i + 1)
                    dve.tensor_reduce(negmax[:, i:i + 1], ps[:, 2 * (i % 2):2 * (i % 2) + 2, :].rearrange(
                        "p a n -> p (a n)")[:, 0:L], X, ALU.max, negate=True).then_inc(c_max, 1)
                    if i:
                        attended(i - 1)
                attended(TB - 1)
                dve.drain()

                def layer_norm(g, n):
                    group_moments(lambda j: acc[:, g, j, :], n % 2, c_moments)
                    dve.wait_ge(c_rstd, 10 * b + n + 1)
                    normalise(lambda j: acc[:, g, j, :], lambda j: acc[:, g, j, :], n % 2)
                    a = acc[:, g, :, :]
                    dve.tensor_tensor(a, a, rows4(gamma_s[:]), ALU.mult)
                    dve.drain()
                    dve.tensor_tensor(a, a, rows4(beta_s[:]), ALU.add)
                    dve.drain()

                for g in range(GB):
                    a = acc[:, g, :, :]
                    dve.tensor_reduce(top3[:], s2raw[:, g, :, :], X, ALU.max)
                    dve.drain()
                    dve.tensor_tensor(s2raw[:, g, :, :], s2raw[:, g, :, :], cols(top3[:], C), ALU.subtract
                                      ).then_inc(d_shift, 1)
                    layer_norm(g, 2 + 4 * g)
                    dve.wait_ge(d_exp, GB * b + g + 1)
                    dve.tensor_reduce(total3[:], s2raw[:, g, :, :], X, ALU.add)
                    dve.drain()
                    dve.reciprocal(total3[:], total3[:])
                    dve.drain()
                    dve.wait_ge(d_att, GB * b + g + 1)
                    for j in range(G):
                        dve.scalar_tensor_tensor(acc[:, g, j, :],
                                                 bank(1 + j // 2)[:, (j % 2) * D:(j % 2 + 1) * D],
                                                 total3[:, j:j + 1], acc[:, g, j, :], ALU.mult, ALU.add)
                    dve.drain()
                    layer_norm(g, 3 + 4 * g)
                    dve.drain().then_inc(d_norm2, 1)
                    dve.wait_ge(d_nT_psum, GB * b + g + 1)
                    dve.tensor_tensor(a, a, rows4(f2b_s[:]), ALU.add)
                    dve.wait_ge(d_f1, GB * b + g + 1)
                    dve.scalar_tensor_tensor(f_hT[:], f_pre[:], 0.2, f_pre[:], ALU.mult, ALU.max
                                             ).then_inc(d_hT, 1)
                    dve.drain()
                    dve.wait_ge(d_ff, GB * b + g + 1)
                    dve.tensor_tensor(a.rearrange("p j d -> p (j d)"),
                                      ps[:, 4:6, :].rearrange("p a n -> p (a n)"),
                                      a.rearrange("p j d -> p (j d)"), ALU.add)
                    dve.drain()
                    layer_norm(g, 4 + 4 * g)
                    dve.tensor_scalar(a, a, 0.0, gates[:, 1:2], ALU.max, ALU.mult)
                    dve.drain()
                    dve.tensor_tensor(res_group(g), res_group(g), a, ALU.add)
                    dve.drain()
                    n = 5 + 4 * g
                    group_moments(res_tile(g), n % 2, c_moments)
                    dve.wait_ge(c_rstd, 10 * b + n + 1)
                    if g:
                        dve.wait_ge(d_stored, 16 * (GB * b + g))
                    normalise(lambda j: acc[:, g, j, :], res_tile(g), n % 2)
                    dve.tensor_copy(split3[:, :, 0:D], a)
                    dve.drain()
                    dve.tensor_tensor(split3[:, :, D:2 * D], a, split3[:, :, 0:D], ALU.subtract
                                      ).then_inc(d_n4, 1)
                    dve.wait_ge(d_logits, GB * b + g + 1)
                    dve.tensor_tensor(logits[:, bass.ds(TB * b + G * g, G), :],
                                      bank(6)[:, 0:G * E].rearrange("p (j e) -> p j e", j=G),
                                      rows4(bg_s[:]), ALU.add)
                    dve.drain().then_inc(d_logits_in, 1)
                stage_end(dve, END_2 + 1 + b)

            dve.tensor_reduce(gsum[:], logits[:], X, ALU.max)
            dve.drain()
            dve.tensor_tensor(pe_exp[:], logits[:], cols(gsum[:], E), ALU.subtract).then_inc(r_shift, 1)
            dve.wait_ge(r_exp, 1)
            dve.tensor_reduce(gsum[:], pe_exp[:], X, ALU.add)
            for t in range(NT):
                dve.max(gtop[:, t, :], pe_exp[:, t, :])
            dve.drain()
            for t in range(NT):
                dve.max_index(gidx[:, t, :], gtop[:, t, :], pe_exp[:, t, :])
            dve.tensor_reduce(denom[:], gtop[:, :, 0:K], X, ALU.add)
            dve.drain()
            dve.scalar_tensor_tensor(denom[:], gsum[:], 1e-8, denom[:], ALU.mult, ALU.add)
            dve.tensor_copy(gidx_f[:], gidx[:, :, 0:K])
            dve.drain()
            dve.reciprocal(denom[:], denom[:])
            dve.wait_ge(r_const, 1)
            for k in range(K):
                dve.tensor_tensor(onehot[:, :, k, :], iota_e[:].unsqueeze(1).to_broadcast([P, NT, E]),
                                  cols(gidx_f[:, :, k], E), ALU.is_equal)
            dve.drain()
            dve.tensor_tensor(count[:], onehot[:, :, 0, :], onehot[:, :, 1, :], ALU.add).then_inc(r_count, 1)
            dve.tensor_tensor(weight[:], gtop[:, :, 0:K], cols(denom[:], K), ALU.mult)
            dve.drain()
            dve.tensor_scalar(weight[:], weight[:], gates[:, 3:4], None, ALU.mult)
            dve.drain()
            dve.tensor_tensor(picked[:], onehot[:], cols(weight[:], E), ALU.mult)
            dve.drain()
            dve.tensor_tensor(combine[:], picked[:, :, 0, :], picked[:, :, 1, :], ALU.add).then_inc(r_combine, 1)
            dve.wait_ge(r_prefix, 1)
            dve.tensor_copy(tiles_upto[:, 0, :, :].rearrange("p t e -> p (t e)"), bank(1)[:, 0:NT * E])
            dve.drain()
            a, shift = 0, 1
            while shift < NT:
                dve.tensor_copy(tiles_upto[:, 1 - a, 0:shift, :], tiles_upto[:, a, 0:shift, :])
                dve.tensor_tensor(tiles_upto[:, 1 - a, shift:NT, :], tiles_upto[:, a, shift:NT, :],
                                  tiles_upto[:, a, 0:NT - shift, :], ALU.add)
                dve.drain()
                a, shift = 1 - a, 2 * shift
            upto = tiles_upto[:, a, :, :]
            dve.tensor_scalar(etiles[:], upto[:, NT - 1, :], 1.0 / P, (P - 1.0) / P - 0.5 + 0.5 / P,
                              ALU.mult, ALU.add)
            dve.drain()
            dve.tensor_scalar(etiles[:], etiles[:], MAGIC, -MAGIC, ALU.add, ALU.add)
            dve.drain()
            dve.tensor_copy(eend[:, 0, :], etiles[:])
            dve.drain()
            a2, shift = 0, 1
            while shift < E:
                dve.tensor_copy(eend[:, 1 - a2, 0:shift], eend[:, a2, 0:shift])
                dve.tensor_tensor(eend[:, 1 - a2, shift:E], eend[:, a2, shift:E], eend[:, a2, 0:E - shift], ALU.add)
                dve.drain()
                a2, shift = 1 - a2, 2 * shift
            ends = eend[:, a2, :]
            dve.tensor_tensor(ended[:], cols(iota_j[:], E), ends.unsqueeze(1).to_broadcast([P, TILES, E]),
                              ALU.is_ge)
            dve.tensor_tensor(etiles[:], ends, etiles[:], ALU.subtract)
            dve.drain()
            dve.tensor_reduce(tile_expert_f[:], ended[:], X, ALU.add)
            dve.tensor_tensor(prefix[:], upto, count_total(ps, NT, E), ALU.subtract)
            dve.drain()
            dve.tensor_scalar(tile_expert[:], tile_expert_f[:], E - 1.0, None, ALU.min)
            dve.tensor_tensor(prefix[:], bank(0)[:, 0:NT * E].rearrange("p (t e) -> p t e", t=NT), prefix[:],
                              ALU.add)
            dve.drain().then_inc(r_expert, 1)
            dve.scalar_tensor_tensor(prefix[:], etiles[:].unsqueeze(1).to_broadcast([P, NT, E]), float(P),
                                     prefix[:], ALU.mult, ALU.add)
            dve.drain()
            dve.tensor_tensor(picked[:], onehot[:], prefix[:].unsqueeze(2).to_broadcast([P, NT, K, E]), ALU.mult)
            dve.drain()
            dve.tensor_reduce(place[:], picked[:], X, ALU.add)
            dve.drain()
            dve.tensor_scalar(place_hi[:], place[:], 1.0 / P, -0.5 + 0.5 / P, ALU.mult, ALU.add)
            dve.drain()
            dve.tensor_scalar(place_hi[:], place_hi[:], MAGIC, -MAGIC, ALU.add, ALU.add)
            dve.drain()
            dve.scalar_tensor_tensor(place_lo[:], place_hi[:], -float(P), place[:], ALU.mult, ALU.add)
            hi_flat = place_hi[:].rearrange("p t k -> p (t k)")
            dve.tensor_tensor(hot_hi[:], iota_j[:].unsqueeze(1).to_broadcast([P, NTK, TILES]),
                              cols(hi_flat, TILES), ALU.is_equal)
            dve.drain()
            dve.tensor_tensor(hot_hi[:], hot_hi[:], cols(token_code[:].rearrange("p t k -> p (t k)"), TILES),
                              ALU.mult)
            dve.drain()
            lo_flat = place_lo[:].rearrange("p t k -> p (t k)")
            for q in range(NTK // 8):
                if q >= 2:
                    dve.wait_ge(r_hot_used, q - 1)
                dve.tensor_tensor(hot_lo[:, q % 2, :, :], iota_p[:].unsqueeze(1).to_broadcast([P, 8, P]),
                                  cols(lo_flat[:, 8 * q:8 * q + 8], P), ALU.is_equal).then_inc(r_hot, 1)
            dve.wait_ge(r_code, 1)
            dve.tensor_copy(code[:], bank(2)[:, 0:TILES])
            dve.drain()
            dve.tensor_scalar(dst_f[:], code[:], 0.0, pad_row[:, 0:1], ALU.is_equal, ALU.mult)
            dve.tensor_scalar(src_f[:], code[:], 0.5, -0.75, ALU.mult, ALU.add)
            dve.drain()
            dve.tensor_tensor(dst_f[:], dst_f[:], code[:], ALU.add)
            dve.tensor_scalar(src_f[:], src_f[:], MAGIC, -MAGIC, ALU.add, ALU.add)
            dve.drain()
            dve.tensor_scalar(dst_row[:], dst_f[:], -1.0, None, ALU.add)
            dve.tensor_scalar(src_row[:], src_f[:], 0.0, None, ALU.max)
            dve.drain()
            dve.wait_ge(r_cT_psum, 1)
            for t in range(NT):
                dve.tensor_copy(combineT[:, t, :], ps[0:E, 4 + t // 4, (t % 4) * P:(t % 4 + 1) * P])
            dve.drain().then_inc(r_cT, 1)
            for n in range(NT // 4):
                dve.wait_ge(r_b2, n + 1)
                for h in range(2):
                    t = 4 * n + 2 * h
                    r = res[:, t:t + 2, :].rearrange("p j d -> p (j d)")
                    last = dve.tensor_tensor(r, bank(2 * (n % 2) + h), r, ALU.add)
                last.then_inc(r_b2_in, 1)
            stage_end(dve, END_4)

            def take_xT(j):
                dve.wait_ge(m_xT_psum, j[0] + 1)
                dve.tensor_copy(xT[:, j[1] % U, :, :, :].rearrange("p a c n -> p (a c n)"),
                                bank16(6 * (j[1] % 2))[:, 0:4 * P]).then_inc(m_xT, 1)

            def name_rows(j):
                dve.tensor_copy(src_now[:, j[1] % U:j[1] % U + 1], src_row[:, bass.ds(j[0], 1)]).then_inc(m_src, 1)

            def split_hidden(j):
                v = j[1] % 2
                dve.wait_ge(m_hid, j[0] + 1)
                hi = hid16[:, v, 0, :, :].rearrange("p m n -> p (m n)")
                lo = hid16[:, v, 1, :, :].rearrange("p m n -> p (m n)")
                dve.tensor_copy(hi, hid[:, v, :])
                dve.drain()
                dve.tensor_tensor(lo, hid[:, v, :], hi, ALU.subtract).then_inc(m_hid16, 1)

            def take_y(j, stored):
                u = j[1] % U
                dve.wait_ge(m_y_psum, j[0] + 1)
                if stored is not None:
                    dve.wait_ge(m_out[u], 16 * stored)
                dve.tensor_copy(dst_now[:, u:u + 1], dst_row[:, bass.ds(j[0], 1)])
                dve.tensor_copy(rows_out[:, u, :], bank(1)[:, 0:D]).then_inc(m_y, 1)

            for j in range(U):
                name_rows((j, j))
            take_xT((0, 0))
            take_xT((1, 1))
            for j in range(TURN):
                if j:
                    take_y((j - 1, j - 1), (j - 1) // U or None)
                take_xT((j + 2, j + 2))
                name_rows((j + U, j + U))
                split_hidden((j, j))
            with dve.Fori(1, TILES // TURN - 1) as i:
                for q in range(TURN):
                    j = TURN * i + q
                    take_y((j - 1, q + TURN - 1), 2 * i + (q - 1) // U)
                    take_xT((j + 2, q + 2))
                    name_rows((j + U, q + U))
                    split_hidden((j, q))
            for j in range((TILES // TURN - 1) * TURN, TILES):
                take_y((j - 1, j - 1), (j - 1) // U)
                if j + 2 < TILES:
                    take_xT((j + 2, j + 2))
                if j + U < TILES:
                    name_rows((j + U, j + U))
                split_hidden((j, j))
            take_y((TILES - 1, TILES - 1), (TILES - 1) // U)
            stage_end(dve, END_5)

            for g in range(NT // G):
                dve.wait_ge(z_in[g % 2], 16 * (g // 2 + 1))
                for k in range(K):
                    for j in range(G):
                        t = G * g + j
                        dve.scalar_tensor_tensor(res[:, t, :], both[:, g % 2, j, k, :], weight[:, t, k:k + 1],
                                                 res[:, t, :], ALU.mult, ALU.add)
                    dve.drain()
                dve.drain().then_inc(z_sum, 1)

        @block.tensor
        def _(pe):
            def done(ins):
                ins.then_inc(su_psum, 1)

            pe.wait_ge(in_w, 16 * 10)
            pe.wait_ge(const_made, 1)
            for c in range(DC):
                for b in range(B):
                    at = (c * B + b) * C
                    last = pe.transpose(bank(0)[:, at:at + C], ctx_s[:, b, c * P:(c + 1) * P], ident[0:C, 0:C])
            done(last)
            for n, name in enumerate(("W", "Wq1", "Wk1", "Wq2", "Wv1")):
                for c in range(DC):
                    for c2 in range(DC):
                        last = pe.transpose(bank(1 + n)[:, c2 * D + c * P:c2 * D + (c + 1) * P],
                                            raw[name][:, c, c2 * P:(c2 + 1) * P], ident[:])
                done(last)
            n_rows = E * HC + DC
            done(pe.transpose(bank(6)[:, 0:n_rows], bias_rows[:], ident[0:n_rows, 0:n_rows]))
            pe.wait_ge(su_copied, 1)

            def product(dst, lhsT, rhs, n=DC):
                for c in range(n):
                    last = pe.matmul(dst, lhsT(c), rhs(c), start=(c == 0), stop=(c == n - 1))
                return last

            for b in range(B):
                last = product(ps[0:C, 0, b * D:(b + 1) * D], lambda c: ctxT[:, c, b, :], lambda c: raw["WT"][:, c, :])
            done(last)
            for o in range(DC):
                last = product(bank(1)[:, o * D:(o + 1) * D], lambda c: raw["Wq1T"][:, c, o * P:(o + 1) * P],
                               lambda c: raw["Wk1T"][:, c, :])
            done(last)
            for o in range(DC):
                last = product(bank(2)[:, o * B * C:(o + 1) * B * C], lambda c: raw["Wk2"][:, c, o * P:(o + 1) * P],
                               lambda c: ctxT[:, c, :, :].rearrange("p b k -> p (b k)"))
            done(last)
            for b in range(B):
                last = product(ps[0:C, 3, b * D:(b + 1) * D], lambda c: ctxT[:, c, b, :], lambda c: raw["Wv2"][:, c, :])
            done(last)
            pe.wait_ge(su_copied, 2)
            for b in range(B):
                for c in range(DC):
                    at = (b * DC + c) * C
                    last = pe.transpose(bank(4)[:, at:at + C], tq[:, b, c * P:(c + 1) * P], ident[0:C, 0:C])
            done(last)
            for o in range(DC):
                last = product(bank(5)[:, o * B * C:(o + 1) * B * C], lambda c: raw["Wq2T"][:, c, o * P:(o + 1) * P],
                               lambda c: K2T[:, c, :])
            done(last)
            pe.wait_ge(su_copied, 3)
            for o in range(DC):
                last = product(bank(6)[:, o * B * C:(o + 1) * B * C], lambda c: raw["Wv1T"][:, c, o * P:(o + 1) * P],
                               lambda c: A2[:, c, :])
            done(last)
            pe.wait_ge(su_abs, 1)
            done(pe.matmul(bank(7)[:, 0:2], ones[:], w_abs[:], start=True, stop=True))
            pe.wait_ge(su_tern, 1)
            for c in range(DC):
                for m in range(HC):
                    last = pe.transpose(bank16(c)[:, m * P:(m + 1) * P], t1_s[:, m, c * P:(c + 1) * P], ident16[:])
                done(last)
            pe.wait_ge(su_tern, 2)
            for n in range(2):
                for m in range(4):
                    for c in range(DC):
                        last = pe.transpose(bank16(2 + n)[:, m * D + c * P:m * D + (c + 1) * P],
                                            t2_s[:, c, (4 * n + m) * P:(4 * n + m + 1) * P], ident16[:])
                done(last)
            stage_end(pe, END_SETUP)

            def transpose_group(bank_of, tile_of):
                for j in range(G):
                    for c in range(DC):
                        last = pe.transpose(bank(bank_of(c))[:, j * P:(j + 1) * P],
                                            tile_of(j)[:, c * P:(c + 1) * P], ident[:])
                return last

            with pe.Fori(0, B) as b:
                for g in range(GB):
                    pe.wait_ge(a_h, GB * b + g + 1)
                    transpose_group(lambda c: DC * g + c, lambda j: h1[:, g, j, :]).then_inc(a_hT_psum, 1)
                for g in range(GB):
                    pe.wait_ge(a_hT, GB * b + g + 1)
                    for j in range(G):
                        for c in range(DC):
                            last = pe.matmul(bank(4 + g)[:, j * C:(j + 1) * C], hT[:, g, c, j * P:(j + 1) * P],
                                             tqT[:, bass.ds(b, 1), c, :].rearrange("p o k -> p (o k)"),
                                             start=(c == 0), stop=(c == DC - 1))
                    last.then_inc(a_scores, 1)
                for g in range(GB):
                    pe.wait_ge(a_probs, GB * b + g + 1)
                    for j in range(G):
                        last = pe.transpose(ps[0:C, 6 + g, j * P:(j + 1) * P], probs[:, g, j, :], ident[:])
                    last.then_inc(a_pT_psum, 1)
                for g in range(GB):
                    pe.wait_ge(a_pT, GB * b + g + 1)
                    for j in range(G):
                        last = pe.matmul(bank(2 * g + j // 2)[:, (j % 2) * D:(j % 2 + 1) * D],
                                         probsT[:, g, j * P:(j + 1) * P],
                                         tq[:, bass.ds(b, 1), :].rearrange("p o d -> p (o d)"),
                                         start=True, stop=True)
                    last.then_inc(a_vec, 1)
                for g in range(GB):
                    pe.wait_ge(a_q, GB * b + g + 1)
                    for c in range(DC):
                        for j in range(G):
                            last = pe.transpose(bank16(4 + g)[:, (c * G + j) * P:(c * G + j + 1) * P],
                                                q1[:, g, j, c * P:(c + 1) * P], ident16[:])
                    last.then_inc(a_qT_psum, 1)
                stage_end(pe, END_SETUP + 1 + b)

            pe.wait_ge(in_vec2, 48)

            q1T_tiles = q1T[:].rearrange("p g c (j n) -> p g c j n", j=G)

            def first_layer(t, u, j):
                pe.wait_ge(f_diag, t + 1)
                for n in range(2):
                    hp = bank(2 * u + n)
                    pe.matmul(hp, diag[:, u, :], b1_s[:, n * 512:(n + 1) * 512], start=True, stop=False)
                for c in range(DC):
                    lhsT = q1T_flat(q1T, t, c, j, G, P, DC)
                    for n in range(2):
                        last = pe.matmul(bank(2 * u + n), lhsT, T1[:, c, n * 512:(n + 1) * 512],
                                         start=False, stop=(c == DC - 1))
                last.then_inc(f_hidden, 1)

            def transposes(t, u):
                pe.wait_ge(f_q, t + 1)
                for m in range(HC):
                    last = pe.transpose(bank16(4 + u)[:, m * P:(m + 1) * P], q2[:, u, m * P:(m + 1) * P], ident16[:])
                last.then_inc(f_qT_psum, 1)

            def second_layer(t, u):
                pe.wait_ge(f_qT, t + 1)
                for m in range(HC):
                    last = pe.matmul(bank(6 + u)[:, 0:D], q2T[:, u, m, :], T2[:, m, :],
                                     start=(m == 0), stop=(m == HC - 1))
                last.then_inc(f_y, 1)

            def stage2_tile(t, u, j, ahead):
                transposes(t, u)
                if ahead:
                    first_layer(t + 3, 1 - u, j)
                second_layer(t, u)

            for t in range(3):
                if t == 2:
                    pe.wait_ge(f_gelu, 1)
                first_layer(t, t % 2, t)
            stage2_tile(0, 0, 3, True)
            with pe.Fori(0, NT // G - 1) as i:
                for q in range(G):
                    stage2_tile(G * i + 1 + q, (q + 1) % 2, q, True)
            for t in range(NT - G + 1, NT):
                stage2_tile(t, t % 2, 0, False)
            stage_end(pe, END_2)

            pe.wait_ge(in_late, 16 * 8)
            with pe.Fori(0, B) as b:
                for g in range(GB):
                    pe.wait_ge(c_n, GB * b + g + 1)
                    transpose_group(lambda c: DC * g + c, lambda j: n3[:, G * g + j, :]).then_inc(c_nT_psum, 1)
                for g in range(GB):
                    pe.wait_ge(c_nT, GB * b + g + 1)
                    for o in range(DC):
                        product(bank(4 + 2 * g + o), lambda c: M1[:, c, o * P:(o + 1) * P],
                                lambda c: nT[:, c, g * 512:(g + 1) * 512]).then_inc(c_qm_psum, 1)
                for i in range(TB):
                    if i >= 4:
                        pe.wait_ge(c_vp, TB * b + i - 3)
                    product(bank(i % 4)[:, 0:DV], lambda c: nT[:, c, i * P:(i + 1) * P],
                            lambda c: WVA[:, bass.ds(b, 1), c, :].rearrange("p o k -> p (o k)")
                            ).then_inc(c_vp_psum, 1)
                pe.wait_ge(c_vp, TB * (b + 1))
                pe.wait_ge(c_qm, 2 * GB * (b + 1))

                def scores(i):
                    L = (i + 1) * P
                    for h in range((L + 511) // 512):
                        n = min(512, L - h * 512)
                        at = bank(2 * (i % 2) + h)
                        for c in range(DC):
                            last = pe.matmul(at[:, 0:n], QmT[:, c, i * P:(i + 1) * P],
                                             nT[:, c, h * 512:h * 512 + n], start=(c == 0),
                                             stop=(c == DC - 1 and h != i // 4))
                        if h == i // 4:
                            last = pe.matmul(at[:, (i % 4) * P:(i % 4 + 1) * P], ident[:], causal[:],
                                             start=False, stop=True)
                    last.then_inc(c_scores, 1)

                scores(0)
                for i in range(TB):
                    pe.wait_ge(c_exp, TB * b + i + 1)
                    for j in range(i + 1):
                        last = pe.transpose(bank(4 + j // 4)[:, (j % 4) * P:(j % 4 + 1) * P],
                                            Pr[:, j * P:(j + 1) * P], ident[:])
                    last.then_inc(c_pT_psum, 1)
                    if i + 1 < TB:
                        scores(i + 1)
                    pe.wait_ge(c_pT, TB * b + i + 1)
                    if i >= 2:
                        pe.wait_ge(c_acc, TB * b + i - 1)
                    product(bank(6 + i % 2)[:, 0:DV], lambda j: PT[:, j * P:(j + 1) * P],
                            lambda j: VP[:, j, :], i + 1).then_inc(c_att, 1)
                pe.wait_ge(c_acc, TB * (b + 1))
                for g in range(GB):
                    pe.wait_ge(d_exp, GB * b + g + 1)
                    for j in range(G):
                        last = pe.transpose(ps[0:C, 0, j * P:(j + 1) * P], s2raw[:, g, j, :], ident[:])
                    last.then_inc(d_pT_psum, 1)
                    pe.wait_ge(d_pT, GB * b + g + 1)
                    for j in range(G):
                        last = pe.matmul(bank(1 + j // 2)[:, (j % 2) * D:(j % 2 + 1) * D], p2T[:, j * P:(j + 1) * P],
                                         V2[:, bass.ds(b, 1), :].rearrange("p o d -> p (o d)"),
                                         start=True, stop=True)
                    last.then_inc(d_att, 1)
                    pe.wait_ge(d_norm2, GB * b + g + 1)
                    transpose_group(lambda c: c, lambda j: acc[:, g, j, :]).then_inc(d_nT_psum, 1)
                    pe.wait_ge(d_nT, GB * b + g + 1)
                    for o in range(DC):
                        last = product(bank(2 + o), lambda c: F1_s[:, c, o * P:(o + 1) * P], lambda c: n2T[:, c, :])
                    last.then_inc(d_f1_psum, 1)
                    pe.wait_ge(d_hT, GB * b + g + 1)
                    for j in range(G):
                        last = product(bank(4 + j // 2)[:, (j % 2) * D:(j % 2 + 1) * D],
                                       lambda c: f_hT[:, c, j * P:(j + 1) * P], lambda c: F2_s[:, c, :])
                    last.then_inc(d_ff, 1)
                    pe.wait_ge(d_n4, GB * b + g + 1)
                    transpose_group(lambda c: c, lambda j: acc[:, g, j, :]).then_inc(d_n4T_psum, 1)
                    pe.wait_ge(d_n4T, GB * b + g + 1)
                    for j in range(G):
                        last = product(bank(6)[:, j * E:(j + 1) * E], lambda c: n2T[:, c, j * P:(j + 1) * P],
                                       lambda c: Wg_s[:, c, :])
                    last.then_inc(d_logits, 1)
                stage_end(pe, END_2 + 1 + b)

            pe.wait_ge(r_const, 1)
            pe.wait_ge(r_count, 1)
            flat_count = count[:].rearrange("p t e -> p (t e)")
            pe.matmul(bank(0)[:, 0:NT * E], strictly_lower[:], flat_count, start=True, stop=True)
            pe.matmul(bank(1)[:, 0:NT * E], ones5[:], flat_count, start=True, stop=True).then_inc(r_prefix, 1)
            pe.wait_ge(r_combine, 1)
            for t in range(NT):
                last = pe.transpose(ps[0:E, 4 + t // 4, (t % 4) * P:(t % 4 + 1) * P], combine[:, t, :], ident[:])
            last.then_inc(r_cT_psum, 1)
            for q in range(NTK // 8):
                pe.wait_ge(r_hot, q + 1)
                for k in range(8):
                    n = 8 * q + k
                    last = pe.matmul(bank(2)[:, 0:TILES], hot_lo[:, q % 2, k, :], hot_hi[:, n, :],
                                     start=(n == 0), stop=(n == NTK - 1))
                last.then_inc(r_hot_used, 1)
                if q == NTK // 8 - 1:
                    pe.drain().then_inc(r_code, 1)
            pe.wait_ge(r_cT, 1)
            for n in range(NT // 4):
                if n >= 2:
                    pe.wait_ge(r_b2_in, n - 1)
                for j in range(4):
                    last = pe.matmul(bank(2 * (n % 2) + j // 2)[:, (j % 2) * D:(j % 2 + 1) * D],
                                     combineT[:, 4 * n + j, :], e2b_s[:], start=True, stop=True)
                last.then_inc(r_b2, 1)
            stage_end(pe, END_4)

            def tile_in(j, turn):
                u = j[1] % U
                pe.wait_ge(m_rows[u], 16 * (turn + 1))
                for n in range(2 * DC):
                    last = pe.transpose(bank16(6 * (j[1] % 2))[:, n * P:(n + 1) * P],
                                        rows_in[:, u, n * P:(n + 1) * P], ident16[:])
                last.then_inc(m_xT_psum, 1)

            def expert_of(j):
                return pe.value_load(tile_expert[0:1, bass.ds(j[0], 1)], min_val=0, max_val=E - 1)

            def first_product(j, e):
                u, v = j[1] % U, j[1] % 2
                pe.wait_ge(m_xT, j[0] + 1)
                hi, lo = expert_w1_at(EWS, e, 0, DC, H), expert_w1_at(EWS, e, 1, DC, H)
                for m in range(HC):
                    dst = bank(2 + 2 * v + m // 4)[:, (m % 4) * P:(m % 4 + 1) * P]
                    terms = [(w(c, m), xT[:, u, a, c, :]) for c in range(DC) for w, a in ((hi, 0), (hi, 1), (lo, 0))]
                    for n, (lhsT, rhs) in enumerate(terms):
                        last = pe.matmul(dst, lhsT, rhs, start=(n == 0), stop=(n == len(terms) - 1))
                last.then_inc(m_hid_psum, 1)

            def second_product(j, e):
                v = j[1] % 2
                pe.wait_ge(m_hid16, j[0] + 1)
                hi, lo = expert_w2_at(EWS, e, 0, DC, H, HC, D), expert_w2_at(EWS, e, 1, DC, H, HC, D)
                terms = [(hid16[:, v, a, m, :], w(m)) for m in range(HC) for a, w in ((0, hi), (0, lo), (1, hi))]
                for n, (lhsT, rhs) in enumerate(terms):
                    last = pe.matmul(bank(1)[:, 0:D], lhsT, rhs, start=(n == 0), stop=(n == len(terms) - 1))
                last.then_inc(m_y_psum, 1)

            def step(j0, q, turn):
                e_next, e_now = expert_of((j0 + 1, q + 1)), expert_of((j0, q))
                if turn is not None:
                    tile_in((j0 + 2, q + 2), turn)
                first_product((j0 + 1, q + 1), e_next)
                second_product((j0, q), e_now)

            pe.wait_ge(r_expert, 1)
            tile_in((0, 0), 0)
            tile_in((1, 1), 0)
            first_product((0, 0), expert_of((0, 0)))
            with pe.Fori(0, TILES // TURN) as i:
                for q in range(TURN):
                    step(TURN * i + q, q, 2 * i + (q + 2) // U)
            for j in range(TILES // TURN * TURN, TILES - 1):
                step(j, j, (j + 2) // U if j + 2 < TILES else None)
            second_product((TILES - 1, TILES - 1), expert_of((TILES - 1, TILES - 1)))
            stage_end(pe, END_5)


def count_total(ps, NT, E):
    return ps[:, 1, 0:NT * E].rearrange("p (t e) -> p t e", t=NT)


def q1T_flat(q1T, t, c, j, G, P, DC):
    flat = q1T[:].rearrange("p g c n -> p (g c n)")
    return flat[:, bass.ds((t - j) * (DC * P) + c * G * P + j * P, P)]


def expert_w1_at(EWS, e, part, DC, H):
    flat = EWS[:].rearrange("p e n -> p (e n)")
    return lambda c, m: flat[:, bass.ds(e * EWS.shape[2] + part * DC * H + c * H + m * P, P)]


def expert_w2_at(EWS, e, part, DC, H, HC, D):
    flat = EWS[:].rearrange("p e n -> p (e n)")
    return lambda m: flat[:, bass.ds(e * EWS.shape[2] + 2 * DC * H + part * HC * D + m * D, D)]


_INS = ['x', 'ctx_1024', 'g_xattn', 'g_ffn', 'L0_xattn_W', 'L0_xattn_b', 'L0_ffn_ln1_g', 'L0_ffn_ln1_b',
        'L0_ffn_w1', 'L0_ffn_b1', 'L0_ffn_ln2_g', 'L0_ffn_ln2_b', 'L0_ffn_w2', 'L0_ffn_b2',
        'L1_xattn_Wk1', 'L1_xattn_Wq1', 'L1_xattn_Wv1', 'L1_xattn_Wk2', 'L1_xattn_Wq2', 'L1_xattn_Wv2',
        'L1_xattn_W1', 'L1_xattn_b1', 'L1_xattn_W2', 'L1_xattn_b2', 'L1_xattn_gamma', 'L1_xattn_beta',
        'L1_ffn_Wg', 'L1_ffn_bg', 'L1_ffn_W1', 'L1_ffn_b1', 'L1_ffn_W2', 'L1_ffn_b2']
_OUTS = [((2, 1024, 256), 'float32')]


def kernel(**inputs):
    import numpy as _np
    import concourse.bacc as _bacc
    from concourse import mybir as _mybir
    from concourse.bass_utils import run_bass_kernel_spmd as _run

    nc = _bacc.Bacc("TRN2", target_bir_lowering=False, num_devices=1)
    arrays, args = {}, []
    for name in _INS:
        a = _np.ascontiguousarray(inputs[name])
        arrays[f"in_{name}_dram"] = a
        args.append(nc.dram_tensor(f"in_{name}_dram", a.shape, _mybir.dt.from_np(a.dtype), kind="ExternalInput").ap())
    for i, (shape, dtype) in enumerate(_OUTS):
        dt = _mybir.dt.from_np(_np.dtype(dtype))
        args.append(nc.dram_tensor(f"out_{i}_dram", shape, dt, kind="ExternalOutput").ap())
    gated_blocks_kernel(nc, *args)
    r = _run(nc, [arrays], core_ids=[0])
    got = tuple(r.results[0][f"out_{i}_dram"] for i in range(len(_OUTS)))
    return got[0]
```

```python
from contextlib import ExitStack

import concourse.bass as bass
from concourse import mybir

F32 = mybir.dt.float32
BF16 = mybir.dt.bfloat16
I32 = mybir.dt.int32
U32 = mybir.dt.uint32
ALU = mybir.AluOpType
ACT = mybir.ActivationFunctionType
X = mybir.AxisListType.X

P = 128
MAGIC = 1.5 * 2.0 ** 23
LN_EPS = 1e-5
L1_EPS = 1e-3
MASKED = -1e30


def gated_blocks_kernel(
    nc: bass.Bass, x, ctx_in, g_xattn, g_ffn,
    W, Wb, ln1_g, ln1_b, w1, b1, ln2_g, ln2_b, w2, b2,
    Wk1, Wq1, Wv1, Wk2, Wq2, Wv2, F1, f1b, F2, f2b, gamma, beta,
    Wg, bg, E1, e1b, E2, e2b, out,
):
    B, S, D = x.shape
    C = ctx_in.shape[1]
    H = w1.shape[0]
    E = Wg.shape[1]
    DC, HC = D // P, H // P
    NT = B * S // P
    TB = S // P
    G = 4
    GB = TB // G
    DV = D + C
    K = 2
    SLOTS = B * S * K
    TILES = (SLOTS + E * (P - 1)) // P
    U = 3
    TURN = 2 * U
    assert D == 256 and S == 1024 and H == 1024 and TILES % U == 0 and TB == GB * G
    EW = 2 * DC * H + 2 * HC * D
    BLK = 1024
    EBLK = EW // 2 // BLK
    EARLY = 5

    split_rows = nc.dram_tensor("split_rows", (B * S, 2 * D), BF16, kind="Internal").ap()
    choice_rows = nc.dram_tensor("choice_rows", (SLOTS + P, D), F32, kind="Internal").ap()

    x_tiles = x.rearrange("b (t p) d -> p (b t) d", p=P)
    out_tiles = out.rearrange("b (t p) d -> p (b t) d", p=P)

    with ExitStack() as stack:
        def sem(name):
            return stack.enter_context(nc.semaphore(name))

        def keep(name, shape, dt=F32):
            return stack.enter_context(nc.sbuf_tensor(name, shape, dt))

        ps = stack.enter_context(nc.psum_tensor("ps", [P, 8, 512], F32))

        def bank(k):
            return ps[:, k, :]

        def bank16(k):
            return ps[:, k, :].bitcast(BF16)

        res = keep("res", [P, NT, D])
        EWS = keep("EWS", [P, E, EW], BF16)
        stage_in = keep("stage_in", [P, 2, BLK])
        ident = keep("ident", [P, P])
        ident16 = keep("ident16", [P, P], BF16)
        causal = keep("causal", [P, P])
        gates = keep("gates", [P, 4])
        minus_half = keep("minus_half", [P, G])
        stats = keep("stats", [P, G, 6])
        moments = keep("moments", [P, 4, G, 2])
        rstd = keep("rstd", [P, 4, G])
        expert_b1 = keep("expert_b1", [P, E * HC])
        logits = keep("logits", [P, NT, E])
        Wg_s = keep("Wg_s", [P, DC, E])
        bg_s = keep("bg_s", [P, E])
        e2b_s = keep("e2b_s", [E, D])
        zero_col = keep("zero_col", [P, 1])

        def expert_w1(e, part):
            return EWS[:, e, part * DC * H:(part + 1) * DC * H].rearrange("p (c h) -> p c h", c=DC)

        def expert_w2(e, part):
            base = 2 * DC * H + part * HC * D
            return EWS[:, e, base:base + HC * D].rearrange("p (m d) -> p m d", m=HC)

        def block_parts(e, k):
            if k < EBLK // 2:
                return expert_w1(e, 0)[:, k, :], expert_w1(e, 1)[:, k, :]
            m = (k - EBLK // 2) * (HC // 2)
            return tuple(expert_w2(e, part)[:, m:m + HC // 2, :].rearrange("p m d -> p (m d)")
                         for part in range(2))

        spare = EWS[:, EARLY:E, :].rearrange("p e n -> p (e n)").bitcast(F32)
        spare_size = (E - EARLY) * EW // 2

        def carve(sizes):
            at, views = 0, []
            for n in sizes:
                views.append(spare[:, at:at + n])
                at += n
            assert at <= spare_size
            return views

        early3 = ExitStack()
        stack.enter_context(early3)

        def sb3(name, shape, dt=F32):
            return early3.enter_context(nc.sbuf_tensor(name, shape, dt))

        M1 = sb3("M1", [P, DC, D])
        WVA = sb3("WVA", [P, B, DC, DV])
        V2 = sb3("V2", [C, B, D])
        F1_s = sb3("F1_s", [P, DC, D])
        F2_s = sb3("F2_s", [P, DC, D])
        f1b_s = sb3("f1b_s", [P, DC])
        f2b_s = sb3("f2b_s", [P, D])
        gamma_s = sb3("gamma_s", [P, D])
        beta_s = sb3("beta_s", [P, D])

        st12 = ExitStack()

        def sb12(name, shape, dt=F32):
            return st12.enter_context(nc.sbuf_tensor(name, shape, dt))

        T1 = sb12("T1", [P, DC, H], BF16)
        T2 = sb12("T2", [P, HC, D], BF16)
        wscale = sb12("wscale", [P, 2])
        wscale_inv = sb12("wscale_inv", [P, 2])
        wscale_127 = sb12("wscale_127", [P, 2])
        q1T = sb12("q1T", [P, NT // G, DC, G * P], BF16)
        scale1 = sb12("scale1", [P, NT])
        inverse1 = sb12("inverse1", [P, NT])
        tq = sb12("tq", [C, B, D])
        tqT = sb12("tqT", [P, B, DC, C])

        setup = ExitStack()

        def sbs(name, shape, dt=F32):
            return setup.enter_context(nc.sbuf_tensor(name, shape, dt))

        ctx_s = sbs("ctx_s", [C, B, D])
        ctxT = sbs("ctxT", [P, DC, B, C])
        raw = {n: v for n, v in zip(
            ["W", "Wq1", "Wk1", "Wq2", "Wv1", "Wk2", "Wv2", "WT", "Wq1T", "Wk1T", "Wq2T", "Wv1T"],
            [v.rearrange("p (c d) -> p c d", c=DC) for v in carve([DC * D] * 12)])}
        Wb_s = sbs("Wb_s", [P, D])
        K2T = sbs("K2T", [P, DC, B * C])
        A2 = sbs("A2", [P, DC, B * C])
        bias_rows = sbs("bias_rows", [E * HC + DC, P])
        ones = sbs("ones", [P, P])
        w_abs = sbs("w_abs", [P, 2])
        borrowed = EWS[:, EARLY - 1, :]
        w1_s = borrowed[:, 0:2 * HC * D].bitcast(F32).rearrange("p (c d) -> p c d", c=HC)
        t1_s = borrowed[:, 2 * HC * D:3 * HC * D].rearrange("p (c d) -> p c d", c=HC)
        t2_s = borrowed[:, 3 * HC * D:4 * HC * D].rearrange("p (c d) -> p c d", c=DC)
        w2_s = stage_in[:]
        graw = sbs("graw", [P, 4])
        setup.close()

        s1 = ExitStack()

        def sb1(name, shape, dt=F32):
            return s1.enter_context(nc.sbuf_tensor(name, shape, dt))

        h_v, u_v, hT_v, pT_v = carve([GB * G * D, GB * G * D, GB * DC * G * P, GB * G * P])
        h1 = h_v.rearrange("p (g j d) -> p g j d", g=GB, j=G)
        u1 = u_v.rearrange("p (g j d) -> p g j d", g=GB, j=G)
        hT = hT_v.rearrange("p (g c n) -> p g c n", g=GB, c=DC)
        probsT = pT_v[0:C, :].rearrange("p (g n) -> p g n", g=GB)
        shifted = sb1("shifted", [P, GB, G, C])
        probs = sb1("probs", [P, GB, G, C])
        q1 = sb1("q1", [P, GB, G, D], BF16)
        top = sb1("top", [P, GB, G])
        total = sb1("total", [P, GB, G])
        ln1_g_s = sb1("ln1_g_s", [P, D])
        ln1_b_s = sb1("ln1_b_s", [P, D])
        b2_s = sb1("b2_s", [P, D])
        sx1 = sb1("sx1", [P, GB, G])
        s1.close()

        y2_v, v2_v, g2_v, bb2_v, b1_v = carve([2 * H, 2 * H, H, H, H])
        y2 = y2_v.rearrange("p (u h) -> p u h", u=2)
        v2 = v2_v.rearrange("p (u h) -> p u h", u=2)
        ln2_g_s, ln2_b_s, b1_s = g2_v, bb2_v, b1_v
        s2 = ExitStack()

        def sb2(name, shape, dt=F32):
            return s2.enter_context(nc.sbuf_tensor(name, shape, dt))

        q2 = sb2("q2", [P, 2, H], BF16)
        q2T = sb2("q2T", [P, 2, HC, P], BF16)
        diag = sb2("diag", [P, 2, P])
        act_scale = sb2("act_scale", [P, 2])
        ysum = sb2("ysum", [P, 2])
        ysq = sb2("ysq", [P, 2])
        neg_mean = sb2("neg_mean", [P, 2])
        rstd2 = sb2("rstd2", [P, 2])
        vmax = sb2("vmax", [P, 2])
        sx2 = sb2("sx2", [P, 2])
        outscale = sb2("outscale", [P, 2])
        square_out = sb2("square_out", [P, 2, H], BF16)
        s2.close()
        st12.close()

        nT_v, QmT_v, n_v, P_v, PT_v, first_v, then_v = carve(
            [DC * S, DC * S, TB * D, S, S, GB * DC * G * P, GB * DC * G * P])
        nT = nT_v.rearrange("p (c s) -> p c s", c=DC)
        QmT = QmT_v.rearrange("p (c s) -> p c s", c=DC)
        n3 = n_v.rearrange("p (t d) -> p t d", t=TB)
        Pr, PT = P_v, PT_v
        ffT = first_v.rearrange("p (g c s) -> p g c s", g=GB, c=DC)
        preT = then_v.rearrange("p (g c s) -> p g c s", g=GB, c=DC)
        split3 = then_v.bitcast(BF16).rearrange("p (g j n) -> p g j n", g=GB, j=G)
        s3 = ExitStack()

        def sb3o(name, shape, dt=F32):
            return s3.enter_context(nc.sbuf_tensor(name, shape, dt))

        VP = sb3o("VP", [P, TB, DV])
        acc = sb3o("acc", [P, B, GB, G, D])
        s2raw = sb3o("s2raw", [P, B, GB, G, C])
        negmax = sb3o("negmax", [P, TB])
        rowsum = sb3o("rowsum", [P, TB])
        rowinv = sb3o("rowinv", [P, TB])
        top3 = sb3o("top3", [P, GB, G])
        total3 = sb3o("total3", [P, GB, G])
        p2T = sb3o("p2T", [C, GB, G * P])
        s3.close()
        early3.close()

        s5 = ExitStack()

        def sb5(name, shape, dt=F32):
            return s5.enter_context(nc.sbuf_tensor(name, shape, dt))

        NTK = NT * K
        weight = sb5("weight", [P, NT, K])
        src_row = sb5("src_row", [P, TILES], I32)
        dst_row = sb5("dst_row", [P, TILES], I32)
        tile_expert = sb5("tile_expert", [P, TILES], I32)
        s4 = ExitStack()

        def sb4(name, shape, dt=F32):
            return s4.enter_context(nc.sbuf_tensor(name, shape, dt))

        pe_exp = sb4("pe_exp", [P, NT, E])
        gsum = sb4("gsum", [P, NT])
        gtop = sb4("gtop", [P, NT, 8])
        gidx = sb4("gidx", [P, NT, 8], U32)
        gidx_f = sb4("gidx_f", [P, NT, K])
        onehot = sb4("onehot", [P, NT, K, E])
        count = sb4("count", [P, NT, E])
        tiles_upto = sb4("tiles_upto", [P, 2, NT, E])
        denom = sb4("denom", [P, NT])
        combine = sb4("combine", [P, NT, E])
        combineT = sb4("combineT", [E, NT, P])
        strictly_lower = sb4("strictly_lower", [P, P])
        ones5 = sb4("ones5", [P, P])
        iota_e = sb4("iota_e", [P, E])
        iota_p = sb4("iota_p", [P, P])
        iota_j = sb4("iota_j", [P, TILES])
        token_code = sb4("token_code", [P, NT, K])
        etiles = sb4("etiles", [P, E])
        eend = sb4("eend", [P, 2, E])
        prefix = sb4("prefix", [P, NT, E])
        place = sb4("place", [P, NT, K])
        picked = sb4("picked", [P, NT, K, E])
        place_hi = sb4("place_hi", [P, NT, K])
        place_lo = sb4("place_lo", [P, NT, K])
        hot_lo = sb4("hot_lo", [P, 2, 8, P])
        hot_hi = sb4("hot_hi", [P, NTK, TILES])
        code = sb4("code", [P, TILES])
        pad_row = sb4("pad_row", [P, 1])
        src_f = sb4("src_f", [P, TILES])
        dst_f = sb4("dst_f", [P, TILES])
        ended = sb4("ended", [P, TILES, E])
        tile_expert_f = sb4("tile_expert_f", [P, TILES])
        s4.close()
        src_now = sb5("src_now", [P, U], I32)
        dst_now = sb5("dst_now", [P, U], I32)
        rows_in = sb5("rows_in", [P, U, 2 * D], BF16)
        xT = sb5("xT", [P, U, 2, DC, P], BF16)
        hid = sb5("hid", [P, 2, HC * P])
        hid16 = sb5("hid16", [P, 2, 2, HC, P], BF16)
        rows_out = sb5("rows_out", [P, U, D])
        s5.close()
        both = EWS[:, 0, :].bitcast(F32).rearrange("p (g j k d) -> p g j k d", g=2, j=G, k=K)

        stage_done, waited_alone = sem("stage_done"), sem("waited_alone")
        in_x, in_w = sem("in_x"), sem("in_w")
        in_vec, in_vec2, in_late = sem("in_vec"), sem("in_vec2"), sem("in_late")
        block_in = [sem("block_in0"), sem("block_in1")]
        block_high, block_split = sem("block_high"), sem("block_split")
        const_made, ident_made = sem("const_made"), sem("ident_made")
        gates_made = sem("gates_made")
        su_psum, su_copied, su_tern, su_abs = sem("su_psum"), sem("su_copied"), sem("su_tern"), sem("su_abs")
        a_moments, a_rstd, a_h, a_hT_psum, a_hT = (sem(n) for n in (
            "a_moments", "a_rstd", "a_h", "a_hT_psum", "a_hT"))
        a_scores, a_shifted, a_probs, a_pT_psum, a_pT, a_vec = (sem(n) for n in (
            "a_scores", "a_shifted", "a_probs", "a_pT_psum", "a_pT", "a_vec"))
        a_q, a_qT_psum, a_qT = sem("a_q"), sem("a_qT_psum"), sem("a_qT")
        f_diag, f_hidden, f_gelu, f_mean, f_sq, f_rstd = (sem(n) for n in (
            "f_diag", "f_hidden", "f_gelu", "f_mean", "f_sq", "f_rstd"))
        f_scaled, f_q, f_qT_psum, f_qT, f_y = (sem(n) for n in (
            "f_scaled", "f_q", "f_qT_psum", "f_qT", "f_y"))
        c_moments, c_rstd, c_n, c_nT_psum, c_nT = (sem(n) for n in (
            "c_moments", "c_rstd", "c_n", "c_nT_psum", "c_nT"))
        c_qm_psum, c_qm, c_vp_psum, c_vp = (sem(n) for n in ("c_qm_psum", "c_qm", "c_vp_psum", "c_vp"))
        c_scores, c_max, c_exp, c_pT_psum, c_pT, c_att, c_acc = (sem(n) for n in (
            "c_scores", "c_max", "c_exp", "c_pT_psum", "c_pT", "c_att", "c_acc"))
        d_moments = [sem(f"d_moments{g}") for g in range(GB)]
        d_rstd = [sem(f"d_rstd{g}") for g in range(GB)]
        d_shift, d_exp, d_pT, d_norm2, d_nT, d_bias = (sem(n) for n in (
            "d_shift", "d_exp", "d_pT", "d_norm2", "d_nT", "d_bias"))
        d_pre, d_hT, d_norm3, d_relu, d_n4, d_hi, d_lo, d_n4T, d_stored = (sem(n) for n in (
            "d_pre", "d_hT", "d_norm3", "d_relu", "d_n4", "d_hi", "d_lo", "d_n4T", "d_stored"))
        RING = 3
        ring_full = [sem(f"ring_full{k}") for k in range(RING)]
        ring_read = [sem(f"ring_read{k}") for k in range(RING)]
        r_const, r_exp, r_count, r_prefix, r_hot, r_hot_used, r_code, r_rows, r_expert = (
            sem(n) for n in ("r_const", "r_exp", "r_count", "r_prefix", "r_hot", "r_hot_used",
                             "r_code", "r_rows", "r_expert"))
        r_shift, r_combine, r_cT_psum, r_cT, r_b2, r_b2_in = (sem(n) for n in (
            "r_shift", "r_combine", "r_cT_psum", "r_cT", "r_b2", "r_b2_in"))
        m_rows = [sem(f"m_rows{u}") for u in range(U)]
        m_out = [sem(f"m_out{u}") for u in range(U)]
        m_src = sem("m_src")
        m_xT_psum, m_xT, m_hid_psum, m_hid, m_hid16, m_y_psum, m_y = (sem(n) for n in (
            "m_xT_psum", "m_xT", "m_hid_psum", "m_hid", "m_hid16", "m_y_psum", "m_y"))
        z_in = [sem("z_in0"), sem("z_in1")]
        z_sum, z_out = sem("z_sum"), sem("z_out")

        def wait_alone(eng, s, n):
            eng.wait_ge(s, n)
            eng.sem_inc(waited_alone, 1)

        def stage_end(eng, n):
            eng.drain().then_inc(stage_done, 1)
            wait_alone(eng, stage_done, 5 * n)

        END_SETUP, END_1, END_2, END_3, END_4, END_5 = 1, 1 + B, 2 + B, 3 + B, 4 + B, 5 + B

        RING_STEPS = (("pT", 1), ("att", 2), ("nT", 2), ("pre", 2), ("ff", 2), ("n4T", 2), ("logits", 1))
        RING_BATCH = GB * sum(size for _, size in RING_STEPS)

        def ring_use(b, g, what, half=0):
            use = RING_BATCH * b
            for name, size in RING_STEPS:
                if name == what:
                    return use + g * size + half
                use += GB * size

        def ring_bank(*use):
            return bank(8 - RING + ring_use(*use) % RING)

        def ring_wait(eng, *use):
            n = ring_use(*use)
            eng.wait_ge(ring_full[n % RING], n // RING + 1)

        def ring_free(*use):
            return ring_read[ring_use(*use) % RING]

        def cols(ap, n):
            return ap.unsqueeze(len(ap.shape)).to_broadcast(list(ap.shape) + [n])

        def rows4(ap):
            return ap.unsqueeze(1).to_broadcast([P, G, ap.shape[-1]])

        block = stack.enter_context(nc.Block())

        @block.sync
        def _(sp):
            def vec(dst, src, s=in_vec):
                sp.dma_start(dst, src.partition_broadcast(P)).then_inc(s, 16)

            def mat(dst, src):
                sp.dma_start(dst, src.rearrange("(c p) n -> p c n", p=P)).then_inc(in_w, 16)

            sp.dma_start(ctx_s[:], ctx_in.rearrange("b c d -> c b d")).then_inc(in_w, 16)
            for name, src in (("W", W), ("Wq1", Wq1), ("Wk1", Wk1), ("Wq2", Wq2), ("Wv1", Wv1),
                              ("Wk2", Wk2), ("Wv2", Wv2)):
                mat(raw[name], src)
            sp.dma_start(bias_rows[0:E * HC, :], e1b.rearrange("e (m p) -> (e m) p", p=P)).then_inc(in_w, 16)
            sp.dma_start(bias_rows[E * HC:E * HC + DC, :], f1b.rearrange("(c p) -> c p", p=P)).then_inc(in_w, 16)
            vec(Wb_s[:], Wb)
            vec(graw[:, 0:2], g_xattn)
            vec(graw[:, 2:4], g_ffn)
            sp.dma_start(w1_s, w1.rearrange("(c p) n -> p c n", p=P)).then_inc(in_x, 16)
            sp.dma_start(w2_s, w2.rearrange("(c p) n -> p c n", p=P)).then_inc(in_x, 16)
            sp.dma_start(res[:], x_tiles).then_inc(in_x, 16)
            for dst, src in ((F1_s, F1), (F2_s, F2), (Wg_s, Wg)):
                sp.dma_start(dst[:], src.rearrange("(c p) n -> p c n", p=P)).then_inc(in_late, 16)
            sp.dma_start(e2b_s[:], e2b).then_inc(in_late, 16)
            for dst, src in ((f2b_s, f2b), (gamma_s, gamma), (beta_s, beta), (bg_s, bg)):
                vec(dst[:], src, in_late)
            stage_end(sp, END_SETUP)
            vec(ln1_g_s[:], ln1_g, in_vec)
            vec(ln1_b_s[:], ln1_b, in_vec)
            vec(b2_s[:], b2, in_vec)
            with sp.Fori(0, B) as b:
                stage_end(sp, END_SETUP + 1 + b)
            vec(ln2_g_s, ln2_g, in_vec2)
            vec(ln2_b_s, ln2_b, in_vec2)
            vec(b1_s, b1, in_vec2)

            def load_block(e, k):
                s = k % 2
                if k < EBLK // 2:
                    sp.dma_start(stage_in[:, s, :], E1[e, k * P:(k + 1) * P, :]).then_inc(block_in[s], 16)
                else:
                    f0 = (k - EBLK // 2) * (HC // 2) * P
                    sp.dma_start(stage_in[:, s, :].rearrange("p (m d) -> p m d", m=HC // 2),
                                 E2[e, f0:f0 + HC // 2 * P, :].rearrange("(m p) d -> p m d", p=P)
                                 ).then_inc(block_in[s], 16)

            load_block(0, 0)
            load_block(0, 1)
            for k in range(2, EBLK):
                sp.wait_ge(block_split, k - 1)
                load_block(0, k)
            with sp.Fori(1, NT // EBLK) as e:
                for k in range(EBLK):
                    wait_alone(sp, block_split, EBLK * e + k - 1)
                    load_block(e, k)
            stage_end(sp, END_2)
            for k in range(EBLK):
                sp.wait_ge(block_split, EBLK * (EARLY - 1) + k - 1)
                load_block(EARLY - 1, k)
            for b in range(B):
                for g in range(GB):
                    sp.wait_ge(d_lo, GB * b + g + 1)
                    sp.dma_start(split_rows[(TB * b + G * g) * P:(TB * b + G * (g + 1)) * P, :].rearrange(
                        "(j p) n -> p j n", p=P), split3[:, g, :, :]).then_inc(d_stored, 16)
            sp.wait_ge(d_stored, 16 * GB * B)
            stage_end(sp, END_3)
            with sp.Fori(EARLY, E) as e:
                for k in range(EBLK):
                    wait_alone(sp, block_split, EBLK * e + k - 1)
                    load_block(e, k)
            stage_end(sp, END_4)
            stage_end(sp, END_5)
            for g in range(2):
                sp.dma_start(both[:, g, :, :, :].rearrange("p j k d -> p j (k d)"),
                             choice_rows[g * G * P * K:(g + 1) * G * P * K, :].rearrange(
                                 "(j p k) d -> p j (k d)", p=P, k=K)).then_inc(z_in[g], 16)
            for g in range(2, NT // G):
                sp.wait_ge(z_sum, g - 1)
                sp.dma_start(both[:, g % 2, :, :, :].rearrange("p j k d -> p j (k d)"),
                             choice_rows[g * G * P * K:(g + 1) * G * P * K, :].rearrange(
                                 "(j p k) d -> p j (k d)", p=P, k=K)).then_inc(z_in[g % 2], 16)
            for g in range(NT // G):
                sp.wait_ge(z_sum, g + 1)
                sp.dma_start(out_tiles[:, g * G:(g + 1) * G, :], res[:, g * G:(g + 1) * G, :]).then_inc(z_out, 16)
            sp.wait_ge(z_out, 16 * (NT // G))

        @block.gpsimd
        def _(pool):
            pool.memset(ident[:], 0.0)
            pool.memset(ident16[:], 0.0)
            pool.memset(causal[:], 0.0)
            pool.memset(minus_half[:], -0.5)
            pool.memset(zero_col[:], 0.0)
            pool.memset(ones[:], 1.0)
            pool.drain()
            pool.affine_select(out=ident[:], in_=ident[:], compare_op=ALU.not_equal, fill=1.0,
                               base=0, pattern=[[-1, P]], channel_multiplier=1)
            pool.affine_select(out=ident16[:], in_=ident16[:], compare_op=ALU.not_equal, fill=1.0,
                               base=0, pattern=[[-1, P]], channel_multiplier=1)
            pool.affine_select(out=causal[:], in_=causal[:], compare_op=ALU.is_ge, fill=MASKED,
                               base=0, pattern=[[-1, P]], channel_multiplier=1)
            pool.drain().then_inc(const_made, 1)

            def rsqrt(dst, var, a, c, half, done):
                pool.tensor_scalar(dst, var, a, c, ALU.mult, ALU.add)
                pool.drain()
                pool.tensor_tensor(dst, dst, half, ALU.pow).then_inc(done, 1)

            def split_block(e, k):
                hi, lo = block_parts(e, k)
                pool.wait_ge(block_high, EBLK * e + k + 1)
                pool.tensor_tensor(lo, stage_in[:, k % 2, :], hi, ALU.subtract).then_inc(block_split, 1)

            stage_end(pool, END_SETUP)
            with pool.Fori(0, B) as b:
                for k in range(2 * GB):
                    wait_alone(pool, a_moments, 2 * GB * b + k + 1)
                    if k < GB:
                        rsqrt(rstd[:, k % 2, :], moments[:, k % 2, :, 1], 1.0, LN_EPS, minus_half[:], a_rstd)
                    else:
                        rsqrt(rstd[:, k % 2, :], moments[:, k % 2, :, 1], 1.0 + LN_EPS, LN_EPS ** 2,
                              minus_half[:], a_rstd)
                stage_end(pool, END_SETUP + 1 + b)

            def hidden_rstd(t, u):
                wait_alone(pool, f_sq, t + 1)
                rsqrt(rstd2[:, u:u + 1], ysq[:, u:u + 1], 1.0 / H, LN_EPS, minus_half[:, 0:1], f_rstd)

            def stage2_tile(t, u, following, e, k):
                wait_alone(pool, f_scaled, t + 1)
                pool.tensor_scalar(q2[:, u, :], v2[:, u, :], -MAGIC, 1.0, ALU.add, ALU.mult).then_inc(f_q, 1)
                if following:
                    hidden_rstd(t + 2, u)
                split_block(e, k)

            hidden_rstd(0, 0)
            hidden_rstd(1, 1)
            with pool.Fori(0, NT // EBLK - 1) as e:
                for k in range(EBLK):
                    stage2_tile(EBLK * e + k, k % 2, True, e, k)
            for k in range(EBLK):
                t = NT - EBLK + k
                stage2_tile(t, k % 2, t + 2 < NT, NT // EBLK - 1, k)
            stage_end(pool, END_2)

            def c_rsqrt(b, g):
                pool.wait_ge(c_moments, GB * b + g + 1)
                rsqrt(rstd[:, g, :], moments[:, g, :, 1], 1.0, LN_EPS, minus_half[:], c_rstd)

            def d_rsqrt(b, g, n):
                pool.wait_ge(d_moments[g], 4 * b + n + 1)
                rsqrt(rstd[:, GB + g, :], moments[:, GB + g, :, 1], 1.0, L1_EPS if n < 3 else LN_EPS,
                      minus_half[:], d_rstd[g])

            def add_bias(b, g):
                pool.wait_ge(d_nT, GB * b + g + 1)
                a = acc[:, b, g, :, :]
                pool.tensor_tensor(a, a, rows4(f2b_s[:]), ALU.add).then_inc(d_bias, 1)

            for b in range(B + 1):
                if b < B:
                    for g in range(GB):
                        c_rsqrt(b, g)
                if b == 0:
                    for k in range(EBLK):
                        split_block(EARLY - 1, k)
                else:
                    for n in range(2):
                        for g in range(GB):
                            d_rsqrt(b - 1, g, n)
                    for g in range(GB):
                        add_bias(b - 1, g)
                    for n in range(2, 4):
                        for g in range(GB):
                            d_rsqrt(b - 1, g, n)
            stage_end(pool, END_3)

            pool.memset(strictly_lower[:], 1.0)
            pool.memset(ones5[:], 1.0)
            pool.iota(iota_e[:], pattern=[[1, E]], base=0, channel_multiplier=0,
                      allow_small_or_imprecise_dtypes=True)
            pool.iota(iota_p[:], pattern=[[1, P]], base=0, channel_multiplier=0,
                      allow_small_or_imprecise_dtypes=True)
            pool.iota(iota_j[:], pattern=[[1, TILES]], base=0, channel_multiplier=0,
                      allow_small_or_imprecise_dtypes=True)
            pool.iota(token_code[:], pattern=[[K * P, NT], [1, K]], base=1, channel_multiplier=K,
                      allow_small_or_imprecise_dtypes=True)
            pool.iota(pad_row[:], pattern=[[0, 1]], base=SLOTS + 1, channel_multiplier=1,
                      allow_small_or_imprecise_dtypes=True)
            pool.drain()
            pool.affine_select(out=strictly_lower[:], in_=strictly_lower[:], compare_op=ALU.is_gt, fill=0.0,
                               base=0, pattern=[[1, P]], channel_multiplier=-1)
            pool.drain().then_inc(r_const, 1)
            with pool.Fori(EARLY, E) as e:
                for k in range(EBLK):
                    split_block(e, k)
            stage_end(pool, END_4)

            def gather(j, u):
                wait_alone(pool, m_src, j + 1)
                pool.indirect_dma_start(
                    out=rows_in[:, u, :], out_offset=None, in_=split_rows,
                    in_offset=bass.IndirectOffsetOnAxis(ap=src_now[:, u:u + 1], axis=0)).then_inc(m_rows[u], 16)

            def scatter(j, u, before):
                wait_alone(pool, m_y, j + 1)
                if before is not None:
                    wait_alone(pool, m_out[(u - 1) % U], before)
                pool.indirect_dma_start(
                    out=choice_rows, out_offset=bass.IndirectOffsetOnAxis(ap=dst_now[:, u:u + 1], axis=0),
                    in_=rows_out[:, u, :], in_offset=None).then_inc(m_out[u], 16)

            for u in range(U):
                gather(u, u)
            gather(U, 0)
            scatter(0, 0, None)
            with pool.Fori(0, TILES // U - 2) as i:
                for k in range(1, U + 1):
                    gather(U * (i + 1) + k, k % U)
                    scatter(U * i + k, k % U, 16 * (i + 1))
            for j in range(TILES - 2 * U + 1, TILES):
                if j + U < TILES:
                    gather(j + U, j % U)
                scatter(j, j % U, 16 * ((j - 1) // U + 1))
            for u in range(U):
                pool.wait_ge(m_out[u], 16 * (TILES // U))
            stage_end(pool, END_5)

        @block.scalar
        def _(act):
            def high_block(e, k):
                act.wait_ge(block_in[k % 2], 16 * ((EBLK // 2) * e + k // 2 + 1))
                act.activation(block_parts(e, k)[0], stage_in[:, k % 2, :], ACT.Copy).then_inc(block_high, 1)

            act.wait_ge(in_vec, 48)
            act.activation(gates[:], graw[:], ACT.Tanh).then_inc(gates_made, 1)
            stage_end(act, END_SETUP)
            with act.Fori(0, B) as b:
                for g in range(GB):
                    act.wait_ge(a_hT_psum, GB * b + g + 1)
                    for c in range(DC):
                        last = act.activation(hT[:, g, c, :], bank(DC * g + c), ACT.Copy)
                    last.then_inc(a_hT, 1)
                for g in range(GB):
                    act.wait_ge(a_shifted, GB * b + g + 1)
                    act.activation(probs[:, g, :, :], shifted[:, g, :, :], ACT.Exp).then_inc(a_probs, 1)
                for g in range(GB):
                    act.wait_ge(a_pT_psum, GB * b + g + 1)
                    act.activation(probsT[:, g, :], ps[0:C, 6 + g, :], ACT.Copy).then_inc(a_pT, 1)
                for g in range(GB):
                    act.wait_ge(a_qT_psum, GB * b + g + 1)
                    act.activation(q1T[:, bass.ds(GB * b + g, 1), :, :].rearrange("p o c n -> p (o c n)"),
                                   bank16(4 + g), ACT.Copy).then_inc(a_qT, 1)
                stage_end(act, END_SETUP + 1 + b)

            def gelu(t, u):
                act.wait_ge(f_hidden, t + 1)
                act.activation(y2[:, u, :], ps[:, 2 * u:2 * u + 2, :].rearrange("p a n -> p (a n)"),
                               ACT.Gelu, scale=act_scale[:, u:u + 1],
                               accum_out=ysum[:, u:u + 1]).then_inc(f_gelu, 1)

            def square(t, u):
                act.wait_ge(f_mean, t + 1)
                act.activation(square_out[:, u, :], y2[:, u, :], ACT.Square, bias=neg_mean[:, u:u + 1],
                               accum_out=ysq[:, u:u + 1]).then_inc(f_sq, 1)

            def stage2_tile(t, u, ahead, e, k):
                if ahead >= 2:
                    square(t + 2, u)
                act.wait_ge(f_qT_psum, t + 1)
                act.activation(q2T[:, u, :, :].rearrange("p m n -> p (m n)"), bank16(4 + u),
                               ACT.Copy).then_inc(f_qT, 1)
                high_block(e, k)
                if ahead >= 3:
                    gelu(t + 3, 1 - u)

            gelu(0, 0)
            gelu(1, 1)
            square(0, 0)
            square(1, 1)
            act.drain()
            gelu(2, 0)
            with act.Fori(0, NT // EBLK - 1) as e:
                for k in range(EBLK):
                    stage2_tile(EBLK * e + k, k % 2, 3, e, k)
            for k in range(EBLK):
                t = NT - EBLK + k
                stage2_tile(t, k % 2, NT - 1 - t, NT // EBLK - 1, k)
            stage_end(act, END_2)

            def c_copy_nT(b, g):
                act.wait_ge(c_nT_psum, GB * b + g + 1)
                for c in range(DC):
                    last = act.activation(nT[:, c, g * 512:(g + 1) * 512], bank(DC * g + c), ACT.Copy)
                last.then_inc(c_nT, 1)

            def c_copy_qm(b, k):
                o, g = k % DC, k // DC
                act.wait_ge(c_qm_psum, DC * GB * b + k + 1)
                act.activation(QmT[:, o, g * 512:(g + 1) * 512], bank((4 + k) % 5), ACT.Copy,
                               scale=float(S) ** -0.5).then_inc(c_qm, 1)

            def c_copy_vp(b, i):
                act.wait_ge(c_vp_psum, TB * b + i + 1)
                act.activation(VP[:, i, :], bank((8 + i) % 5)[:, 0:DV], ACT.Copy).then_inc(c_vp, 1)

            def c_tile(b, i):
                L = (i + 1) * P
                act.wait_ge(c_max, TB * b + i + 1)
                if i:
                    act.wait_ge(c_pT_psum, TB * b + i)
                act.activation(Pr[:, 0:L], ps[:, 0:2, :].rearrange("p a n -> p (a n)")[:, 0:L], ACT.Exp,
                               bias=negmax[:, i:i + 1], accum_out=rowsum[:, i:i + 1]).then_inc(c_exp, 1)
                act.wait_ge(c_pT_psum, TB * b + i + 1)
                act.activation(PT[:, 0:L], ps[:, 2:4, :].rearrange("p a n -> p (a n)")[:, 0:L],
                               ACT.Copy).then_inc(c_pT, 1)

            def d_exponential(b, g):
                act.wait_ge(d_shift, GB * b + g + 1)
                act.activation(s2raw[:, b, g, :, :], s2raw[:, b, g, :, :], ACT.Exp).then_inc(d_exp, 1)

            def d_copy(b, g, what, dst, n, done, **how):
                for c in range(n):
                    ring_wait(act, b, g, what, c)
                    src = ring_bank(b, g, what, c)
                    bias = {"bias": how["bias"][:, c:c + 1]} if how else {}
                    act.activation(dst(c), src[0:dst(c).shape[0], :], ACT.Identity if how else ACT.Copy, **bias
                                   ).then_inc(ring_free(b, g, what, c), 1)
                act.drain().then_inc(done, 1)

            def d_copy_pT(b, g):
                d_copy(b, g, "pT", lambda c: p2T[:, g, :], 1, d_pT)

            def d_copy_nT(b, g):
                d_copy(b, g, "nT", lambda c: ffT[:, g, c, :], DC, d_nT)

            def d_copy_pre(b, g):
                if b:
                    act.wait_ge(d_stored, 16 * GB * b)
                d_copy(b, g, "pre", lambda c: preT[:, g, c, :], DC, d_pre, bias=f1b_s)

            def d_copy_n4T(b, g):
                d_copy(b, g, "n4T", lambda c: ffT[:, g, c, :], DC, d_n4T)

            def d_relu_norm3(b, g):
                act.wait_ge(d_norm3, GB * b + g + 1)
                act.activation(acc[:, b, g, :, :], acc[:, b, g, :, :], ACT.Relu).then_inc(d_relu, 1)

            def d_high(b, g):
                act.wait_ge(d_n4, GB * b + g + 1)
                act.activation(split3[:, g, :, 0:D], acc[:, b, g, :, :], ACT.Copy).then_inc(d_hi, 1)

            for b in range(B):
                y = b - 1
                if y >= 0:
                    d_exponential(y, 0)
                c_copy_nT(b, 0)
                c_copy_nT(b, 1)
                if y >= 0:
                    d_exponential(y, 1)
                    d_copy_pT(y, 0)
                c_copy_qm(b, 0)
                c_copy_qm(b, 1)
                if y >= 0:
                    d_copy_pT(y, 1)
                c_copy_qm(b, 2)
                c_copy_qm(b, 3)
                for i in range(TB):
                    c_copy_vp(b, i)
                for i in range(TB):
                    if y < 0 and i % 2:
                        high_block(EARLY - 1, i // 2)
                    c_tile(b, i)
                    if y < 0:
                        continue
                    if i < 2:
                        d_copy_nT(y, i)
                    elif i == 2:
                        d_copy_pre(y, 0)
                    elif i == 3:
                        d_copy_pre(y, 1)
                    elif i == 5:
                        d_relu_norm3(y, 0)
                    elif i == 6:
                        d_relu_norm3(y, 1)
                    elif i == 7:
                        d_high(y, 0)
                        d_high(y, 1)
                if y >= 0:
                    d_copy_n4T(y, 0)
                    d_copy_n4T(y, 1)
            for part in (d_exponential, d_copy_pT, d_copy_nT, d_copy_pre, d_relu_norm3, d_high, d_copy_n4T):
                for g in range(GB):
                    part(B - 1, g)
            stage_end(act, END_3)

            act.wait_ge(r_shift, 1)
            act.activation(pe_exp[:], pe_exp[:], ACT.Exp).then_inc(r_exp, 1)
            with act.Fori(EARLY, E) as e:
                for k in range(EBLK):
                    high_block(e, k)
            stage_end(act, END_4)

            def hidden(j, v, e):
                act.wait_ge(m_hid_psum, j + 1)
                for m in range(HC):
                    last = act.activation(hid[:, v, m * P:(m + 1) * P],
                                          bank(2 + 2 * v + m // 4)[:, (m % 4) * P:(m % 4 + 1) * P],
                                          ACT.Gelu_apprx_tanh, bias=expert_b1[:, bass.ds(e * HC + m, 1)])
                last.then_inc(m_hid, 1)

            def expert_of(j):
                return act.value_load(tile_expert[0:1, bass.ds(j, 1)], min_val=0, max_val=E - 1)

            act.wait_ge(r_expert, 1)
            with act.Fori(0, TILES // TURN) as i:
                for q in range(TURN):
                    hidden(TURN * i + q, q % 2, expert_of(TURN * i + q))
            for j in range(TILES // TURN * TURN, TILES):
                hidden(j, j % 2, expert_of(j))
            stage_end(act, END_5)

        @block.vector
        def _(dve):
            def copied(n=1):
                dve.drain().then_inc(su_copied, n)

            def step(n):
                dve.wait_ge(su_psum, n)

            dve.wait_ge(in_x, 48)
            dve.tensor_reduce(w_abs[:, 0:1], w1_s.rearrange("p a b -> p (a b)"), X, ALU.add,
                              apply_absolute_value=True)
            dve.tensor_reduce(w_abs[:, 1:2], w2_s.rearrange("p a b -> p (a b)"), X, ALU.add,
                              apply_absolute_value=True)
            dve.drain().then_inc(su_abs, 1)
            step(1)
            dve.tensor_copy(ctxT[:].rearrange("p c b k -> p (c b k)"), bank(0)[:, 0:DC * B * C])
            for n, name in enumerate(("WT", "Wq1T", "Wk1T", "Wq2T", "Wv1T")):
                step(2 + n)
                dve.tensor_copy(raw[name].rearrange("p c d -> p (c d)"), bank(1 + n))
            step(7)
            dve.tensor_copy(expert_b1[:], bank(6)[:, 0:E * HC])
            dve.tensor_copy(f1b_s[:], bank(6)[:, E * HC:E * HC + DC])
            copied()
            step(8)
            dve.wait_ge(in_vec, 48)
            dve.tensor_tensor(tq[:], ps[0:C, 0, :].rearrange("p (b d) -> p b d", b=B),
                              Wb_s[0:C, :].unsqueeze(1).to_broadcast([C, B, D]), ALU.add)
            step(9)
            dve.tensor_copy(M1[:].rearrange("p c d -> p (c d)"), bank(1))
            step(10)
            dve.tensor_copy(K2T[:].rearrange("p c d -> p (c d)"), bank(2)[:, 0:DC * B * C])
            step(11)
            dve.tensor_copy(V2[:].rearrange("p c d -> p (c d)"), ps[0:C, 3, :])
            copied()
            step(12)
            dve.tensor_copy(tqT[:].rearrange("p b c k -> p (b c k)"), bank(4)[:, 0:DC * B * C])
            step(13)
            dve.tensor_scalar(A2[:].rearrange("p c d -> p (c d)"), bank(5)[:, 0:DC * B * C],
                              float(C) ** -0.5, None, ALU.mult)
            copied()
            step(14)
            for b in range(B):
                dve.tensor_copy(WVA[:, b, :, D:DV],
                                bank(6)[:, 0:DC * B * C].rearrange("p (c b k) -> p c b k", c=DC, b=B)[:, :, b, :])
                dve.tensor_copy(WVA[:, b, :, 0:D], raw["Wv1"])
            step(15)
            dve.tensor_scalar(wscale[:], bank(7)[:, 0:2], 1.0 / (H * D), 1e-5, ALU.mult, ALU.max)
            dve.drain()
            dve.reciprocal(wscale_inv[:], wscale[:])
            dve.tensor_scalar(wscale_127[:], wscale[:], 1.0 / 127.0, None, ALU.mult)
            dve.drain()
            for n, (w_s, t_s) in enumerate(((w1_s, t1_s), (w2_s, t2_s))):
                flat = w_s.rearrange("p a b -> p (a b)")
                dve.tensor_scalar(flat, flat, wscale_inv[:, n:n + 1], MAGIC, ALU.mult, ALU.add)
                dve.drain()
                dve.tensor_scalar(flat, flat, -MAGIC, 1.0, ALU.add, ALU.min)
                dve.drain()
                dve.tensor_scalar(t_s.rearrange("p a b -> p (a b)"), flat, -1.0, None, ALU.max)
                dve.drain().then_inc(su_tern, 1)
            for n in range(DC):
                step(16 + n)
                dve.tensor_copy(T1[:, n, :], bank16(n))
            for n in range(2):
                step(18 + n)
                dve.tensor_copy(T2[:, 4 * n:4 * n + 4, :].rearrange("p m d -> p (m d)"), bank16(2 + n))
            dve.wait_ge(gates_made, 1)
            stage_end(dve, END_SETUP)

            def group_moments(tile_of, k, done):
                for j in range(G):
                    dve.bn_stats(stats[:, j, :], tile_of(j))
                dve.drain()
                for j in range(G):
                    dve.bn_aggr(moments[:, k, j, :], stats[:, j, :])
                dve.drain().then_inc(done, 1)

            def normalise(out_of, tile_of, k):
                for j in range(G):
                    dve.tensor_scalar(out_of(j), tile_of(j), moments[:, k, j, 0:1], rstd[:, k, j:j + 1],
                                      ALU.subtract, ALU.mult)
                dve.drain()

            dve.wait_ge(in_vec, 96)
            with dve.Fori(0, B) as b:
                def res_tile(g):
                    return lambda j: res[:, bass.ds(TB * b + G * g + j, 1), :].rearrange("p o d -> p (o d)")

                def res_group(g):
                    return res[:, bass.ds(TB * b + G * g, G), :]

                for g in range(GB):
                    group_moments(res_tile(g), g, a_moments)
                for g in range(GB):
                    dve.wait_ge(a_rstd, 2 * GB * b + g + 1)
                    normalise(lambda j: h1[:, g, j, :], res_tile(g), g)
                    dve.drain().then_inc(a_h, 1)
                for g in range(GB):
                    dve.wait_ge(a_scores, GB * b + g + 1)
                    sc = bank(4 + g)[:, 0:G * C].rearrange("p (j k) -> p j k", j=G)
                    dve.tensor_reduce(top[:, g, :], sc, X, ALU.max)
                    dve.drain()
                    dve.tensor_tensor(shifted[:, g, :, :], sc, cols(top[:, g, :], C), ALU.subtract
                                      ).then_inc(a_shifted, 1)
                for g in range(GB):
                    dve.wait_ge(a_probs, GB * b + g + 1)
                    dve.tensor_reduce(total[:, g, :], probs[:, g, :, :], X, ALU.add)
                    dve.drain()
                    dve.reciprocal(total[:, g, :], total[:, g, :])
                    dve.drain()
                    dve.wait_ge(a_vec, GB * b + g + 1)
                    for j in range(G):
                        dve.tensor_scalar(h1[:, g, j, :], bank(2 * g + j // 2)[:, (j % 2) * D:(j % 2 + 1) * D],
                                          total[:, g, j:j + 1], 0.0, ALU.mult, ALU.max)
                    dve.drain()
                    dve.scalar_tensor_tensor(res_group(g), h1[:, g, :, :], gates[:, 0:1], res_group(g),
                                             ALU.mult, ALU.add)
                    dve.drain()
                    group_moments(res_tile(g), g, a_moments)
                for g in range(GB):
                    dve.wait_ge(a_rstd, 2 * GB * b + GB + g + 1)
                    normalise(lambda j: u1[:, g, j, :], res_tile(g), g)
                    u = u1[:, g, :, :]
                    dve.tensor_tensor(u, u, rows4(ln1_g_s[:]), ALU.mult)
                    dve.scalar_tensor_tensor(res_group(g), rows4(b2_s[:]), gates[:, 2:3], res_group(g),
                                             ALU.mult, ALU.add)
                    dve.drain()
                    dve.tensor_tensor(u, u, rows4(ln1_b_s[:]), ALU.add)
                    dve.drain()
                    dve.tensor_reduce(top[:, g, :], u, X, ALU.max, apply_absolute_value=True)
                    dve.drain()
                    dve.tensor_scalar(top[:, g, :], top[:, g, :], 1e-5, None, ALU.max)
                    dve.drain()
                    dve.reciprocal(sx1[:, g, :], top[:, g, :])
                    dve.drain()
                    dve.tensor_scalar(sx1[:, g, :], sx1[:, g, :], 127.0, None, ALU.mult)
                    dve.tensor_scalar(scale1[:, bass.ds(TB * b + G * g, G)], top[:, g, :],
                                      wscale_127[:, 0:1], None, ALU.mult)
                    dve.drain()
                    dve.tensor_scalar(inverse1[:, bass.ds(TB * b + G * g, G)], sx1[:, g, :],
                                      wscale_inv[:, 0:1], None, ALU.mult)
                    for j in range(G):
                        dve.tensor_scalar(u1[:, g, j, :], u1[:, g, j, :], sx1[:, g, j:j + 1], MAGIC,
                                          ALU.mult, ALU.add)
                    dve.drain()
                    dve.tensor_scalar(q1[:, g, :, :], u, -MAGIC, None, ALU.add).then_inc(a_q, 1)
                stage_end(dve, END_SETUP + 1 + b)

            dve.wait_ge(in_vec2, 48)

            def make_diag(t, u):
                dve.tensor_scalar(diag[:, u, :], ident[:], inverse1[:, bass.ds(t, 1)], None, ALU.mult)
                dve.tensor_copy(act_scale[:, u:u + 1], scale1[:, bass.ds(t, 1)])
                dve.drain().then_inc(f_diag, 1)

            def finish(t, u):
                dve.wait_ge(f_y, t + 1)
                r = res[:, bass.ds(t, 1), :].rearrange("p o d -> p (o d)")
                dve.scalar_tensor_tensor(r, bank(6 + u)[:, 0:D], outscale[:, u:u + 1], r, ALU.mult, ALU.add)

            def start_row(t, u, ahead):
                dve.wait_ge(f_gelu, t + 1)
                dve.tensor_scalar(neg_mean[:, u:u + 1], ysum[:, u:u + 1], -1.0 / H, None, ALU.mult
                                  ).then_inc(f_mean, 1)
                if ahead >= 2:
                    make_diag(t + 2, u)

            def centre(t, u, reused):
                if reused:
                    dve.wait_ge(f_q, t - 1)
                dve.scalar_tensor_tensor(v2[:, u, :], y2[:, u, :], neg_mean[:, u:u + 1], ln2_g_s,
                                         ALU.add, ALU.mult)

            def hidden_row(t, u, ahead, reused, before):
                if ahead >= 1:
                    start_row(t + 1, 1 - u, ahead - 1)
                v = v2[:, u, :]
                dve.drain()
                dve.wait_ge(f_rstd, t + 1)
                dve.scalar_tensor_tensor(v, v, rstd2[:, u:u + 1], ln2_b_s, ALU.mult, ALU.add)
                if ahead >= 1:
                    centre(t + 1, 1 - u, reused)
                dve.drain()
                dve.tensor_reduce(vmax[:, u:u + 1], v, X, ALU.max, apply_absolute_value=True)
                dve.drain()
                dve.tensor_scalar(vmax[:, u:u + 1], vmax[:, u:u + 1], 1e-5, 1.0 / 127.0, ALU.max, ALU.mult)
                dve.drain()
                dve.reciprocal(sx2[:, u:u + 1], vmax[:, u:u + 1])
                dve.tensor_scalar(outscale[:, u:u + 1], vmax[:, u:u + 1], wscale[:, 1:2], gates[:, 2:3],
                                  ALU.mult, ALU.mult)
                dve.drain()
                dve.tensor_scalar(v, v, sx2[:, u:u + 1], MAGIC, ALU.mult, ALU.add).then_inc(f_scaled, 1)
                if before:
                    finish(t - 1, 1 - u)

            make_diag(0, 0)
            make_diag(1, 1)
            start_row(0, 0, 2)
            dve.drain()
            centre(0, 0, False)
            dve.drain()
            hidden_row(0, 0, 3, False, False)
            with dve.Fori(0, (NT - G) // 2) as i:
                hidden_row(2 * i + 1, 1, 3, True, True)
                hidden_row(2 * i + 2, 0, 3, True, True)
            for t in range(NT - G + 1, NT):
                hidden_row(t, t % 2, NT - 1 - t, True, True)
            finish(NT - 1, 1)
            stage_end(dve, END_2)

            dve.wait_ge(in_late, 16 * 8)

            def c_moments_of(b, g):
                group_moments(lambda j: res[:, TB * b + G * g + j, :], g, c_moments)

            def c_normalise(b, g):
                dve.wait_ge(c_rstd, GB * b + g + 1)
                normalise(lambda j: n3[:, G * g + j, :], lambda j: res[:, TB * b + G * g + j, :], g)
                dve.drain().then_inc(c_n, 1)

            def c_attended(b, i):
                g, j = i // G, i % G
                dve.wait_ge(c_att, TB * b + i + 1)
                dve.reciprocal(rowinv[:, i:i + 1], rowsum[:, i:i + 1])
                dve.drain()
                o = bank(4)
                dve.scalar_tensor_tensor(acc[:, b, g, j, :], o[:, 0:D], rowinv[:, i:i + 1], n3[:, i, :],
                                         ALU.mult, ALU.add)
                dve.tensor_scalar(s2raw[:, b, g, j, :], o[:, D:DV], rowinv[:, i:i + 1], None, ALU.mult
                                  ).then_inc(c_acc, 1)

            def c_tile(b, i):
                L = (i + 1) * P
                dve.wait_ge(c_scores, TB * b + i + 1)
                dve.tensor_reduce(negmax[:, i:i + 1], ps[:, 0:2, :].rearrange("p a n -> p (a n)")[:, 0:L],
                                  X, ALU.max, negate=True).then_inc(c_max, 1)
                if i:
                    c_attended(b, i - 1)

            def d_shift_scores(b, g):
                dve.drain()
                dve.tensor_reduce(top3[:, g, :], s2raw[:, b, g, :, :], X, ALU.max)
                dve.drain()
                dve.tensor_tensor(s2raw[:, b, g, :, :], s2raw[:, b, g, :, :], cols(top3[:, g, :], C),
                                  ALU.subtract).then_inc(d_shift, 1)

            def norm_start(b, g):
                group_moments(lambda j: acc[:, b, g, j, :], GB + g, d_moments[g])
                for j in range(G):
                    a = acc[:, b, g, j, :]
                    dve.scalar_tensor_tensor(a, a, moments[:, GB + g, j, 0:1], gamma_s[:],
                                             ALU.subtract, ALU.mult)

            def norm_end(b, g, n):
                dve.drain()
                dve.wait_ge(d_rstd[g], 4 * b + n + 1)
                for j in range(G):
                    a = acc[:, b, g, j, :]
                    dve.scalar_tensor_tensor(a, a, rstd[:, GB + g, j:j + 1], beta_s[:], ALU.mult, ALU.add)

            def halves(b, g, what):
                for h in range(2):
                    ring_wait(dve, b, g, what, h)
                    yield h, ring_bank(b, g, what, h), ring_free(b, g, what, h)

            def d_attended(b, g):
                dve.wait_ge(d_exp, GB * b + g + 1)
                dve.tensor_reduce(total3[:, g, :], s2raw[:, b, g, :, :], X, ALU.add)
                dve.drain()
                dve.reciprocal(total3[:, g, :], total3[:, g, :])
                dve.drain()
                for h, at, read in halves(b, g, "att"):
                    for j in (2 * h, 2 * h + 1):
                        a = acc[:, b, g, j, :]
                        last = dve.scalar_tensor_tensor(a, at[:, (j % 2) * D:(j % 2 + 1) * D],
                                                        total3[:, g, j:j + 1], a, ALU.mult, ALU.add)
                    last.then_inc(read, 1)
                dve.drain()

            def d_norm1_to_norm2(b, g):
                norm_end(b, g, 0)
                d_attended(b, g)
                norm_start(b, g)

            def d_end_norm2(b, g):
                norm_end(b, g, 1)
                dve.drain().then_inc(d_norm2, 1)

            def d_leaky_relu(b, g):
                dve.wait_ge(d_pre, GB * b + g + 1)
                dve.scalar_tensor_tensor(ffT[:, g, :, :], preT[:, g, :, :], 0.2, preT[:, g, :, :],
                                         ALU.mult, ALU.max).then_inc(d_hT, 1)

            def d_fed_forward(b, g):
                dve.wait_ge(d_bias, GB * b + g + 1)
                for h, at, read in halves(b, g, "ff"):
                    a = acc[:, b, g, 2 * h:2 * h + 2, :].rearrange("p j d -> p (j d)")
                    dve.tensor_tensor(a, at, a, ALU.add).then_inc(read, 1)
                dve.drain()
                norm_start(b, g)

            def d_end_norm3(b, g):
                norm_end(b, g, 2)
                dve.drain().then_inc(d_norm3, 1)

            def d_to_stream(b, g):
                r = res[:, TB * b + G * g:TB * b + G * (g + 1), :]
                dve.wait_ge(d_relu, GB * b + g + 1)
                dve.scalar_tensor_tensor(r, acc[:, b, g, :, :], gates[:, 1:2], r, ALU.mult, ALU.add)
                dve.drain()
                group_moments(lambda j: res[:, TB * b + G * g + j, :], GB + g, d_moments[g])

            def d_norm4(b, g):
                dve.wait_ge(d_rstd[g], 4 * b + 4)
                normalise(lambda j: acc[:, b, g, j, :], lambda j: res[:, TB * b + G * g + j, :], GB + g)
                dve.drain().then_inc(d_n4, 1)

            def d_low(b, g):
                dve.wait_ge(d_hi, GB * b + g + 1)
                dve.tensor_tensor(split3[:, g, :, D:2 * D], acc[:, b, g, :, :], split3[:, g, :, 0:D],
                                  ALU.subtract).then_inc(d_lo, 1)

            def d_logits(b, g):
                ring_wait(dve, b, g, "logits")
                t = TB * b + G * g
                dve.tensor_tensor(logits[:, t:t + G, :],
                                  ring_bank(b, g, "logits")[:, 0:G * E].rearrange("p (j e) -> p j e", j=G),
                                  rows4(bg_s[:]), ALU.add).then_inc(ring_free(b, g, "logits"), 1)

            for b in range(B):
                y = b - 1
                c_moments_of(b, 0)
                c_moments_of(b, 1)
                if y >= 0:
                    d_shift_scores(y, 0)
                c_normalise(b, 0)
                c_normalise(b, 1)
                if y >= 0:
                    d_shift_scores(y, 1)
                    norm_start(y, 0)
                    norm_start(y, 1)
                    d_norm1_to_norm2(y, 0)
                    d_norm1_to_norm2(y, 1)
                for i in range(TB):
                    c_tile(b, i)
                    if y < 0:
                        continue
                    if i < 2:
                        d_end_norm2(y, i)
                    elif i == 3:
                        d_leaky_relu(y, 0)
                    elif i == 4:
                        d_leaky_relu(y, 1)
                        d_fed_forward(y, 0)
                    elif i == 5:
                        d_fed_forward(y, 1)
                        d_end_norm3(y, 0)
                    elif i == 6:
                        d_end_norm3(y, 1)
                        d_to_stream(y, 0)
                        d_to_stream(y, 1)
                    elif i == 7:
                        d_norm4(y, 0)
                        d_norm4(y, 1)
                c_attended(b, TB - 1)
                if y >= 0:
                    d_low(y, 0)
                    d_low(y, 1)
                    d_logits(y, 0)
                    d_logits(y, 1)
            for g in range(GB):
                d_shift_scores(B - 1, g)
            for g in range(GB):
                norm_start(B - 1, g)
            for part in (d_norm1_to_norm2, d_end_norm2, d_leaky_relu, d_fed_forward, d_end_norm3, d_to_stream, d_norm4,
                         d_low, d_logits):
                for g in range(GB):
                    part(B - 1, g)
            stage_end(dve, END_3)

            dve.tensor_reduce(gsum[:], logits[:], X, ALU.max)
            dve.drain()
            dve.tensor_tensor(pe_exp[:], logits[:], cols(gsum[:], E), ALU.subtract).then_inc(r_shift, 1)
            dve.wait_ge(r_exp, 1)
            dve.tensor_reduce(gsum[:], pe_exp[:], X, ALU.add)
            for t in range(NT):
                dve.max(gtop[:, t, :], pe_exp[:, t, :])
            dve.drain()
            for t in range(NT):
                dve.max_index(gidx[:, t, :], gtop[:, t, :], pe_exp[:, t, :])
            dve.tensor_reduce(denom[:], gtop[:, :, 0:K], X, ALU.add)
            dve.drain()
            dve.scalar_tensor_tensor(denom[:], gsum[:], 1e-8, denom[:], ALU.mult, ALU.add)
            dve.tensor_copy(gidx_f[:], gidx[:, :, 0:K])
            dve.drain()
            dve.reciprocal(denom[:], denom[:])
            dve.wait_ge(r_const, 1)
            for k in range(K):
                dve.tensor_tensor(onehot[:, :, k, :], iota_e[:].unsqueeze(1).to_broadcast([P, NT, E]),
                                  cols(gidx_f[:, :, k], E), ALU.is_equal)
            dve.drain()
            dve.tensor_tensor(count[:], onehot[:, :, 0, :], onehot[:, :, 1, :], ALU.add).then_inc(r_count, 1)
            dve.tensor_tensor(weight[:], gtop[:, :, 0:K], cols(denom[:], K), ALU.mult)
            dve.drain()
            dve.tensor_scalar(weight[:], weight[:], gates[:, 3:4], None, ALU.mult)
            dve.drain()
            dve.tensor_tensor(picked[:], onehot[:], cols(weight[:], E), ALU.mult)
            dve.drain()
            dve.tensor_tensor(combine[:], picked[:, :, 0, :], picked[:, :, 1, :], ALU.add).then_inc(r_combine, 1)
            dve.wait_ge(r_prefix, 1)
            dve.tensor_copy(tiles_upto[:, 0, :, :].rearrange("p t e -> p (t e)"), bank(1)[:, 0:NT * E])
            dve.drain()
            a, shift = 0, 1
            while shift < NT:
                dve.tensor_copy(tiles_upto[:, 1 - a, 0:shift, :], tiles_upto[:, a, 0:shift, :])
                dve.tensor_tensor(tiles_upto[:, 1 - a, shift:NT, :], tiles_upto[:, a, shift:NT, :],
                                  tiles_upto[:, a, 0:NT - shift, :], ALU.add)
                dve.drain()
                a, shift = 1 - a, 2 * shift
            upto = tiles_upto[:, a, :, :]
            dve.tensor_scalar(etiles[:], upto[:, NT - 1, :], 1.0 / P, (P - 1.0) / P - 0.5 + 0.5 / P,
                              ALU.mult, ALU.add)
            dve.drain()
            dve.tensor_scalar(etiles[:], etiles[:], MAGIC, -MAGIC, ALU.add, ALU.add)
            dve.drain()
            dve.tensor_copy(eend[:, 0, :], etiles[:])
            dve.drain()
            a2, shift = 0, 1
            while shift < E:
                dve.tensor_copy(eend[:, 1 - a2, 0:shift], eend[:, a2, 0:shift])
                dve.tensor_tensor(eend[:, 1 - a2, shift:E], eend[:, a2, shift:E], eend[:, a2, 0:E - shift], ALU.add)
                dve.drain()
                a2, shift = 1 - a2, 2 * shift
            ends = eend[:, a2, :]
            dve.tensor_tensor(ended[:], cols(iota_j[:], E), ends.unsqueeze(1).to_broadcast([P, TILES, E]),
                              ALU.is_ge)
            dve.tensor_tensor(etiles[:], ends, etiles[:], ALU.subtract)
            dve.drain()
            dve.tensor_reduce(tile_expert_f[:], ended[:], X, ALU.add)
            dve.tensor_tensor(prefix[:], upto, count_total(ps, NT, E), ALU.subtract)
            dve.drain()
            dve.tensor_scalar(tile_expert[:], tile_expert_f[:], E - 1.0, None, ALU.min)
            dve.tensor_tensor(prefix[:], bank(0)[:, 0:NT * E].rearrange("p (t e) -> p t e", t=NT), prefix[:],
                              ALU.add)
            dve.drain().then_inc(r_expert, 1)
            dve.scalar_tensor_tensor(prefix[:], etiles[:].unsqueeze(1).to_broadcast([P, NT, E]), float(P),
                                     prefix[:], ALU.mult, ALU.add)
            dve.drain()
            dve.tensor_tensor(picked[:], onehot[:], prefix[:].unsqueeze(2).to_broadcast([P, NT, K, E]), ALU.mult)
            dve.drain()
            dve.tensor_reduce(place[:], picked[:], X, ALU.add)
            dve.drain()
            dve.tensor_scalar(place_hi[:], place[:], 1.0 / P, -0.5 + 0.5 / P, ALU.mult, ALU.add)
            dve.drain()
            dve.tensor_scalar(place_hi[:], place_hi[:], MAGIC, -MAGIC, ALU.add, ALU.add)
            dve.drain()
            dve.scalar_tensor_tensor(place_lo[:], place_hi[:], -float(P), place[:], ALU.mult, ALU.add)
            hi_flat = place_hi[:].rearrange("p t k -> p (t k)")
            dve.tensor_tensor(hot_hi[:], iota_j[:].unsqueeze(1).to_broadcast([P, NTK, TILES]),
                              cols(hi_flat, TILES), ALU.is_equal)
            dve.drain()
            dve.tensor_tensor(hot_hi[:], hot_hi[:], cols(token_code[:].rearrange("p t k -> p (t k)"), TILES),
                              ALU.mult)
            dve.drain()
            lo_flat = place_lo[:].rearrange("p t k -> p (t k)")
            for q in range(NTK // 8):
                if q >= 2:
                    dve.wait_ge(r_hot_used, q - 1)
                dve.tensor_tensor(hot_lo[:, q % 2, :, :], iota_p[:].unsqueeze(1).to_broadcast([P, 8, P]),
                                  cols(lo_flat[:, 8 * q:8 * q + 8], P), ALU.is_equal).then_inc(r_hot, 1)
            dve.wait_ge(r_code, 1)
            dve.tensor_copy(code[:], bank(2)[:, 0:TILES])
            dve.drain()
            dve.tensor_scalar(dst_f[:], code[:], 0.0, pad_row[:, 0:1], ALU.is_equal, ALU.mult)
            dve.tensor_scalar(src_f[:], code[:], 0.5, -0.75, ALU.mult, ALU.add)
            dve.drain()
            dve.tensor_tensor(dst_f[:], dst_f[:], code[:], ALU.add)
            dve.tensor_scalar(src_f[:], src_f[:], MAGIC, -MAGIC, ALU.add, ALU.add)
            dve.drain()
            dve.tensor_scalar(dst_row[:], dst_f[:], -1.0, None, ALU.add)
            dve.tensor_scalar(src_row[:], src_f[:], 0.0, None, ALU.max)
            dve.drain()
            dve.wait_ge(r_cT_psum, 1)
            for t in range(NT):
                dve.tensor_copy(combineT[:, t, :], ps[0:E, 4 + t // 4, (t % 4) * P:(t % 4 + 1) * P])
            dve.drain().then_inc(r_cT, 1)
            for n in range(NT // 4):
                dve.wait_ge(r_b2, n + 1)
                for h in range(2):
                    t = 4 * n + 2 * h
                    r = res[:, t:t + 2, :].rearrange("p j d -> p (j d)")
                    last = dve.tensor_tensor(r, bank(2 * (n % 2) + h), r, ALU.add)
                last.then_inc(r_b2_in, 1)
            stage_end(dve, END_4)

            def take_xT(j):
                dve.wait_ge(m_xT_psum, j[0] + 1)
                dve.tensor_copy(xT[:, j[1] % U, :, :, :].rearrange("p a c n -> p (a c n)"),
                                bank16(6 * (j[1] % 2))[:, 0:4 * P]).then_inc(m_xT, 1)

            def name_rows(j):
                dve.tensor_copy(src_now[:, j[1] % U:j[1] % U + 1], src_row[:, bass.ds(j[0], 1)]).then_inc(m_src, 1)

            def split_hidden(j):
                v = j[1] % 2
                dve.wait_ge(m_hid, j[0] + 1)
                hi = hid16[:, v, 0, :, :].rearrange("p m n -> p (m n)")
                lo = hid16[:, v, 1, :, :].rearrange("p m n -> p (m n)")
                dve.tensor_copy(hi, hid[:, v, :])
                dve.drain()
                dve.tensor_tensor(lo, hid[:, v, :], hi, ALU.subtract).then_inc(m_hid16, 1)

            def take_y(j, stored):
                u = j[1] % U
                dve.wait_ge(m_y_psum, j[0] + 1)
                if stored is not None:
                    dve.wait_ge(m_out[u], 16 * stored)
                dve.tensor_copy(dst_now[:, u:u + 1], dst_row[:, bass.ds(j[0], 1)])
                dve.tensor_copy(rows_out[:, u, :], bank(1)[:, 0:D]).then_inc(m_y, 1)

            for j in range(U):
                name_rows((j, j))
            take_xT((0, 0))
            take_xT((1, 1))
            for j in range(TURN):
                if j:
                    take_y((j - 1, j - 1), (j - 1) // U or None)
                take_xT((j + 2, j + 2))
                name_rows((j + U, j + U))
                split_hidden((j, j))
            with dve.Fori(1, TILES // TURN - 1) as i:
                for q in range(TURN):
                    j = TURN * i + q
                    take_y((j - 1, q + TURN - 1), 2 * i + (q - 1) // U)
                    take_xT((j + 2, q + 2))
                    name_rows((j + U, q + U))
                    split_hidden((j, q))
            for j in range((TILES // TURN - 1) * TURN, TILES):
                take_y((j - 1, j - 1), (j - 1) // U)
                if j + 2 < TILES:
                    take_xT((j + 2, j + 2))
                if j + U < TILES:
                    name_rows((j + U, j + U))
                split_hidden((j, j))
            take_y((TILES - 1, TILES - 1), (TILES - 1) // U)
            stage_end(dve, END_5)

            for g in range(NT // G):
                dve.wait_ge(z_in[g % 2], 16 * (g // 2 + 1))
                for k in range(K):
                    for j in range(G):
                        t = G * g + j
                        dve.scalar_tensor_tensor(res[:, t, :], both[:, g % 2, j, k, :], weight[:, t, k:k + 1],
                                                 res[:, t, :], ALU.mult, ALU.add)
                    dve.drain()
                dve.drain().then_inc(z_sum, 1)

        @block.tensor
        def _(pe):
            def done(ins):
                ins.then_inc(su_psum, 1)

            pe.wait_ge(in_w, 16 * 10)
            pe.wait_ge(const_made, 1)
            for c in range(DC):
                for b in range(B):
                    at = (c * B + b) * C
                    last = pe.transpose(bank(0)[:, at:at + C], ctx_s[:, b, c * P:(c + 1) * P], ident[0:C, 0:C])
            done(last)
            for n, name in enumerate(("W", "Wq1", "Wk1", "Wq2", "Wv1")):
                for c in range(DC):
                    for c2 in range(DC):
                        last = pe.transpose(bank(1 + n)[:, c2 * D + c * P:c2 * D + (c + 1) * P],
                                            raw[name][:, c, c2 * P:(c2 + 1) * P], ident[:])
                done(last)
            n_rows = E * HC + DC
            done(pe.transpose(bank(6)[:, 0:n_rows], bias_rows[:], ident[0:n_rows, 0:n_rows]))
            pe.wait_ge(su_copied, 1)

            def product(dst, lhsT, rhs, n=DC):
                for c in range(n):
                    last = pe.matmul(dst, lhsT(c), rhs(c), start=(c == 0), stop=(c == n - 1))
                return last

            for b in range(B):
                last = product(ps[0:C, 0, b * D:(b + 1) * D], lambda c: ctxT[:, c, b, :], lambda c: raw["WT"][:, c, :])
            done(last)
            for o in range(DC):
                last = product(bank(1)[:, o * D:(o + 1) * D], lambda c: raw["Wq1T"][:, c, o * P:(o + 1) * P],
                               lambda c: raw["Wk1T"][:, c, :])
            done(last)
            for o in range(DC):
                last = product(bank(2)[:, o * B * C:(o + 1) * B * C], lambda c: raw["Wk2"][:, c, o * P:(o + 1) * P],
                               lambda c: ctxT[:, c, :, :].rearrange("p b k -> p (b k)"))
            done(last)
            for b in range(B):
                last = product(ps[0:C, 3, b * D:(b + 1) * D], lambda c: ctxT[:, c, b, :], lambda c: raw["Wv2"][:, c, :])
            done(last)
            pe.wait_ge(su_copied, 2)
            for b in range(B):
                for c in range(DC):
                    at = (b * DC + c) * C
                    last = pe.transpose(bank(4)[:, at:at + C], tq[:, b, c * P:(c + 1) * P], ident[0:C, 0:C])
            done(last)
            for o in range(DC):
                last = product(bank(5)[:, o * B * C:(o + 1) * B * C], lambda c: raw["Wq2T"][:, c, o * P:(o + 1) * P],
                               lambda c: K2T[:, c, :])
            done(last)
            pe.wait_ge(su_copied, 3)
            for o in range(DC):
                last = product(bank(6)[:, o * B * C:(o + 1) * B * C], lambda c: raw["Wv1T"][:, c, o * P:(o + 1) * P],
                               lambda c: A2[:, c, :])
            done(last)
            pe.wait_ge(su_abs, 1)
            done(pe.matmul(bank(7)[:, 0:2], ones[:], w_abs[:], start=True, stop=True))
            pe.wait_ge(su_tern, 1)
            for c in range(DC):
                for m in range(HC):
                    last = pe.transpose(bank16(c)[:, m * P:(m + 1) * P], t1_s[:, m, c * P:(c + 1) * P], ident16[:])
                done(last)
            pe.wait_ge(su_tern, 2)
            for n in range(2):
                for m in range(4):
                    for c in range(DC):
                        last = pe.transpose(bank16(2 + n)[:, m * D + c * P:m * D + (c + 1) * P],
                                            t2_s[:, c, (4 * n + m) * P:(4 * n + m + 1) * P], ident16[:])
                done(last)
            stage_end(pe, END_SETUP)

            def transpose_group(bank_of, tile_of):
                for j in range(G):
                    for c in range(DC):
                        last = pe.transpose(bank(bank_of(c))[:, j * P:(j + 1) * P],
                                            tile_of(j)[:, c * P:(c + 1) * P], ident[:])
                return last

            with pe.Fori(0, B) as b:
                for g in range(GB):
                    pe.wait_ge(a_h, GB * b + g + 1)
                    transpose_group(lambda c: DC * g + c, lambda j: h1[:, g, j, :]).then_inc(a_hT_psum, 1)
                for g in range(GB):
                    pe.wait_ge(a_hT, GB * b + g + 1)
                    for j in range(G):
                        for c in range(DC):
                            last = pe.matmul(bank(4 + g)[:, j * C:(j + 1) * C], hT[:, g, c, j * P:(j + 1) * P],
                                             tqT[:, bass.ds(b, 1), c, :].rearrange("p o k -> p (o k)"),
                                             start=(c == 0), stop=(c == DC - 1))
                    last.then_inc(a_scores, 1)
                for g in range(GB):
                    pe.wait_ge(a_probs, GB * b + g + 1)
                    for j in range(G):
                        last = pe.transpose(ps[0:C, 6 + g, j * P:(j + 1) * P], probs[:, g, j, :], ident[:])
                    last.then_inc(a_pT_psum, 1)
                for g in range(GB):
                    pe.wait_ge(a_pT, GB * b + g + 1)
                    for j in range(G):
                        last = pe.matmul(bank(2 * g + j // 2)[:, (j % 2) * D:(j % 2 + 1) * D],
                                         probsT[:, g, j * P:(j + 1) * P],
                                         tq[:, bass.ds(b, 1), :].rearrange("p o d -> p (o d)"),
                                         start=True, stop=True)
                    last.then_inc(a_vec, 1)
                for g in range(GB):
                    pe.wait_ge(a_q, GB * b + g + 1)
                    for c in range(DC):
                        for j in range(G):
                            last = pe.transpose(bank16(4 + g)[:, (c * G + j) * P:(c * G + j + 1) * P],
                                                q1[:, g, j, c * P:(c + 1) * P], ident16[:])
                    last.then_inc(a_qT_psum, 1)
                stage_end(pe, END_SETUP + 1 + b)

            pe.wait_ge(in_vec2, 48)

            q1T_tiles = q1T[:].rearrange("p g c (j n) -> p g c j n", j=G)

            def first_layer(t, u, j):
                pe.wait_ge(f_diag, t + 1)
                for n in range(2):
                    hp = bank(2 * u + n)
                    pe.matmul(hp, diag[:, u, :], b1_s[:, n * 512:(n + 1) * 512], start=True, stop=False)
                for c in range(DC):
                    lhsT = q1T_flat(q1T, t, c, j, G, P, DC)
                    for n in range(2):
                        last = pe.matmul(bank(2 * u + n), lhsT, T1[:, c, n * 512:(n + 1) * 512],
                                         start=False, stop=(c == DC - 1))
                last.then_inc(f_hidden, 1)

            def transposes(t, u):
                pe.wait_ge(f_q, t + 1)
                for m in range(HC):
                    last = pe.transpose(bank16(4 + u)[:, m * P:(m + 1) * P], q2[:, u, m * P:(m + 1) * P], ident16[:])
                last.then_inc(f_qT_psum, 1)

            def second_layer(t, u):
                pe.wait_ge(f_qT, t + 1)
                for m in range(HC):
                    last = pe.matmul(bank(6 + u)[:, 0:D], q2T[:, u, m, :], T2[:, m, :],
                                     start=(m == 0), stop=(m == HC - 1))
                last.then_inc(f_y, 1)

            def stage2_tile(t, u, j, ahead):
                transposes(t, u)
                if ahead:
                    first_layer(t + 3, 1 - u, j)
                second_layer(t, u)

            for t in range(3):
                if t == 2:
                    pe.wait_ge(f_gelu, 1)
                first_layer(t, t % 2, t)
            stage2_tile(0, 0, 3, True)
            with pe.Fori(0, NT // G - 1) as i:
                for q in range(G):
                    stage2_tile(G * i + 1 + q, (q + 1) % 2, q, True)
            for t in range(NT - G + 1, NT):
                stage2_tile(t, t % 2, 0, False)
            stage_end(pe, END_2)

            pe.wait_ge(in_late, 16 * 8)

            def c_transposes(b, g):
                pe.wait_ge(c_n, GB * b + g + 1)
                transpose_group(lambda c: DC * g + c, lambda j: n3[:, G * g + j, :]).then_inc(c_nT_psum, 1)

            def c_queries(b, g):
                pe.wait_ge(c_nT, GB * b + g + 1)
                if b and g == 0:
                    pe.wait_ge(c_acc, TB * b)
                for o in range(DC):
                    product(bank((4 + DC * g + o) % 5), lambda c: M1[:, c, o * P:(o + 1) * P],
                            lambda c: nT[:, c, g * 512:(g + 1) * 512]).then_inc(c_qm_psum, 1)

            def c_values(b, i):
                if 1 <= i <= 4:
                    pe.wait_ge(c_qm, DC * GB * b + i)
                elif i > 4:
                    pe.wait_ge(c_vp, TB * b + i - 4)
                product(bank((8 + i) % 5)[:, 0:DV], lambda c: nT[:, c, i * P:(i + 1) * P],
                        lambda c: WVA[:, b, c, :]).then_inc(c_vp_psum, 1)

            def c_score(b, i):
                L = (i + 1) * P
                for h in range((L + 511) // 512):
                    n = min(512, L - h * 512)
                    for c in range(DC):
                        last = pe.matmul(bank(h)[:, 0:n], QmT[:, c, i * P:(i + 1) * P],
                                         nT[:, c, h * 512:h * 512 + n], start=(c == 0),
                                         stop=(c == DC - 1 and h != i // 4))
                    if h == i // 4:
                        last = pe.matmul(bank(h)[:, (i % 4) * P:(i % 4 + 1) * P], ident[:], causal[:],
                                         start=False, stop=True)
                last.then_inc(c_scores, 1)

            def c_tile(b, i):
                pe.wait_ge(c_exp, TB * b + i + 1)
                for j in range(i + 1):
                    last = pe.transpose(bank(2 + j // 4)[:, (j % 4) * P:(j % 4 + 1) * P],
                                        Pr[:, j * P:(j + 1) * P], ident[:])
                last.then_inc(c_pT_psum, 1)
                if i + 1 < TB:
                    c_score(b, i + 1)
                pe.wait_ge(c_pT, TB * b + i + 1)
                if i:
                    pe.wait_ge(c_acc, TB * b + i)
                product(bank(4)[:, 0:DV], lambda j: PT[:, j * P:(j + 1) * P],
                        lambda j: VP[:, j, :], i + 1).then_inc(c_att, 1)

            def ring_fill(b, g, what, h=0):
                n = ring_use(b, g, what, h)
                if n >= RING:
                    pe.wait_ge(ring_read[n % RING], n // RING)
                return ring_bank(b, g, what, h), ring_full[n % RING]

            def d_transposes(b, g, what):
                for c in range(DC):
                    at, full = ring_fill(b, g, what, c)
                    for j in range(G):
                        last = pe.transpose(at[:, j * P:(j + 1) * P], acc[:, b, g, j, c * P:(c + 1) * P],
                                            ident[:])
                    last.then_inc(full, 1)

            def d_probsT(b, g):
                pe.wait_ge(d_exp, GB * b + g + 1)
                at, full = ring_fill(b, g, "pT")
                for j in range(G):
                    last = pe.transpose(at[0:C, j * P:(j + 1) * P], s2raw[:, b, g, j, :], ident[:])
                last.then_inc(full, 1)

            def d_attention(b, g):
                pe.wait_ge(d_pT, GB * b + g + 1)
                for h in range(2):
                    at, full = ring_fill(b, g, "att", h)
                    for j in (2 * h, 2 * h + 1):
                        last = pe.matmul(at[:, (j % 2) * D:(j % 2 + 1) * D], p2T[:, g, j * P:(j + 1) * P],
                                         V2[:, b, :], start=True, stop=True)
                    last.then_inc(full, 1)

            def d_norm2T(b, g):
                pe.wait_ge(d_norm2, GB * b + g + 1)
                d_transposes(b, g, "nT")

            def d_first(b, g):
                pe.wait_ge(d_nT, GB * b + g + 1)
                for o in range(DC):
                    at, full = ring_fill(b, g, "pre", o)
                    product(at, lambda c: F1_s[:, c, o * P:(o + 1) * P], lambda c: ffT[:, g, c, :]
                            ).then_inc(full, 1)

            def d_second(b, g):
                pe.wait_ge(d_hT, GB * b + g + 1)
                for h in range(2):
                    at, full = ring_fill(b, g, "ff", h)
                    for j in (2 * h, 2 * h + 1):
                        last = product(at[:, (j % 2) * D:(j % 2 + 1) * D],
                                       lambda c: ffT[:, g, c, j * P:(j + 1) * P], lambda c: F2_s[:, c, :])
                    last.then_inc(full, 1)

            def d_norm4T(b, g):
                pe.wait_ge(d_n4, GB * b + g + 1)
                d_transposes(b, g, "n4T")

            def d_gate_logits(b, g):
                pe.wait_ge(d_n4T, GB * b + g + 1)
                at, full = ring_fill(b, g, "logits")
                for j in range(G):
                    last = product(at[:, j * E:(j + 1) * E], lambda c: ffT[:, g, c, j * P:(j + 1) * P],
                                   lambda c: Wg_s[:, c, :])
                last.then_inc(full, 1)

            for b in range(B):
                y = b - 1
                c_transposes(b, 0)
                if y >= 0:
                    d_probsT(y, 0)
                c_transposes(b, 1)
                c_queries(b, 0)
                if y >= 0:
                    d_probsT(y, 1)
                    d_attention(y, 0)
                c_queries(b, 1)
                for i in range(TB):
                    c_values(b, i)
                    if y >= 0 and i == 3:
                        d_attention(y, 1)
                pe.wait_ge(c_vp, TB * (b + 1))
                c_score(b, 0)
                for i in range(TB):
                    c_tile(b, i)
                    if y < 0:
                        continue
                    if i < 2:
                        d_norm2T(y, i)
                    elif i == 2:
                        d_first(y, 0)
                        d_first(y, 1)
                    elif i == 3:
                        d_second(y, 0)
                    elif i == 4:
                        d_second(y, 1)
                if y >= 0:
                    for g in range(GB):
                        d_norm4T(y, g)
                    for g in range(GB):
                        d_gate_logits(y, g)
            for part in (d_probsT, d_attention, d_norm2T, d_first, d_second, d_norm4T, d_gate_logits):
                for g in range(GB):
                    part(B - 1, g)
            stage_end(pe, END_3)

            pe.wait_ge(r_const, 1)
            pe.wait_ge(r_count, 1)
            flat_count = count[:].rearrange("p t e -> p (t e)")
            pe.matmul(bank(0)[:, 0:NT * E], strictly_lower[:], flat_count, start=True, stop=True)
            pe.matmul(bank(1)[:, 0:NT * E], ones5[:], flat_count, start=True, stop=True).then_inc(r_prefix, 1)
            pe.wait_ge(r_combine, 1)
            for t in range(NT):
                last = pe.transpose(ps[0:E, 4 + t // 4, (t % 4) * P:(t % 4 + 1) * P], combine[:, t, :], ident[:])
            last.then_inc(r_cT_psum, 1)
            for q in range(NTK // 8):
                pe.wait_ge(r_hot, q + 1)
                for k in range(8):
                    n = 8 * q + k
                    last = pe.matmul(bank(2)[:, 0:TILES], hot_lo[:, q % 2, k, :], hot_hi[:, n, :],
                                     start=(n == 0), stop=(n == NTK - 1))
                last.then_inc(r_hot_used, 1)
                if q == NTK // 8 - 1:
                    pe.drain().then_inc(r_code, 1)
            pe.wait_ge(r_cT, 1)
            for n in range(NT // 4):
                if n >= 2:
                    pe.wait_ge(r_b2_in, n - 1)
                for j in range(4):
                    last = pe.matmul(bank(2 * (n % 2) + j // 2)[:, (j % 2) * D:(j % 2 + 1) * D],
                                     combineT[:, 4 * n + j, :], e2b_s[:], start=True, stop=True)
                last.then_inc(r_b2, 1)
            stage_end(pe, END_4)

            def tile_in(j, turn):
                u = j[1] % U
                pe.wait_ge(m_rows[u], 16 * (turn + 1))
                for n in range(2 * DC):
                    last = pe.transpose(bank16(6 * (j[1] % 2))[:, n * P:(n + 1) * P],
                                        rows_in[:, u, n * P:(n + 1) * P], ident16[:])
                last.then_inc(m_xT_psum, 1)

            def expert_of(j):
                return pe.value_load(tile_expert[0:1, bass.ds(j[0], 1)], min_val=0, max_val=E - 1)

            def first_product(j, e):
                u, v = j[1] % U, j[1] % 2
                pe.wait_ge(m_xT, j[0] + 1)
                hi, lo = expert_w1_at(EWS, e, 0, DC, H), expert_w1_at(EWS, e, 1, DC, H)
                for m in range(HC):
                    dst = bank(2 + 2 * v + m // 4)[:, (m % 4) * P:(m % 4 + 1) * P]
                    terms = [(w(c, m), xT[:, u, a, c, :]) for c in range(DC) for w, a in ((hi, 0), (hi, 1), (lo, 0))]
                    for n, (lhsT, rhs) in enumerate(terms):
                        last = pe.matmul(dst, lhsT, rhs, start=(n == 0), stop=(n == len(terms) - 1))
                last.then_inc(m_hid_psum, 1)

            def second_product(j, e):
                v = j[1] % 2
                pe.wait_ge(m_hid16, j[0] + 1)
                hi, lo = expert_w2_at(EWS, e, 0, DC, H, HC, D), expert_w2_at(EWS, e, 1, DC, H, HC, D)
                terms = [(hid16[:, v, a, m, :], w(m)) for m in range(HC) for a, w in ((0, hi), (0, lo), (1, hi))]
                for n, (lhsT, rhs) in enumerate(terms):
                    last = pe.matmul(bank(1)[:, 0:D], lhsT, rhs, start=(n == 0), stop=(n == len(terms) - 1))
                last.then_inc(m_y_psum, 1)

            def step(j0, q, turn, e_now):
                e_next = expert_of((j0 + 1, q + 1))
                if turn is not None:
                    tile_in((j0 + 2, q + 2), turn)
                first_product((j0 + 1, q + 1), e_next)
                second_product((j0, q), e_now)
                return e_next

            pe.wait_ge(r_expert, 1)
            tile_in((0, 0), 0)
            tile_in((1, 1), 0)
            first_product((0, 0), expert_of((0, 0)))
            with pe.Fori(0, TILES // TURN) as i:
                e = expert_of((TURN * i, 0))
                for q in range(TURN):
                    e = step(TURN * i + q, q, 2 * i + (q + 2) // U, e)
            rest = TILES // TURN * TURN
            e = expert_of((rest, rest))
            for j in range(rest, TILES - 1):
                e = step(j, j, (j + 2) // U if j + 2 < TILES else None, e)
            second_product((TILES - 1, TILES - 1), e)
            stage_end(pe, END_5)


def count_total(ps, NT, E):
    return ps[:, 1, 0:NT * E].rearrange("p (t e) -> p t e", t=NT)


def q1T_flat(q1T, t, c, j, G, P, DC):
    flat = q1T[:].rearrange("p g c n -> p (g c n)")
    return flat[:, bass.ds((t - j) * (DC * P) + c * G * P + j * P, P)]


def expert_w1_at(EWS, e, part, DC, H):
    flat = EWS[:].rearrange("p e n -> p (e n)")
    return lambda c, m: flat[:, bass.ds(e * EWS.shape[2] + part * DC * H + c * H + m * P, P)]


def expert_w2_at(EWS, e, part, DC, H, HC, D):
    flat = EWS[:].rearrange("p e n -> p (e n)")
    return lambda m: flat[:, bass.ds(e * EWS.shape[2] + 2 * DC * H + part * HC * D + m * D, D)]


_INS = ['x', 'ctx_1024', 'g_xattn', 'g_ffn', 'L0_xattn_W', 'L0_xattn_b', 'L0_ffn_ln1_g', 'L0_ffn_ln1_b',
        'L0_ffn_w1', 'L0_ffn_b1', 'L0_ffn_ln2_g', 'L0_ffn_ln2_b', 'L0_ffn_w2', 'L0_ffn_b2',
        'L1_xattn_Wk1', 'L1_xattn_Wq1', 'L1_xattn_Wv1', 'L1_xattn_Wk2', 'L1_xattn_Wq2', 'L1_xattn_Wv2',
        'L1_xattn_W1', 'L1_xattn_b1', 'L1_xattn_W2', 'L1_xattn_b2', 'L1_xattn_gamma', 'L1_xattn_beta',
        'L1_ffn_Wg', 'L1_ffn_bg', 'L1_ffn_W1', 'L1_ffn_b1', 'L1_ffn_W2', 'L1_ffn_b2']
_OUTS = [((2, 1024, 256), 'float32')]


def kernel(**inputs):
    import numpy as _np
    import concourse.bacc as _bacc
    from concourse import mybir as _mybir
    from concourse.bass_utils import run_bass_kernel_spmd as _run

    nc = _bacc.Bacc("TRN2", target_bir_lowering=False, num_devices=1)
    arrays, args = {}, []
    for name in _INS:
        a = _np.ascontiguousarray(inputs[name])
        arrays[f"in_{name}_dram"] = a
        args.append(nc.dram_tensor(f"in_{name}_dram", a.shape, _mybir.dt.from_np(a.dtype), kind="ExternalInput").ap())
    for i, (shape, dtype) in enumerate(_OUTS):
        dt = _mybir.dt.from_np(_np.dtype(dtype))
        args.append(nc.dram_tensor(f"out_{i}_dram", shape, dt, kind="ExternalOutput").ap())
    gated_blocks_kernel(nc, *args)
    r = _run(nc, [arrays], core_ids=[0])
    got = tuple(r.results[0][f"out_{i}_dram"] for i in range(len(_OUTS)))
    return got[0]
```

```python
from contextlib import ExitStack

import concourse.bass as bass
from concourse import mybir

F32 = mybir.dt.float32
BF16 = mybir.dt.bfloat16
I32 = mybir.dt.int32
U32 = mybir.dt.uint32
ALU = mybir.AluOpType
ACT = mybir.ActivationFunctionType
X = mybir.AxisListType.X

P = 128
MAGIC = 1.5 * 2.0 ** 23
LN_EPS = 1e-5
L1_EPS = 1e-3
MASKED = -1e30


def gated_blocks_kernel(
    nc: bass.Bass, x, ctx_in, g_xattn, g_ffn,
    W, Wb, ln1_g, ln1_b, w1, b1, ln2_g, ln2_b, w2, b2,
    Wk1, Wq1, Wv1, Wk2, Wq2, Wv2, F1, f1b, F2, f2b, gamma, beta,
    Wg, bg, E1, e1b, E2, e2b, out,
):
    B, S, D = x.shape
    C = ctx_in.shape[1]
    H = w1.shape[0]
    E = Wg.shape[1]
    DC, HC = D // P, H // P
    NT = B * S // P
    TB = S // P
    G = 4
    GB = TB // G
    NG = NT // G
    DV = D + C
    K = 2
    SLOTS = B * S * K
    TILES = (SLOTS + E * (P - 1)) // P
    U = 3
    TURN = 2 * U
    assert D == 256 and S == 1024 and H == 1024 and TILES % U == 0 and TB == GB * G
    EW = 2 * DC * H + 2 * HC * D
    BLK = 1024
    EBLK = EW // 2 // BLK
    BITS = 3
    assert E <= 1 << BITS
    EARLY = 5
    ORDER = list(range(EARLY)) + list(range(EARLY + 1, E)) + [EARLY]

    split_rows = nc.dram_tensor("split_rows", (B * S, 2 * D), BF16, kind="Internal").ap()
    choice_rows = nc.dram_tensor("choice_rows", (SLOTS + P, D), F32, kind="Internal").ap()

    x_tiles = x.rearrange("b (t p) d -> p (b t) d", p=P)
    out_tiles = out.rearrange("b (t p) d -> p (b t) d", p=P)

    with ExitStack() as stack:
        def sem(name):
            return stack.enter_context(nc.semaphore(name))

        def keep(name, shape, dt=F32):
            return stack.enter_context(nc.sbuf_tensor(name, shape, dt))

        ps = stack.enter_context(nc.psum_tensor("ps", [P, 8, 512], F32))

        def bank(k):
            return ps[:, k, :]

        def bank16(k):
            return ps[:, k, :].bitcast(BF16)

        res = keep("res", [P, NT, D])
        EWS = keep("EWS", [P, E, EW], BF16)
        stage_in = keep("stage_in", [P, 2, BLK])
        ident = keep("ident", [P, P])
        ident16 = keep("ident16", [P, P], BF16)
        causal = keep("causal", [P, P])
        gates = keep("gates", [P, 4])
        minus_half = keep("minus_half", [P, G])
        stats = keep("stats", [P, G, 6])
        moments = keep("moments", [P, NG, G, 2])
        rstd = keep("rstd", [P, NG, G])
        expert_b1 = keep("expert_b1", [P, E * HC])
        logits = keep("logits", [P, NT, E])
        Wg_s = keep("Wg_s", [P, DC, E])
        bg_s = keep("bg_s", [P, E])
        e2b_s = keep("e2b_s", [E, D])
        zero_col = keep("zero_col", [P, 1])

        def expert_w1(e, part):
            return EWS[:, e, part * DC * H:(part + 1) * DC * H].rearrange("p (c h) -> p c h", c=DC)

        def expert_w2(e):
            return EWS[:, e, 2 * DC * H:EW].rearrange("p (m a d) -> p m a d", m=HC, a=2)

        def block_parts(e, k):
            if k < EBLK // 2:
                return expert_w1(e, 0)[:, k, :], expert_w1(e, 1)[:, k, :]
            m = (k - EBLK // 2) * (HC // 2)
            return tuple(expert_w2(e)[:, m:m + HC // 2, part, :] for part in range(2))

        def block_in_buffer(k):
            at = stage_in[:, k % 2, :]
            return at if k < EBLK // 2 else at.rearrange("p (m d) -> p m d", m=HC // 2)

        spare = EWS[:, EARLY:E, :].rearrange("p e n -> p (e n)").bitcast(F32)

        unloaded = EWS[:, 0:EARLY - 1, :].rearrange("p e n -> p (e n)").bitcast(F32)

        def carve(sizes, place=spare):
            at, views = 0, []
            for n in sizes:
                views.append(place[:, at:at + n])
                at += n
            assert at <= place.shape[1]
            return views

        early3 = ExitStack()
        stack.enter_context(early3)

        def sb3(name, shape, dt=F32):
            return early3.enter_context(nc.sbuf_tensor(name, shape, dt))

        M1 = sb3("M1", [P, DC, D])
        WVA = sb3("WVA", [P, B, DC, DV])
        V2 = sb3("V2", [C, B, D])
        F1_s = sb3("F1_s", [P, DC, D])
        F2_s = sb3("F2_s", [P, DC, D])
        f1b_s = sb3("f1b_s", [P, DC])
        f2b_s = sb3("f2b_s", [P, D])
        gamma_s = sb3("gamma_s", [P, D])
        beta_s = sb3("beta_s", [P, D])

        st12 = ExitStack()

        def sb12(name, shape, dt=F32):
            return st12.enter_context(nc.sbuf_tensor(name, shape, dt))

        T1 = sb12("T1", [P, DC, H], BF16)
        T2 = sb12("T2", [P, HC, D], BF16)
        wscale = sb12("wscale", [P, 2])
        wscale_inv = sb12("wscale_inv", [P, 2])
        wscale_127 = sb12("wscale_127", [P, 2])
        q1T = sb12("q1T", [P, NT // G, DC, G * P], BF16)
        scale1 = sb12("scale1", [P, NT])
        inverse1 = sb12("inverse1", [P, NT])
        inverse_rest = sb12("inverse_rest", [P, NT])
        inverse_parts = sb12("inverse_parts", [P, NT, 3, 3], BF16)
        tq = sb12("tq", [C, B, D])
        tqT = sb12("tqT", [P, B, DC, C])

        ctx_s, ctxT, Wb_s, K2T, A2, bias_rows, ones, w_abs, w_sum, pT_v, b1_v, b1_rest_v, b1_parts_v, *raw_v = carve(
            [B * D, DC * B * C, D, DC * B * C, DC * B * C, P, P, 2, 2, NG * G * P, H, H, 2 * H] + [DC * D] * 12,
            unloaded)
        b1_s, b1_rest = b1_v[0:1, :], b1_rest_v[0:1, :]
        b1_parts = b1_parts_v[0:1, :].bitcast(BF16).rearrange("p (a h) -> p a h", a=4)[:, 0:3, :]
        ctx_s = ctx_s[0:C, :].rearrange("p (b d) -> p b d", b=B)
        ctxT = ctxT.rearrange("p (c b k) -> p c b k", c=DC, b=B)
        K2T, A2 = (v.rearrange("p (c k) -> p c k", c=DC) for v in (K2T, A2))
        bias_rows = bias_rows[0:E * HC + DC, :]
        raw = {n: v.rearrange("p (c d) -> p c d", c=DC) for n, v in zip(
            ["W", "Wq1", "Wk1", "Wq2", "Wv1", "Wk2", "Wv2", "WT", "Wq1T", "Wk1T", "Wq2T", "Wv1T"], raw_v)}
        borrowed = EWS[:, EARLY - 1, :]
        w1_s = borrowed[:, 0:2 * HC * D].bitcast(F32).rearrange("p (c d) -> p c d", c=HC)
        t1_s = borrowed[:, 2 * HC * D:3 * HC * D].rearrange("p (c d) -> p c d", c=HC)
        t2_s = borrowed[:, 3 * HC * D:4 * HC * D].rearrange("p (c d) -> p c d", c=DC)
        w2_s = stage_in[:]

        s1 = ExitStack()

        def sb1(name, shape, dt=F32):
            return s1.enter_context(nc.sbuf_tensor(name, shape, dt))

        h_v, hT_v = carve([NG * G * D, NG * DC * G * P])
        h1 = h_v.rearrange("p (g j d) -> p g j d", g=NG, j=G)
        hT = hT_v.rearrange("p (g c n) -> p g c n", g=NG, c=DC)
        probsT = pT_v[0:C, :].rearrange("p (g n) -> p g n", g=NG)
        probs = sb1("probs", [P, NG, G, C])
        q1 = sb1("q1", [P, NG, G, D], BF16)
        top = sb1("top", [P, NG, G])
        total = sb1("total", [P, NG, G])
        ln1_g_s = sb1("ln1_g_s", [P, D])
        ln1_b_s = sb1("ln1_b_s", [P, D])
        b2_s = sb1("b2_s", [P, D])
        sx1 = sb1("sx1", [P, NG, G])
        graw = sb1("graw", [P, 4])
        minus_magic = sb1("minus_magic", [P, 1])
        s1.close()

        y2_v, v2_v, _, g2_v, bb2_v, b1_rows_v, invT_v = carve(
            [2 * H, 2 * H, NG * G * D + NG * DC * G * P - 4 * H, H, H, H // 2, NT * P // 2])
        y2 = y2_v.rearrange("p (u h) -> p u h", u=2)
        v2 = v2_v.rearrange("p (u h) -> p u h", u=2)
        ln2_g_s, ln2_b_s = g2_v, bb2_v
        b1_rows = b1_rows_v[0:9, :].bitcast(BF16)
        inverseT = invT_v[0:9, :].bitcast(BF16)
        s2 = ExitStack()

        def sb2(name, shape, dt=F32):
            return s2.enter_context(nc.sbuf_tensor(name, shape, dt))

        q2 = sb2("q2", [P, 2, H], BF16)
        q2T = sb2("q2T", [P, 2, HC, P], BF16)
        ysum = sb2("ysum", [P, 2])
        ysq = sb2("ysq", [P, 2])
        neg_mean = sb2("neg_mean", [P, 2])
        rstd2 = sb2("rstd2", [P, 2])
        vmax = sb2("vmax", [P, 2])
        sx2 = sb2("sx2", [P, 2])
        outscale = sb2("outscale", [P, 2])
        square_out = sb2("square_out", [P, 2, H], BF16)
        s2.close()
        st12.close()

        first_v, then_v, nT_v, n_v, QmT_v, P_v, PT_v = carve(
            [GB * DC * G * P, GB * DC * G * P, DC * S, TB * D, DC * S, S, S])
        assert 2 * GB * DC * G * P >= 4 * H and 2 * GB * DC * G * P + DC * S + TB * D <= NG * G * D + NG * DC * G * P
        assert 2 * GB * DC * G * P <= EW // 2
        nT = nT_v.rearrange("p (c s) -> p c s", c=DC)
        QmT = QmT_v.rearrange("p (c s) -> p c s", c=DC)
        n3 = n_v.rearrange("p (t d) -> p t d", t=TB)
        Pr, PT = P_v, PT_v
        ffT = first_v.rearrange("p (g c s) -> p g c s", g=GB, c=DC)
        preT = then_v.rearrange("p (g c s) -> p g c s", g=GB, c=DC)
        split3 = then_v.bitcast(BF16).rearrange("p (g j n) -> p g j n", g=GB, j=G)
        s3 = ExitStack()

        def sb3o(name, shape, dt=F32):
            return s3.enter_context(nc.sbuf_tensor(name, shape, dt))

        VP = sb3o("VP", [P, TB, DV])
        acc = sb3o("acc", [P, B, GB, G, D])
        s2raw = sb3o("s2raw", [P, B, GB, G, C])
        negmax = sb3o("negmax", [P, TB])
        rowsum = sb3o("rowsum", [P, TB])
        rowinv = sb3o("rowinv", [P, TB])
        top3 = sb3o("top3", [P, GB, G])
        total3 = sb3o("total3", [P, GB, G])
        p2T = sb3o("p2T", [C, GB, G * P])
        s3.close()
        early3.close()

        s5 = ExitStack()

        def sb5(name, shape, dt=F32):
            return s5.enter_context(nc.sbuf_tensor(name, shape, dt))

        NTK = NT * K
        weight = sb5("weight", [P, NT, K])
        src_row = sb5("src_row", [P, TILES], I32)
        dst_row = sb5("dst_row", [P, TILES], I32)
        tile_expert = sb5("tile_expert", [P, TILES], I32)
        packed = sb5("packed", [1, TILES + 8], I32)
        pe_exp = sb5("pe_exp", [P, NT, E])
        gsum = sb5("gsum", [P, NT])
        gtop = sb5("gtop", [P, NT, 8])
        gidx = sb5("gidx", [P, NT, 8], U32)
        gidx_f = sb5("gidx_f", [P, NT, K])
        onehot = sb5("onehot", [P, NT, K, E])
        count = sb5("count", [P, NT, E])
        tiles_upto = sb5("tiles_upto", [P, 2, NT, E])
        denom = sb5("denom", [P, NT])
        combine = sb5("combine", [P, NT, E])
        combineT = sb5("combineT", [E, NT, P])
        strictly_lower = sb5("strictly_lower", [P, P])
        ones5 = sb5("ones5", [P, P])
        iota_e = sb5("iota_e", [P, E])
        iota_p = sb5("iota_p", [P, P])
        iota_j = sb5("iota_j", [P, TILES])
        code_in = sb5("code_in", [P, NT, K])
        code_tile = sb5("code_tile", [P, NT, K])
        etiles = sb5("etiles", [P, E])
        eend = sb5("eend", [P, 2, E])
        prefix = sb5("prefix", [P, NT, E])
        place = sb5("place", [P, NT, K])
        picked = sb5("picked", [P, NT, K, E])
        place_hi = sb5("place_hi", [P, NT, K])
        place_lo = sb5("place_lo", [P, NT, K])
        hot_hi = sb5("hot_hi", [P, NTK, TILES], BF16)
        coded = sb5("coded", [P, NTK, 2, TILES], BF16)
        code = sb5("code", [P, TILES])
        pad_row = sb5("pad_row", [P, 1])
        src_f = sb5("src_f", [P, TILES])
        dst_f = sb5("dst_f", [P, TILES])
        ended = sb5("ended", [P, TILES, E])
        tile_expert_f = sb5("tile_expert_f", [P, TILES])
        packing = ended[0:1, :, :].rearrange("p j e -> p (j e)")[:, 0:4 * (TILES + 8)].rearrange(
            "p (a j) -> p a j", a=4)
        src_now = sb5("src_now", [P, U], I32)
        dst_now = sb5("dst_now", [P, U], I32)
        rows_in = sb5("rows_in", [P, U, 2 * D], BF16)
        xT = sb5("xT", [P, U, 2, DC, P], BF16)
        hid = sb5("hid", [P, 2, HC * P])
        hot_lo = hid[:, 0, :].bitcast(BF16).rearrange("p (u k n) -> p u k n", u=2, k=8)
        hid16 = sb5("hid16", [P, 2, 2, HC, P], BF16)
        rows_out = sb5("rows_out", [P, U, D])
        s5.close()
        both = EWS[:, 0:2, :].rearrange("p e n -> p (e n)").bitcast(F32).rearrange(
            "p (t k d) -> p t k d", t=NT, k=K)

        stage_done, waited_alone = sem("stage_done"), sem("waited_alone")
        in_x = [sem(f"in_x{g}") for g in range(NG)]
        in_first, in_w12, in_w, in_gates = sem("in_first"), sem("in_w12"), sem("in_w"), sem("in_gates")
        in_vec, in_vec2, in_late = sem("in_vec"), sem("in_vec2"), sem("in_late")
        block_in = [sem("block_in0"), sem("block_in1")]
        block_high, block_split = sem("block_high"), sem("block_split")
        const_made, gates_made = sem("const_made"), sem("gates_made")
        su_psum, su_copied, su_abs, su_scale, su_rounded, su_tern = (sem(n) for n in (
            "su_psum", "su_copied", "su_abs", "su_scale", "su_rounded", "su_tern"))
        a_moments, a_rstd, a_h, a_hT = (sem(n) for n in ("a_moments", "a_rstd", "a_h", "a_hT"))
        a_shifted, a_probs, a_pT, a_total, a_relu, a_centred = (sem(n) for n in (
            "a_shifted", "a_probs", "a_pT", "a_total", "a_relu", "a_centred"))
        a_rounded, a_q, a_qT, a_b2 = (sem(n) for n in ("a_rounded", "a_q", "a_qT", "a_b2"))
        in_b1, in_b1_rows, b1_high, b1_left = (sem(n) for n in ("in_b1", "in_b1_rows", "b1_high", "b1_left"))
        a_inverse, a_inverseT_psum = sem("a_inverse"), sem("a_inverseT_psum")
        f_hidden, f_gelu, f_mean, f_sq, f_rstd = (sem(n) for n in (
            "f_hidden", "f_gelu", "f_mean", "f_sq", "f_rstd"))
        f_scaled, f_q, f_qT_psum, f_qT, f_y = (sem(n) for n in (
            "f_scaled", "f_q", "f_qT_psum", "f_qT", "f_y"))
        c_moments, c_rstd, c_n, c_nT_psum, c_nT = (sem(n) for n in (
            "c_moments", "c_rstd", "c_n", "c_nT_psum", "c_nT"))
        c_qm_psum, c_qm, c_vp_psum, c_vp = (sem(n) for n in ("c_qm_psum", "c_qm", "c_vp_psum", "c_vp"))
        c_scores, c_max, c_exp, c_pT_psum, c_pT, c_att, c_acc = (sem(n) for n in (
            "c_scores", "c_max", "c_exp", "c_pT_psum", "c_pT", "c_att", "c_acc"))
        d_moments = [sem(f"d_moments{g}") for g in range(GB)]
        d_rstd = [sem(f"d_rstd{g}") for g in range(GB)]
        d_shift, d_exp, d_pT, d_norm2, d_nT, d_bias = (sem(n) for n in (
            "d_shift", "d_exp", "d_pT", "d_norm2", "d_nT", "d_bias"))
        d_pre, d_hT, d_norm3, d_relu, d_n4, d_hi, d_lo, d_n4T, d_stored = (sem(n) for n in (
            "d_pre", "d_hT", "d_norm3", "d_relu", "d_n4", "d_hi", "d_lo", "d_n4T", "d_stored"))
        r_const, r_exp, r_count, r_prefix, r_hot, r_hot_used, r_code, r_expert = (
            sem(n) for n in ("r_const", "r_exp", "r_count", "r_prefix", "r_hot", "r_hot_used",
                             "r_code", "r_expert"))
        r_shift, r_combine, r_cT_psum, r_cT, r_b2, r_b2_in = (sem(n) for n in (
            "r_shift", "r_combine", "r_cT_psum", "r_cT", "r_b2", "r_b2_in"))
        r_packed = sem("r_packed")
        m_rows = [sem(f"m_rows{u}") for u in range(U)]
        m_out = [sem(f"m_out{u}") for u in range(U)]
        m_src = sem("m_src")
        m_xT_psum, m_xT, m_hid_psum, m_hid, m_hid16, m_y_psum, m_y = (sem(n) for n in (
            "m_xT_psum", "m_xT", "m_hid_psum", "m_hid", "m_hid16", "m_y_psum", "m_y"))
        Z = 4
        z_in = [sem(f"z_in{n}") for n in range(NT // Z)]
        z_sum, z_out = sem("z_sum"), sem("z_out")

        def wait_alone(eng, s, n):
            eng.wait_ge(s, n)
            eng.sem_inc(waited_alone, 1)

        def stage_end(eng, n):
            eng.drain().then_inc(stage_done, 1)
            wait_alone(eng, stage_done, 5 * n)

        END_1, END_2, END_3, END_5 = 1, 2, 3, 4

        class Ring:

            def __init__(self, name, first, size, steps, groups):
                self.first, self.size, self.steps, self.groups = first, size, steps, groups
                self.full = [sem(f"{name}_full{k}") for k in range(size)]
                self.read = [sem(f"{name}_read{k}") for k in range(size)]

            def use(self, turn, g, what, half=0):
                use = turn * self.groups * sum(size for _, size in self.steps)
                for name, size in self.steps:
                    if name == what:
                        return use + g * size + half
                    use += self.groups * size

            def bank(self, *which):
                return bank(self.first + self.use(*which) % self.size)

            def wait(self, eng, *which):
                n = self.use(*which)
                eng.wait_ge(self.full[n % self.size], n // self.size + 1)

            def free(self, *which):
                return self.read[self.use(*which) % self.size]

            def fill(self, eng, *which):
                n = self.use(*which)
                if n >= self.size:
                    eng.wait_ge(self.read[n % self.size], n // self.size)
                return self.bank(*which), self.full[n % self.size]

        a_ring = Ring("a_ring", 0, 6, (("hT", 2), ("scores", 1), ("pT", 1), ("att", 2), ("qT", 1)), NG)
        D_STEPS = (("pT", 1), ("att", 2), ("nT", 2), ("pre", 2), ("ff", 2), ("n4T", 2), ("logits", 1))
        beside_ring, last_ring = Ring("beside", 5, 3, D_STEPS, GB), Ring("last", 0, 6, D_STEPS, GB)

        def d_ring(b):
            return beside_ring if b < B - 1 else last_ring

        def d_turn(b):
            return b if b < B - 1 else 0

        def cols(ap, n):
            return ap.unsqueeze(len(ap.shape)).to_broadcast(list(ap.shape) + [n])

        def rows4(ap):
            return ap.unsqueeze(1).to_broadcast([P, G, ap.shape[-1]])

        B2_BANKS = (4, 6, 0, 4)
        LATE = (E - 1 - EARLY) * EBLK
        SU_TRANSPOSED = {1: "W", 5: "Wq1", 6: "Wk1", 7: "Wq2", 8: "Wv1"}

        block = stack.enter_context(nc.Block())

        @block.sync
        def _(sp):
            def vec(dst, src, s):
                sp.dma_start(dst, src.partition_broadcast(P)).then_inc(s, 16)

            def mat(dst, src, s):
                sp.dma_start(dst, src.rearrange("(c p) n -> p c n", p=P)).then_inc(s, 16)

            def group_in(g):
                sp.dma_start(res[:, G * g:G * (g + 1), :], x_tiles[:, G * g:G * (g + 1), :]).then_inc(in_x[g], 16)

            group_in(0)
            sp.dma_start(ctx_s, ctx_in.rearrange("b c d -> c b d")).then_inc(in_first, 16)
            mat(raw["W"], W, in_first)
            vec(Wb_s, Wb, in_first)
            for g in range(1, NG):
                group_in(g)
            vec(graw[:, 0:2], g_xattn, in_gates)
            vec(graw[:, 2:4], g_ffn, in_gates)
            mat(w1_s, w1, in_w12)
            mat(w2_s, w2, in_w12)
            vec(ln1_g_s[:], ln1_g, in_vec)
            vec(ln1_b_s[:], ln1_b, in_vec)
            vec(b2_s[:], b2, in_vec)
            for name, src in (("Wq1", Wq1), ("Wk1", Wk1), ("Wq2", Wq2), ("Wv1", Wv1), ("Wk2", Wk2), ("Wv2", Wv2)):
                mat(raw[name], src, in_w)
            sp.dma_start(bias_rows[0:E * HC, :], e1b.rearrange("e (m p) -> (e m) p", p=P)).then_inc(in_w, 16)
            sp.dma_start(bias_rows[E * HC:E * HC + DC, :], f1b.rearrange("(c p) -> c p", p=P)).then_inc(in_w, 16)
            vec(ln2_g_s, ln2_g, in_vec2)
            vec(ln2_b_s, ln2_b, in_vec2)
            sp.dma_start(b1_s, b1.partition_broadcast(1)).then_inc(in_b1, 16)
            for dst, src in ((F1_s, F1), (F2_s, F2), (Wg_s, Wg)):
                mat(dst[:], src, in_late)
            sp.dma_start(e2b_s[:], e2b).then_inc(in_late, 16)
            for dst, src in ((f2b_s, f2b), (gamma_s, gamma), (beta_s, beta), (bg_s, bg)):
                vec(dst[:], src, in_late)

            def load_block(n, e, k):
                s = k % 2
                if k < EBLK // 2:
                    sp.dma_start(stage_in[:, s, :], E1[e, k * P:(k + 1) * P, :]).then_inc(block_in[s], 16)
                else:
                    f0 = (k - EBLK // 2) * (HC // 2) * P
                    sp.dma_start(stage_in[:, s, :].rearrange("p (m d) -> p m d", m=HC // 2),
                                 E2[e, f0:f0 + HC // 2 * P, :].rearrange("(m p) d -> p m d", p=P)
                                 ).then_inc(block_in[s], 16)

            sp.wait_ge(b1_high, 2)
            sp.wait_ge(b1_left, 2)
            for a in range(3):
                for k in range(3):
                    sp.dma_start(b1_rows[3 * a + k:3 * a + k + 1, :], b1_parts[:, a, :]).then_inc(in_b1_rows, 16)
            sp.wait_ge(in_b1_rows, 16 * 9)
            sp.wait_ge(su_tern, 2)
            load_block(0, 0, 0)
            load_block(0, 0, 1)
            stage_end(sp, END_1)
            for k in range(2, EBLK):
                sp.wait_ge(block_split, k - 1)
                load_block(0, 0, k)
            with sp.Fori(1, NT // EBLK) as e:
                for k in range(EBLK):
                    wait_alone(sp, block_split, EBLK * e + k - 1)
                    load_block(e, e, k)
            stage_end(sp, END_2)

            def load_next(n, k):
                sp.wait_ge(block_split, EBLK * n + k - 1)
                load_block(n, ORDER[n], k)

            def store_split(b, g):
                sp.wait_ge(d_lo, GB * b + g + 1)
                sp.dma_start(split_rows[(TB * b + G * g) * P:(TB * b + G * (g + 1)) * P, :].rearrange(
                    "(j p) n -> p j n", p=P), split3[:, g, :, :]).then_inc(d_stored, 16)

            for k in range(EBLK):
                load_next(EARLY - 1, k)
            load_next(EARLY, 0)
            load_next(EARLY, 1)
            for b in range(B):
                for g in range(GB):
                    store_split(b, g)
                if b == B - 2:
                    for n in range(EARLY, E - 1):
                        for k in range(2 if n == EARLY else 0, EBLK):
                            load_next(n, k)
                    load_next(E - 1, 0)
                    load_next(E - 1, 1)
            sp.wait_ge(d_stored, 16 * GB * B)
            stage_end(sp, END_3)
            for k in range(2, EBLK):
                load_next(E - 1, k)
            stage_end(sp, END_5)
            for n in range(NT // Z):
                sp.dma_start(both[:, Z * n:Z * (n + 1), :, :].rearrange("p j k d -> p j (k d)"),
                             choice_rows[n * Z * P * K:(n + 1) * Z * P * K, :].rearrange(
                                 "(j p k) d -> p j (k d)", p=P, k=K)).then_inc(z_in[n], 16)
            for n in range(NT // Z):
                sp.wait_ge(z_sum, n + 1)
                sp.dma_start(out_tiles[:, Z * n:Z * (n + 1), :], res[:, Z * n:Z * (n + 1), :]).then_inc(z_out, 16)
            sp.wait_ge(z_out, 16 * (NT // Z))

        @block.gpsimd
        def _(pool):
            pool.memset(ident[:], 0.0)
            pool.memset(ident16[:], 0.0)
            pool.memset(causal[:], 0.0)
            pool.memset(minus_half[:], -0.5)
            pool.memset(zero_col[:], 0.0)
            pool.memset(ones, 1.0)
            pool.memset(minus_magic[:], -MAGIC)
            pool.drain()
            pool.affine_select(out=ident[:], in_=ident[:], compare_op=ALU.not_equal, fill=1.0,
                               base=0, pattern=[[-1, P]], channel_multiplier=1)
            pool.affine_select(out=ident16[:], in_=ident16[:], compare_op=ALU.not_equal, fill=1.0,
                               base=0, pattern=[[-1, P]], channel_multiplier=1)
            pool.affine_select(out=causal[:], in_=causal[:], compare_op=ALU.is_ge, fill=MASKED,
                               base=0, pattern=[[-1, P]], channel_multiplier=1)
            pool.drain().then_inc(const_made, 1)

            def rsqrt(dst, var, a, c, half, done):
                pool.tensor_scalar(dst, var, a, c, ALU.mult, ALU.add)
                pool.drain()
                pool.tensor_tensor(dst, dst, half, ALU.pow).then_inc(done, 1)

            def split_block(n, e, k):
                hi, lo = block_parts(e, k)
                pool.wait_ge(block_high, EBLK * n + k + 1)
                pool.tensor_tensor(lo, block_in_buffer(k), hi, ALU.subtract).then_inc(block_split, 1)

            def a_rsqrt(g, a, c, n):
                pool.wait_ge(a_moments, NG * n + g + 1)
                rsqrt(rstd[:, g, :], moments[:, g, :, 1], a, c, minus_half[:], a_rstd)

            def a_add_b2(g):
                pool.wait_ge(a_centred, g + 1)
                r = res[:, G * g:G * (g + 1), :]
                pool.tensor_tensor(r, r, rows4(b2_s[:]), ALU.add).then_inc(a_b2, 1)

            for g in range(NG):
                a_rsqrt(g, 1.0, LN_EPS, 0)
            pool.wait_ge(gates_made, 1)
            pool.wait_ge(in_vec, 48)
            pool.tensor_scalar(b2_s[:], b2_s[:], gates[:, 2:3], 0.0, ALU.mult, ALU.add)
            pool.wait_ge(su_scale, 1)
            for n, w_s in enumerate((w1_s, w2_s)):
                flat = w_s.rearrange("p a b -> p (a b)")
                pool.tensor_scalar(flat, flat, wscale_inv[:, n:n + 1], MAGIC, ALU.mult, ALU.add
                                   ).then_inc(su_rounded, 1)
            pool.wait_ge(in_b1, 16)
            pool.wait_ge(b1_high, 1)
            pool.tensor_tensor(b1_rest, b1_s, b1_parts[:, 0, :], ALU.subtract).then_inc(b1_left, 1)
            for g in range(NG):
                a_rsqrt(g, 1.0 + LN_EPS, LN_EPS ** 2, 1)
                if g:
                    a_add_b2(g - 1)
            a_add_b2(NG - 1)
            pool.wait_ge(b1_high, 2)
            pool.tensor_tensor(b1_parts[:, 2, :], b1_rest, b1_parts[:, 1, :], ALU.subtract).then_inc(b1_left, 1)
            for g in range(NG):
                pool.wait_ge(a_rounded, g + 1)
                pool.tensor_scalar(q1[:, g, :, :], h1[:, g, :, :], -MAGIC, 1.0, ALU.add, ALU.mult).then_inc(a_q, 1)
            stage_end(pool, END_1)

            def hidden_rstd(t, u):
                wait_alone(pool, f_sq, t + 1)
                rsqrt(rstd2[:, u:u + 1], ysq[:, u:u + 1], 1.0 / H, LN_EPS, minus_half[:, 0:1], f_rstd)

            def c_rsqrt(b, g):
                pool.wait_ge(c_moments, GB * b + g + 1)
                rsqrt(rstd[:, g, :], moments[:, g, :, 1], 1.0, LN_EPS, minus_half[:], c_rstd)

            def stage2_tile(t, u, following, e, k):
                wait_alone(pool, f_scaled, t + 1)
                pool.tensor_scalar(q2[:, u, :], v2[:, u, :], -MAGIC, 1.0, ALU.add, ALU.mult).then_inc(f_q, 1)
                split_block(e, e, k)
                if following:
                    hidden_rstd(t + 2, u)

            hidden_rstd(0, 0)
            hidden_rstd(1, 1)
            with pool.Fori(0, NT // EBLK - 1) as e:
                for k in range(EBLK):
                    stage2_tile(EBLK * e + k, k % 2, True, e, k)
            for k in range(EBLK):
                t = NT - EBLK + k
                stage2_tile(t, k % 2, t + 2 < NT, NT // EBLK - 1, k)
            for g in range(GB):
                c_rsqrt(0, g)
            stage_end(pool, END_2)

            def split_late(first, end):
                for at in range(first, end):
                    n = EARLY + at // EBLK
                    split_block(n, ORDER[n], at % EBLK)

            def d_rsqrt(b, g, n):
                pool.wait_ge(d_moments[g], 4 * b + n + 1)
                rsqrt(rstd[:, GB + g, :], moments[:, GB + g, :, 1], 1.0, L1_EPS if n < 3 else LN_EPS,
                      minus_half[:], d_rstd[g])

            def add_bias(b, g):
                pool.wait_ge(d_nT, GB * b + g + 1)
                a = acc[:, b, g, :, :]
                pool.tensor_tensor(a, a, rows4(f2b_s[:]), ALU.add).then_inc(d_bias, 1)

            for b in range(B + 1):
                if 0 < b < B:
                    for g in range(GB):
                        c_rsqrt(b, g)
                if b == 0:
                    for k in range(EBLK):
                        split_block(EARLY - 1, EARLY - 1, k)
                else:
                    y, last_turn = b - 1, b == B
                    for g in range(GB):
                        d_rsqrt(y, g, 0)
                    if last_turn:
                        split_late(0, 2)
                        d_rsqrt(y, 0, 1)
                        split_late(2, 3)
                        add_bias(y, 0)
                        d_rsqrt(y, 1, 1)
                        split_late(3, 4)
                        add_bias(y, 1)
                    else:
                        for g in range(GB):
                            d_rsqrt(y, g, 1)
                        for g in range(GB):
                            add_bias(y, g)
                    for g in range(GB):
                        d_rsqrt(y, g, 2)
                    if last_turn:
                        split_late(4, 6)
                    for g in range(GB):
                        d_rsqrt(y, g, 3)
            split_late(6, LATE)
            stage_end(pool, END_3)

            pool.memset(strictly_lower[:], 1.0)
            pool.memset(ones5[:], 1.0)
            pool.iota(iota_e[:], pattern=[[1, E]], base=0, channel_multiplier=0,
                      allow_small_or_imprecise_dtypes=True)
            pool.iota(iota_p[:], pattern=[[1, P]], base=0, channel_multiplier=0,
                      allow_small_or_imprecise_dtypes=True)
            pool.iota(iota_j[:], pattern=[[1, TILES]], base=0, channel_multiplier=0,
                      allow_small_or_imprecise_dtypes=True)
            pool.iota(code_in[:], pattern=[[0, NT], [1, K]], base=1, channel_multiplier=K,
                      allow_small_or_imprecise_dtypes=True)
            pool.iota(code_tile[:], pattern=[[K * P, NT], [0, K]], base=0, channel_multiplier=0,
                      allow_small_or_imprecise_dtypes=True)
            pool.iota(pad_row[:], pattern=[[0, 1]], base=SLOTS + 1, channel_multiplier=1,
                      allow_small_or_imprecise_dtypes=True)
            pool.drain()
            pool.affine_select(out=strictly_lower[:], in_=strictly_lower[:], compare_op=ALU.is_gt, fill=0.0,
                               base=0, pattern=[[1, P]], channel_multiplier=-1)
            pool.drain().then_inc(r_const, 1)
            for k in range(EBLK):
                split_block(E - 1, ORDER[E - 1], k)

            def gather(j, u):
                wait_alone(pool, m_src, j + 1)
                pool.indirect_dma_start(
                    out=rows_in[:, u, :], out_offset=None, in_=split_rows,
                    in_offset=bass.IndirectOffsetOnAxis(ap=src_now[:, u:u + 1], axis=0)).then_inc(m_rows[u], 16)

            def scatter(j, u, before):
                wait_alone(pool, m_y, j + 1)
                if before is not None:
                    wait_alone(pool, m_out[(u - 1) % U], before)
                pool.indirect_dma_start(
                    out=choice_rows, out_offset=bass.IndirectOffsetOnAxis(ap=dst_now[:, u:u + 1], axis=0),
                    in_=rows_out[:, u, :], in_offset=None).then_inc(m_out[u], 16)

            for j in range(TURN):
                gather(j, j % U)
            scatter(0, 0, None)
            gather(TURN, 0)
            with pool.Fori(0, TILES // U - 3) as i:
                for k in range(1, U + 1):
                    scatter(U * i + k, k % U, 16 * (i + 1))
                    gather(U * i + k + TURN, k % U)
            for j in range(TILES - 3 * U + 1, TILES):
                scatter(j, j % U, 16 * ((j - 1) // U + 1))
                if j + TURN < TILES:
                    gather(j + TURN, j % U)
            for u in range(U):
                pool.wait_ge(m_out[u], 16 * (TILES // U))
            stage_end(pool, END_5)

        @block.scalar
        def _(act):
            def high_block(n, e, k):
                act.wait_ge(block_in[k % 2], 16 * ((EBLK // 2) * n + k // 2 + 1))
                act.activation(block_parts(e, k)[0], block_in_buffer(k), ACT.Copy).then_inc(block_high, 1)

            su_to = {
                0: lambda at: (act.activation(ctxT.rearrange("p c b k -> p (c b k)"), at[:, 0:DC * B * C], ACT.Copy),),
                3: lambda at: (act.activation(tqT[:].rearrange("p b c k -> p (b c k)"), at[:, 0:DC * B * C], ACT.Copy),),
                4: lambda at: (act.activation(w_sum, at[:, 0:2], ACT.Copy),),
                9: lambda at: (act.activation(expert_b1[:], at[:, 0:E * HC], ACT.Copy),
                               act.activation(f1b_s[:], at[:, E * HC:E * HC + DC], ACT.Copy)),
                10: lambda at: (act.activation(K2T.rearrange("p c k -> p (c k)"), at[:, 0:DC * B * C], ACT.Copy),),
                11: lambda at: (act.activation(V2[:].rearrange("p b d -> p (b d)"), at[0:C, :], ACT.Copy),),
                12: lambda at: (act.activation(M1[:].rearrange("p c d -> p (c d)"), at, ACT.Copy),),
                13: lambda at: (act.activation(A2.rearrange("p c k -> p (c k)"), at[:, 0:DC * B * C], ACT.Copy,
                                               scale=float(C) ** -0.5),),
            }

            def su_copy(n):
                act.wait_ge(su_psum, n + 1)
                at = bank(6 + n % 2)
                if n in su_to:
                    su_to[n](at)
                elif n in SU_TRANSPOSED:
                    act.activation(raw[SU_TRANSPOSED[n] + "T"].rearrange("p c d -> p (c d)"), at, ACT.Copy)
                elif n == 14:
                    for b in range(B):
                        act.activation(WVA[:, b, :, D:DV], at[:, 0:DC * B * C].rearrange(
                            "p (c b k) -> p c b k", c=DC, b=B)[:, :, b, :], ACT.Copy)
                        act.activation(WVA[:, b, :, 0:D], raw["Wv1"], ACT.Copy)
                elif n < 17:
                    act.activation(T1[:, n - 15, :], bank16(6 + n % 2), ACT.Copy)
                else:
                    m = 4 * (n - 17)
                    act.activation(T2[:, m:m + 4, :].rearrange("p m d -> p (m d)"), bank16(6 + n % 2), ACT.Copy)
                act.drain().then_inc(su_copied, 1)

            def a_copy(g, what, dst, n, done):
                for c in range(n):
                    a_ring.wait(act, 0, g, what, c)
                    src = a_ring.bank(0, g, what, c)[0:dst(c).shape[0], :]
                    act.activation(dst(c), src.bitcast(BF16) if what == "qT" else src, ACT.Copy
                                   ).then_inc(a_ring.free(0, g, what, c), 1)
                act.drain().then_inc(done, 1)

            act.wait_ge(in_gates, 32)
            act.activation(gates[:], graw[:], ACT.Tanh).then_inc(gates_made, 1)
            su_copy(0)
            su_copy(1)
            su_copy(3)
            for g in range(NG):
                a_copy(g, "hT", lambda c: hT[:, g, c, :], DC, a_hT)
            act.wait_ge(in_w12, 32)
            act.activation(t1_s.rearrange("p a b -> p (a b)"), w1_s.rearrange("p a b -> p (a b)"), ACT.Abs,
                           accum_out=w_abs[:, 0:1])
            act.activation(t2_s.rearrange("p a b -> p (a b)"), w2_s.rearrange("p a b -> p (a b)"), ACT.Abs,
                           accum_out=w_abs[:, 1:2])
            act.drain().then_inc(su_abs, 1)
            su_copy(4)
            for g in range(NG):
                act.wait_ge(a_shifted, g + 1)
                act.activation(probs[:, g, :, :], probs[:, g, :, :], ACT.Exp).then_inc(a_probs, 1)
            for g in range(NG):
                a_copy(g, "pT", lambda c: probsT[:, g, :], 1, a_pT)
            for g in range(NG):
                act.wait_ge(a_total, g + 1)
                for h in range(2):
                    a_ring.wait(act, 0, g, "att", h)
                    for j in (2 * h, 2 * h + 1):
                        last = act.activation(h1[:, g, j, :],
                                              a_ring.bank(0, g, "att", h)[:, (j % 2) * D:(j % 2 + 1) * D],
                                              ACT.Relu, scale=total[:, g, j:j + 1])
                    last.then_inc(a_ring.free(0, g, "att", h), 1)
                act.drain().then_inc(a_relu, 1)
            for n in range(5, 15):
                su_copy(n)
            act.wait_ge(in_b1, 16)
            act.activation(b1_parts[:, 0, :], b1_s, ACT.Copy).then_inc(b1_high, 1)
            for n, (w_s, t_s) in enumerate(((w1_s, t1_s), (w2_s, t2_s))):
                act.wait_ge(su_rounded, n + 1)
                act.activation(t_s.rearrange("p a b -> p (a b)"), w_s.rearrange("p a b -> p (a b)"), ACT.Sign,
                               bias=minus_magic[:]).then_inc(su_tern, 1)
            act.wait_ge(b1_left, 1)
            act.activation(b1_parts[:, 1, :], b1_rest, ACT.Copy).then_inc(b1_high, 1)
            for n in range(15, 19):
                su_copy(n)
            for g in range(NG):
                a_copy(g, "qT", lambda c: q1T[:, g, :, :].rearrange("p c n -> p (c n)"), 1, a_qT)
            act.wait_ge(a_inverseT_psum, 1)
            for k in range(2):
                act.activation(inverseT[:, k * 8 * P:(k + 1) * 8 * P], bank16(6 + k)[0:9, :], ACT.Copy)
            stage_end(act, END_1)

            def gelu(t, u):
                act.wait_ge(f_hidden, t + 1)
                act.activation(y2[:, u, :], ps[:, 2 * u:2 * u + 2, :].rearrange("p a n -> p (a n)"),
                               ACT.Gelu, scale=scale1[:, bass.ds(t, 1)],
                               accum_out=ysum[:, u:u + 1]).then_inc(f_gelu, 1)

            def square(t, u):
                act.wait_ge(f_mean, t + 1)
                act.activation(square_out[:, u, :], y2[:, u, :], ACT.Square, bias=neg_mean[:, u:u + 1],
                               accum_out=ysq[:, u:u + 1]).then_inc(f_sq, 1)

            def stage2_tile(t, u, ahead, e, k):
                high_block(e, e, k)
                if ahead >= 2:
                    square(t + 2, u)
                act.wait_ge(f_qT_psum, t + 1)
                act.activation(q2T[:, u, :, :].rearrange("p m n -> p (m n)"), bank16(4 + u),
                               ACT.Copy).then_inc(f_qT, 1)
                if ahead >= 3:
                    gelu(t + 3, 1 - u)

            def c_copy_nT(b, g):
                act.wait_ge(c_nT_psum, GB * b + g + 1)
                for c in range(DC):
                    last = act.activation(nT[:, c, g * 512:(g + 1) * 512], bank(DC * g + c), ACT.Copy)
                last.then_inc(c_nT, 1)

            gelu(0, 0)
            gelu(1, 1)
            square(0, 0)
            square(1, 1)
            act.drain()
            gelu(2, 0)
            with act.Fori(0, NT // EBLK - 1) as e:
                for k in range(EBLK):
                    stage2_tile(EBLK * e + k, k % 2, 3, e, k)
            for k in range(EBLK):
                t = NT - EBLK + k
                stage2_tile(t, k % 2, NT - 1 - t, NT // EBLK - 1, k)
            c_copy_nT(0, 0)
            c_copy_nT(0, 1)
            stage_end(act, END_2)

            def c_copy_qm(b, k):
                o, g = k % DC, k // DC
                act.wait_ge(c_qm_psum, DC * GB * b + k + 1)
                act.activation(QmT[:, o, g * 512:(g + 1) * 512], bank((4 + k) % 5), ACT.Copy,
                               scale=float(S) ** -0.5).then_inc(c_qm, 1)

            def c_copy_vp(b, i):
                act.wait_ge(c_vp_psum, TB * b + i + 1)
                act.activation(VP[:, i, :], bank((8 + i) % 5)[:, 0:DV], ACT.Copy).then_inc(c_vp, 1)

            def c_tile(b, i):
                L = (i + 1) * P
                act.wait_ge(c_max, TB * b + i + 1)
                if i:
                    act.wait_ge(c_pT_psum, TB * b + i)
                act.activation(Pr[:, 0:L], ps[:, 0:2, :].rearrange("p a n -> p (a n)")[:, 0:L], ACT.Exp,
                               bias=negmax[:, i:i + 1], accum_out=rowsum[:, i:i + 1]).then_inc(c_exp, 1)
                act.wait_ge(c_pT_psum, TB * b + i + 1)
                act.activation(PT[:, 0:L], ps[:, 2:4, :].rearrange("p a n -> p (a n)")[:, 0:L],
                               ACT.Copy).then_inc(c_pT, 1)

            def d_exponential(b, g):
                act.wait_ge(d_shift, GB * b + g + 1)
                act.activation(s2raw[:, b, g, :, :], s2raw[:, b, g, :, :], ACT.Exp).then_inc(d_exp, 1)

            def d_copy(b, g, what, dst, n, done, **how):
                for c in range(n):
                    d_ring(b).wait(act, d_turn(b), g, what, c)
                    src = d_ring(b).bank(d_turn(b), g, what, c)
                    bias = {"bias": how["bias"][:, c:c + 1]} if how else {}
                    act.activation(dst(c), src[0:dst(c).shape[0], :], ACT.Identity if how else ACT.Copy, **bias
                                   ).then_inc(d_ring(b).free(d_turn(b), g, what, c), 1)
                act.drain().then_inc(done, 1)

            def d_copy_pT(b, g):
                d_copy(b, g, "pT", lambda c: p2T[:, g, :], 1, d_pT)

            def d_copy_nT(b, g):
                d_copy(b, g, "nT", lambda c: ffT[:, g, c, :], DC, d_nT)

            def d_copy_pre(b, g):
                if b:
                    act.wait_ge(d_stored, 16 * GB * b)
                d_copy(b, g, "pre", lambda c: preT[:, g, c, :], DC, d_pre, bias=f1b_s)

            def d_copy_n4T(b, g):
                d_copy(b, g, "n4T", lambda c: ffT[:, g, c, :], DC, d_n4T)

            def d_relu_norm3(b, g):
                act.wait_ge(d_norm3, GB * b + g + 1)
                act.activation(acc[:, b, g, :, :], acc[:, b, g, :, :], ACT.Relu).then_inc(d_relu, 1)

            def d_high(b, g):
                act.wait_ge(d_n4, GB * b + g + 1)
                act.activation(split3[:, g, :, 0:D], acc[:, b, g, :, :], ACT.Copy).then_inc(d_hi, 1)

            for b in range(B):
                y = b - 1
                if y >= 0:
                    d_exponential(y, 0)
                if b:
                    c_copy_nT(b, 0)
                    c_copy_nT(b, 1)
                if y >= 0:
                    d_exponential(y, 1)
                    d_copy_pT(y, 0)
                c_copy_qm(b, 0)
                c_copy_qm(b, 1)
                if y >= 0:
                    d_copy_pT(y, 1)
                c_copy_qm(b, 2)
                c_copy_qm(b, 3)
                for i in range(TB):
                    c_copy_vp(b, i)
                for i in range(TB):
                    if y < 0 and i % 2:
                        high_block(EARLY - 1, EARLY - 1, i // 2)
                    c_tile(b, i)
                    if y < 0:
                        continue
                    if i < 2:
                        d_copy_nT(y, i)
                    elif i == 2:
                        d_copy_pre(y, 0)
                    elif i == 3:
                        d_copy_pre(y, 1)
                    elif i == 5:
                        d_relu_norm3(y, 0)
                    elif i == 6:
                        d_relu_norm3(y, 1)
                    elif i == 7:
                        d_high(y, 0)
                        d_high(y, 1)
                if y >= 0:
                    d_copy_n4T(y, 0)
                    d_copy_n4T(y, 1)
            def high_late(first, end):
                for at in range(first, end):
                    n = EARLY + at // EBLK
                    high_block(n, ORDER[n], at % EBLK)

            y = B - 1
            for part in (d_exponential, d_copy_pT):
                for g in range(GB):
                    part(y, g)
            act.wait_ge(c_acc, TB * B)
            high_late(0, 4)
            d_copy_nT(y, 0)
            d_copy_pre(y, 0)
            high_late(4, 5)
            d_copy_nT(y, 1)
            d_copy_pre(y, 1)
            high_late(5, 6)
            for g in range(GB):
                d_relu_norm3(y, g)
            high_late(6, LATE)
            for g in range(GB):
                d_high(y, g)
                d_copy_n4T(y, g)
            stage_end(act, END_3)

            act.wait_ge(r_shift, 1)
            act.activation(pe_exp[:], pe_exp[:], ACT.Exp).then_inc(r_exp, 1)
            act.wait_ge(r_cT_psum, 1)
            for n in range(NT // 4):
                last = act.activation(combineT[:, 4 * n:4 * n + 4, :].rearrange("e t p -> e (t p)"),
                                      ps[0:E, 4 + n, :], ACT.Copy)
            last.then_inc(r_cT, 1)
            for k in range(EBLK):
                high_block(E - 1, ORDER[E - 1], k)

            def hidden(j, v, e):
                act.wait_ge(m_hid_psum, j + 1)
                for m in range(HC):
                    last = act.activation(hid[:, v, m * P:(m + 1) * P],
                                          bank(2 + 2 * v + m // 4)[:, (m % 4) * P:(m % 4 + 1) * P],
                                          ACT.Gelu_apprx_tanh, bias=expert_b1[:, bass.ds(e * HC + m, 1)])
                last.then_inc(m_hid, 1)

            def expert_of(j):
                return act.value_load(tile_expert[0:1, bass.ds(j, 1)], min_val=0, max_val=E - 1)

            act.wait_ge(r_expert, 1)
            with act.Fori(0, TILES // TURN) as i:
                for q in range(TURN):
                    hidden(TURN * i + q, q % 2, expert_of(TURN * i + q))
            for j in range(TILES // TURN * TURN, TILES):
                hidden(j, j % 2, expert_of(j))
            stage_end(act, END_5)

        @block.vector
        def _(dve):
            def group_moments(tile_of, k, done):
                for j in range(G):
                    dve.bn_stats(stats[:, j, :], tile_of(j))
                dve.drain()
                for j in range(G):
                    dve.bn_aggr(moments[:, k, j, :], stats[:, j, :])
                dve.drain().then_inc(done, 1)

            def normalise(out_of, tile_of, k):
                for j in range(G):
                    dve.tensor_scalar(out_of(j), tile_of(j), moments[:, k, j, 0:1], rstd[:, k, j:j + 1],
                                      ALU.subtract, ALU.mult)
                dve.drain()

            def res_tile(g):
                return lambda j: res[:, G * g + j, :]

            for g in range(NG):
                dve.wait_ge(in_x[g], 16)
                group_moments(res_tile(g), g, a_moments)
            for g in range(NG):
                dve.wait_ge(a_rstd, g + 1)
                normalise(lambda j: h1[:, g, j, :], res_tile(g), g)
                dve.drain().then_inc(a_h, 1)
                if g == 0:
                    dve.wait_ge(su_psum, 3)
                    dve.tensor_tensor(tq[:], bank(6)[0:C, :].rearrange("p (b d) -> p b d", b=B),
                                      Wb_s[0:C, :].unsqueeze(1).to_broadcast([C, B, D]), ALU.add)
                    dve.drain().then_inc(su_copied, 1)
            for g in range(NG):
                a_ring.wait(dve, 0, g, "scores")
                sc = a_ring.bank(0, g, "scores")[:, 0:G * C].rearrange("p (j k) -> p j k", j=G)
                dve.tensor_reduce(top[:, g, :], sc, X, ALU.max)
                dve.drain()
                dve.tensor_tensor(probs[:, g, :, :], sc, cols(top[:, g, :], C), ALU.subtract)
                dve.drain().then_inc(a_shifted, 1)
                dve.sem_inc(a_ring.free(0, g, "scores"), 1)
            dve.wait_ge(su_copied, 5)
            dve.tensor_scalar(wscale[:], w_sum, 1.0 / (H * D), 1e-5, ALU.mult, ALU.max)
            dve.drain()
            dve.reciprocal(wscale_inv[:], wscale[:])
            dve.tensor_scalar(wscale_127[:], wscale[:], 1.0 / 127.0, None, ALU.mult)
            dve.drain().then_inc(su_scale, 1)
            for g in range(NG):
                dve.wait_ge(a_probs, g + 1)
                dve.tensor_reduce(total[:, g, :], probs[:, g, :, :], X, ALU.add)
                dve.drain()
                dve.reciprocal(total[:, g, :], total[:, g, :])
                dve.drain().then_inc(a_total, 1)
            dve.wait_ge(in_vec, 48)
            for g in range(NG):
                r = res[:, G * g:G * (g + 1), :]
                dve.wait_ge(a_relu, g + 1)
                dve.scalar_tensor_tensor(r, h1[:, g, :, :], gates[:, 0:1], r, ALU.mult, ALU.add)
                dve.drain()
                group_moments(res_tile(g), g, a_moments)
                for j in range(G):
                    last = dve.scalar_tensor_tensor(h1[:, g, j, :], res[:, G * g + j, :],
                                                    moments[:, g, j, 0:1], ln1_g_s[:], ALU.subtract, ALU.mult)
                last.then_inc(a_centred, 1)
            for g in range(NG):
                dve.wait_ge(a_rstd, NG + g + 1)
                u, at = h1[:, g, :, :], slice(G * g, G * (g + 1))
                for j in range(G):
                    dve.scalar_tensor_tensor(h1[:, g, j, :], h1[:, g, j, :], rstd[:, g, j:j + 1], ln1_b_s[:],
                                             ALU.mult, ALU.add)
                dve.drain()
                dve.tensor_reduce(top[:, g, :], u, X, ALU.max, apply_absolute_value=True)
                dve.drain()
                dve.tensor_scalar(top[:, g, :], top[:, g, :], 1e-5, None, ALU.max)
                dve.drain()
                dve.reciprocal(sx1[:, g, :], top[:, g, :])
                dve.tensor_scalar(scale1[:, at], top[:, g, :], wscale_127[:, 0:1], None, ALU.mult)
                dve.drain()
                dve.tensor_scalar(sx1[:, g, :], sx1[:, g, :], 127.0, None, ALU.mult)
                dve.drain()
                dve.tensor_scalar(inverse1[:, at], sx1[:, g, :], wscale_inv[:, 0:1], None, ALU.mult)
                for j in range(G):
                    last = dve.tensor_scalar(h1[:, g, j, :], h1[:, g, j, :], sx1[:, g, j:j + 1], MAGIC,
                                             ALU.mult, ALU.add)
                last.then_inc(a_rounded, 1)
            dve.drain()
            rest = inverse_rest[:]
            dve.tensor_copy(inverse_parts[:, :, :, 0], cols(inverse1[:], 3))
            dve.drain()
            dve.tensor_tensor(rest, inverse1[:], inverse_parts[:, :, 0, 0], ALU.subtract)
            dve.drain()
            dve.tensor_copy(inverse_parts[:, :, :, 1], cols(rest, 3))
            dve.drain()
            dve.tensor_tensor(inverse_parts[:, :, :, 2], cols(rest, 3), inverse_parts[:, :, :, 1], ALU.subtract
                              ).then_inc(a_inverse, 1)
            dve.wait_ge(a_b2, NG)
            stage_end(dve, END_1)

            dve.wait_ge(in_vec2, 32)

            def finish(t, u):
                dve.wait_ge(f_y, t + 1)
                r = res[:, bass.ds(t, 1), :].rearrange("p o d -> p (o d)")
                dve.scalar_tensor_tensor(r, bank(6 + u)[:, 0:D], outscale[:, u:u + 1], r, ALU.mult, ALU.add)

            def start_row(t, u):
                dve.wait_ge(f_gelu, t + 1)
                dve.tensor_scalar(neg_mean[:, u:u + 1], ysum[:, u:u + 1], -1.0 / H, None, ALU.mult
                                  ).then_inc(f_mean, 1)

            def centre(t, u, reused):
                if reused:
                    dve.wait_ge(f_q, t - 1)
                dve.scalar_tensor_tensor(v2[:, u, :], y2[:, u, :], neg_mean[:, u:u + 1], ln2_g_s,
                                         ALU.add, ALU.mult)

            def hidden_row(t, u, ahead, reused, before):
                if ahead >= 1:
                    start_row(t + 1, 1 - u)
                v = v2[:, u, :]
                dve.drain()
                dve.wait_ge(f_rstd, t + 1)
                dve.scalar_tensor_tensor(v, v, rstd2[:, u:u + 1], ln2_b_s, ALU.mult, ALU.add)
                if ahead >= 1:
                    centre(t + 1, 1 - u, reused)
                if before:
                    finish(t - 2, u)
                dve.drain()
                dve.tensor_reduce(vmax[:, u:u + 1], v, X, ALU.max, apply_absolute_value=True)
                dve.drain()
                dve.tensor_scalar(vmax[:, u:u + 1], vmax[:, u:u + 1], 1e-5, 1.0 / 127.0, ALU.max, ALU.mult)
                dve.drain()
                dve.reciprocal(sx2[:, u:u + 1], vmax[:, u:u + 1])
                dve.tensor_scalar(outscale[:, u:u + 1], vmax[:, u:u + 1], wscale[:, 1:2], gates[:, 2:3],
                                  ALU.mult, ALU.mult)
                dve.drain()
                dve.tensor_scalar(v, v, sx2[:, u:u + 1], MAGIC, ALU.mult, ALU.add).then_inc(f_scaled, 1)

            def c_moments_of(b, g):
                group_moments(lambda j: res[:, TB * b + G * g + j, :], g, c_moments)

            def c_normalise(b, g):
                dve.wait_ge(c_rstd, GB * b + g + 1)
                normalise(lambda j: n3[:, G * g + j, :], lambda j: res[:, TB * b + G * g + j, :], g)
                dve.drain().then_inc(c_n, 1)

            start_row(0, 0)
            dve.drain()
            centre(0, 0, False)
            dve.drain()
            hidden_row(0, 0, 3, False, False)
            hidden_row(1, 1, 3, True, False)
            with dve.Fori(1, (NT - G) // 2) as i:
                hidden_row(2 * i, 0, 3, True, True)
                hidden_row(2 * i + 1, 1, 3, True, True)
            for t in range(NT - G, NT):
                hidden_row(t, t % 2, NT - 1 - t, True, True)
            c_moments_of(0, 0)
            c_moments_of(0, 1)
            c_normalise(0, 0)
            c_normalise(0, 1)
            finish(NT - 2, 0)
            finish(NT - 1, 1)
            stage_end(dve, END_2)

            dve.wait_ge(in_late, 16 * 8)

            def c_attended(b, i):
                g, j = i // G, i % G
                dve.wait_ge(c_att, TB * b + i + 1)
                dve.reciprocal(rowinv[:, i:i + 1], rowsum[:, i:i + 1])
                dve.drain()
                o = bank(4)
                dve.scalar_tensor_tensor(acc[:, b, g, j, :], o[:, 0:D], rowinv[:, i:i + 1], n3[:, i, :],
                                         ALU.mult, ALU.add)
                dve.tensor_scalar(s2raw[:, b, g, j, :], o[:, D:DV], rowinv[:, i:i + 1], None, ALU.mult
                                  ).then_inc(c_acc, 1)

            def c_tile(b, i):
                L = (i + 1) * P
                dve.wait_ge(c_scores, TB * b + i + 1)
                dve.tensor_reduce(negmax[:, i:i + 1], ps[:, 0:2, :].rearrange("p a n -> p (a n)")[:, 0:L],
                                  X, ALU.max, negate=True).then_inc(c_max, 1)
                if i:
                    c_attended(b, i - 1)

            def d_shift_scores(b, g):
                dve.drain()
                dve.tensor_reduce(top3[:, g, :], s2raw[:, b, g, :, :], X, ALU.max)
                dve.drain()
                dve.tensor_tensor(s2raw[:, b, g, :, :], s2raw[:, b, g, :, :], cols(top3[:, g, :], C),
                                  ALU.subtract).then_inc(d_shift, 1)

            def norm_start(b, g):
                group_moments(lambda j: acc[:, b, g, j, :], GB + g, d_moments[g])
                for j in range(G):
                    a = acc[:, b, g, j, :]
                    dve.scalar_tensor_tensor(a, a, moments[:, GB + g, j, 0:1], gamma_s[:],
                                             ALU.subtract, ALU.mult)

            def norm_end(b, g, n):
                dve.drain()
                dve.wait_ge(d_rstd[g], 4 * b + n + 1)
                for j in range(G):
                    a = acc[:, b, g, j, :]
                    dve.scalar_tensor_tensor(a, a, rstd[:, GB + g, j:j + 1], beta_s[:], ALU.mult, ALU.add)

            def halves(b, g, what):
                for h in range(2):
                    d_ring(b).wait(dve, d_turn(b), g, what, h)
                    yield h, d_ring(b).bank(d_turn(b), g, what, h), d_ring(b).free(d_turn(b), g, what, h)

            def d_attended(b, g):
                dve.wait_ge(d_exp, GB * b + g + 1)
                dve.tensor_reduce(total3[:, g, :], s2raw[:, b, g, :, :], X, ALU.add)
                dve.drain()
                dve.reciprocal(total3[:, g, :], total3[:, g, :])
                dve.drain()
                for h, at, read in halves(b, g, "att"):
                    for j in (2 * h, 2 * h + 1):
                        a = acc[:, b, g, j, :]
                        last = dve.scalar_tensor_tensor(a, at[:, (j % 2) * D:(j % 2 + 1) * D],
                                                        total3[:, g, j:j + 1], a, ALU.mult, ALU.add)
                    last.then_inc(read, 1)
                dve.drain()

            def d_norm1_to_norm2(b, g):
                norm_end(b, g, 0)
                d_attended(b, g)
                norm_start(b, g)

            def d_end_norm2(b, g):
                norm_end(b, g, 1)
                dve.drain().then_inc(d_norm2, 1)

            def d_leaky_relu(b, g):
                dve.wait_ge(d_pre, GB * b + g + 1)
                dve.scalar_tensor_tensor(ffT[:, g, :, :], preT[:, g, :, :], 0.2, preT[:, g, :, :],
                                         ALU.mult, ALU.max).then_inc(d_hT, 1)

            def d_fed_forward(b, g):
                dve.wait_ge(d_bias, GB * b + g + 1)
                for h, at, read in halves(b, g, "ff"):
                    a = acc[:, b, g, 2 * h:2 * h + 2, :].rearrange("p j d -> p (j d)")
                    dve.tensor_tensor(a, at, a, ALU.add).then_inc(read, 1)
                dve.drain()
                norm_start(b, g)

            def d_end_norm3(b, g):
                norm_end(b, g, 2)
                dve.drain().then_inc(d_norm3, 1)

            def d_to_stream(b, g):
                r = res[:, TB * b + G * g:TB * b + G * (g + 1), :]
                dve.wait_ge(d_relu, GB * b + g + 1)
                dve.scalar_tensor_tensor(r, acc[:, b, g, :, :], gates[:, 1:2], r, ALU.mult, ALU.add)
                dve.drain()
                group_moments(lambda j: res[:, TB * b + G * g + j, :], GB + g, d_moments[g])

            def d_norm4(b, g):
                dve.wait_ge(d_rstd[g], 4 * b + 4)
                normalise(lambda j: acc[:, b, g, j, :], lambda j: res[:, TB * b + G * g + j, :], GB + g)
                dve.drain().then_inc(d_n4, 1)

            def d_low(b, g):
                dve.wait_ge(d_hi, GB * b + g + 1)
                dve.tensor_tensor(split3[:, g, :, D:2 * D], acc[:, b, g, :, :], split3[:, g, :, 0:D],
                                  ALU.subtract).then_inc(d_lo, 1)

            def d_logits(b, g):
                d_ring(b).wait(dve, d_turn(b), g, "logits")
                t = TB * b + G * g
                dve.tensor_tensor(logits[:, t:t + G, :],
                                  d_ring(b).bank(d_turn(b), g, "logits")[:, 0:G * E].rearrange("p (j e) -> p j e", j=G),
                                  rows4(bg_s[:]), ALU.add).then_inc(d_ring(b).free(d_turn(b), g, "logits"), 1)

            for b in range(B):
                y = b - 1
                if b:
                    c_moments_of(b, 0)
                    c_moments_of(b, 1)
                if y >= 0:
                    d_shift_scores(y, 0)
                if b:
                    c_normalise(b, 0)
                    c_normalise(b, 1)
                if y >= 0:
                    d_shift_scores(y, 1)
                    norm_start(y, 0)
                    norm_start(y, 1)
                    d_norm1_to_norm2(y, 0)
                    d_norm1_to_norm2(y, 1)
                for i in range(TB):
                    c_tile(b, i)
                    if y < 0:
                        continue
                    if i < 2:
                        d_end_norm2(y, i)
                    elif i == 3:
                        d_leaky_relu(y, 0)
                    elif i == 4:
                        d_leaky_relu(y, 1)
                        d_fed_forward(y, 0)
                    elif i == 5:
                        d_fed_forward(y, 1)
                        d_end_norm3(y, 0)
                    elif i == 6:
                        d_end_norm3(y, 1)
                        d_to_stream(y, 0)
                        d_to_stream(y, 1)
                    elif i == 7:
                        d_norm4(y, 0)
                        d_norm4(y, 1)
                c_attended(b, TB - 1)
                if y >= 0:
                    d_low(y, 0)
                    d_low(y, 1)
                    d_logits(y, 0)
                    d_logits(y, 1)
            y = B - 1
            for g in range(GB):
                d_shift_scores(y, g)
            for g in range(GB):
                norm_start(y, g)
            for g in range(GB):
                d_norm1_to_norm2(y, g)
                d_end_norm2(y, g)
            d_leaky_relu(y, 0)
            d_fed_forward(y, 0)
            d_leaky_relu(y, 1)
            d_end_norm3(y, 0)
            d_fed_forward(y, 1)
            d_to_stream(y, 0)
            d_end_norm3(y, 1)
            d_norm4(y, 0)
            d_to_stream(y, 1)
            d_low(y, 0)
            d_norm4(y, 1)
            d_low(y, 1)
            for g in range(GB):
                d_logits(y, g)
            stage_end(dve, END_3)

            dve.tensor_reduce(gsum[:], logits[:], X, ALU.max)
            dve.drain()
            dve.tensor_tensor(pe_exp[:], logits[:], cols(gsum[:], E), ALU.subtract).then_inc(r_shift, 1)
            dve.wait_ge(r_exp, 1)
            dve.tensor_reduce(gsum[:], pe_exp[:], X, ALU.add)
            for t in range(NT):
                dve.max(gtop[:, t, :], pe_exp[:, t, :])
            dve.drain()
            for t in range(NT):
                dve.max_index(gidx[:, t, :], gtop[:, t, :], pe_exp[:, t, :])
            dve.tensor_reduce(denom[:], gtop[:, :, 0:K], X, ALU.add)
            dve.drain()
            dve.scalar_tensor_tensor(denom[:], gsum[:], 1e-8, denom[:], ALU.mult, ALU.add)
            dve.tensor_copy(gidx_f[:], gidx[:, :, 0:K])
            dve.drain()
            dve.reciprocal(denom[:], denom[:])
            dve.wait_ge(r_const, 1)
            for k in range(K):
                dve.tensor_tensor(onehot[:, :, k, :], iota_e[:].unsqueeze(1).to_broadcast([P, NT, E]),
                                  cols(gidx_f[:, :, k], E), ALU.is_equal)
            dve.drain()
            dve.tensor_tensor(count[:], onehot[:, :, 0, :], onehot[:, :, 1, :], ALU.add).then_inc(r_count, 1)
            dve.tensor_tensor(weight[:], gtop[:, :, 0:K], cols(denom[:], K), ALU.mult)
            dve.drain()
            dve.tensor_scalar(weight[:], weight[:], gates[:, 3:4], None, ALU.mult)
            dve.drain()
            dve.tensor_tensor(picked[:], onehot[:], cols(weight[:], E), ALU.mult)
            dve.drain()
            dve.tensor_tensor(combine[:], picked[:, :, 0, :], picked[:, :, 1, :], ALU.add).then_inc(r_combine, 1)
            dve.wait_ge(r_prefix, 1)
            dve.tensor_copy(tiles_upto[:, 0, :, :].rearrange("p t e -> p (t e)"), bank(1)[:, 0:NT * E])
            dve.drain()
            a, shift = 0, 1
            while shift < NT:
                dve.tensor_copy(tiles_upto[:, 1 - a, 0:shift, :], tiles_upto[:, a, 0:shift, :])
                dve.tensor_tensor(tiles_upto[:, 1 - a, shift:NT, :], tiles_upto[:, a, shift:NT, :],
                                  tiles_upto[:, a, 0:NT - shift, :], ALU.add)
                dve.drain()
                a, shift = 1 - a, 2 * shift
            upto = tiles_upto[:, a, :, :]
            dve.tensor_scalar(etiles[:], upto[:, NT - 1, :], 1.0 / P, (P - 1.0) / P - 0.5 + 0.5 / P,
                              ALU.mult, ALU.add)
            dve.drain()
            dve.tensor_scalar(etiles[:], etiles[:], MAGIC, -MAGIC, ALU.add, ALU.add)
            dve.drain()
            dve.tensor_copy(eend[:, 0, :], etiles[:])
            dve.drain()
            a2, shift = 0, 1
            while shift < E:
                dve.tensor_copy(eend[:, 1 - a2, 0:shift], eend[:, a2, 0:shift])
                dve.tensor_tensor(eend[:, 1 - a2, shift:E], eend[:, a2, shift:E], eend[:, a2, 0:E - shift], ALU.add)
                dve.drain()
                a2, shift = 1 - a2, 2 * shift
            ends = eend[:, a2, :]
            dve.tensor_tensor(ended[:], cols(iota_j[:], E), ends.unsqueeze(1).to_broadcast([P, TILES, E]),
                              ALU.is_ge)
            dve.tensor_tensor(etiles[:], ends, etiles[:], ALU.subtract)
            dve.drain()
            dve.tensor_reduce(tile_expert_f[:], ended[:], X, ALU.add)
            dve.tensor_tensor(prefix[:], upto, count_total(ps, NT, E), ALU.subtract)
            dve.drain()
            dve.tensor_scalar(tile_expert[:], tile_expert_f[:], E - 1.0, None, ALU.min)
            dve.tensor_tensor(prefix[:], bank(0)[:, 0:NT * E].rearrange("p (t e) -> p t e", t=NT), prefix[:],
                              ALU.add)
            dve.drain().then_inc(r_expert, 1)
            dve.scalar_tensor_tensor(prefix[:], etiles[:].unsqueeze(1).to_broadcast([P, NT, E]), float(P),
                                     prefix[:], ALU.mult, ALU.add)
            dve.drain()
            dve.tensor_tensor(picked[:], onehot[:], prefix[:].unsqueeze(2).to_broadcast([P, NT, K, E]), ALU.mult)
            dve.drain()
            dve.tensor_reduce(place[:], picked[:], X, ALU.add)
            dve.drain()
            dve.tensor_scalar(place_hi[:], place[:], 1.0 / P, -0.5 + 0.5 / P, ALU.mult, ALU.add)
            dve.drain()
            dve.tensor_scalar(place_hi[:], place_hi[:], MAGIC, -MAGIC, ALU.add, ALU.add)
            dve.drain()
            dve.scalar_tensor_tensor(place_lo[:], place_hi[:], -float(P), place[:], ALU.mult, ALU.add)
            hi_flat = place_hi[:].rearrange("p t k -> p (t k)")
            dve.tensor_tensor(hot_hi[:], iota_j[:].unsqueeze(1).to_broadcast([P, NTK, TILES]),
                              cols(hi_flat, TILES), ALU.is_equal)
            dve.drain()
            for a, part in enumerate((code_in, code_tile)):
                dve.tensor_tensor(coded[:, :, a, :], hot_hi[:], cols(part[:].rearrange("p t k -> p (t k)"), TILES),
                                  ALU.mult)
            lo_flat = place_lo[:].rearrange("p t k -> p (t k)")
            for q in range(NTK // 8):
                if q >= 2:
                    dve.wait_ge(r_hot_used, q - 1)
                dve.tensor_tensor(hot_lo[:, q % 2, :, :], iota_p[:].unsqueeze(1).to_broadcast([P, 8, P]),
                                  cols(lo_flat[:, 8 * q:8 * q + 8], P), ALU.is_equal).then_inc(r_hot, 1)
            dve.wait_ge(r_code, 1)
            dve.tensor_copy(code[:], bank(2)[:, 0:TILES])
            dve.drain()
            dve.tensor_tensor(code[:], bank(2)[:, TILES:2 * TILES], code[:], ALU.add)
            dve.drain()
            dve.tensor_scalar(dst_f[:], code[:], 0.0, pad_row[:, 0:1], ALU.is_equal, ALU.mult)
            dve.tensor_scalar(src_f[:], code[:], 0.5, -0.75, ALU.mult, ALU.add)
            dve.drain()
            dve.tensor_tensor(dst_f[:], dst_f[:], code[:], ALU.add)
            dve.tensor_scalar(src_f[:], src_f[:], MAGIC, -MAGIC, ALU.add, ALU.add)
            dve.drain()
            dve.tensor_scalar(dst_row[:], dst_f[:], -1.0, None, ALU.add)
            dve.tensor_scalar(src_row[:], src_f[:], 0.0, None, ALU.max)
            dve.drain()

            def take_xT(j):
                dve.wait_ge(m_xT_psum, j[0] + 1)
                dve.tensor_copy(xT[:, j[1] % U, :, :, :].rearrange("p a c n -> p (a c n)"),
                                bank16(6 * (j[1] % 2))[:, 0:4 * P]).then_inc(m_xT, 1)

            def name_rows(j):
                dve.tensor_copy(src_now[:, j[1] % U:j[1] % U + 1], src_row[:, bass.ds(j[0], 1)]).then_inc(m_src, 1)

            def split_hidden(j):
                v = j[1] % 2
                dve.wait_ge(m_hid, j[0] + 1)
                hi = hid16[:, v, 0, :, :].rearrange("p m n -> p (m n)")
                lo = hid16[:, v, 1, :, :].rearrange("p m n -> p (m n)")
                dve.tensor_copy(hi, hid[:, v, :])
                dve.drain()
                dve.tensor_tensor(lo, hid[:, v, :], hi, ALU.subtract).then_inc(m_hid16, 1)

            def take_y(j, stored):
                u = j[1] % U
                dve.wait_ge(m_y_psum, j[0] + 1)
                if stored is not None:
                    dve.wait_ge(m_out[u], 16 * stored)
                dve.tensor_copy(dst_now[:, u:u + 1], dst_row[:, bass.ds(j[0], 1)])
                y = bank(1 + 6 * (j[1] % 2))
                dve.tensor_copy(rows_out[:, u, :], y[:, 0:D])
                dve.drain()
                dve.tensor_tensor(rows_out[:, u, :], y[:, D:2 * D], rows_out[:, u, :], ALU.add).then_inc(m_y, 1)

            for j in range(U):
                name_rows((j, j))
            dve.memset(packing[:, 0, TILES:TILES + 8], 0.0)
            dve.tensor_copy(packing[:, 0, 0:TILES], tile_expert[0:1, :])
            for n in range(NT // 4):
                dve.wait_ge(r_b2, n + 1)
                for h in range(2):
                    t = 4 * n + 2 * h
                    r = res[:, t:t + 2, :].rearrange("p j d -> p (j d)")
                    last = dve.tensor_tensor(r, bank(B2_BANKS[n] + h), r, ALU.add)
                last.then_inc(r_b2_in, 1)
            for a in range(3):
                n, held = TILES + 8 - (1 << a), 1 << a
                dve.drain()
                dve.tensor_copy(packing[:, a + 1, n:TILES + 8], packing[:, a, n:TILES + 8])
                dve.scalar_tensor_tensor(packing[:, a + 1, 0:n], packing[:, a, held:TILES + 8],
                                         float(1 << BITS * held), packing[:, a, 0:n], ALU.mult, ALU.add)
            dve.drain()
            dve.tensor_copy(packed[:], packing[:, 3, :]).then_inc(r_packed, 1)
            take_xT((0, 0))
            name_rows((U, U))
            take_xT((1, 1))
            for j in range(TURN):
                take_xT((j + 2, j + 2))
                if j >= 2:
                    take_y((j - 2, j - 2), (j - 2) // U or None)
                name_rows((j + U + 1, j + U + 1))
                split_hidden((j, j))
            with dve.Fori(1, TILES // TURN - 1) as i:
                for q in range(TURN):
                    j = TURN * i + q
                    take_xT((j + 2, q + 2))
                    take_y((j - 2, q + TURN - 2), 2 * i + (q - 2) // U)
                    name_rows((j + U + 1, q + U + 1))
                    split_hidden((j, q))
            for j in range((TILES // TURN - 1) * TURN, TILES):
                if j + 2 < TILES:
                    take_xT((j + 2, j + 2))
                take_y((j - 2, j - 2), (j - 2) // U)
                if j + U + 1 < TILES:
                    name_rows((j + U + 1, j + U + 1))
                split_hidden((j, j))
            for j in (TILES - 2, TILES - 1):
                take_y((j, j), j // U)
            stage_end(dve, END_5)

            for n in range(NT // Z):
                dve.wait_ge(z_in[n], 16)
                for k in range(K):
                    for t in range(Z * n, Z * (n + 1)):
                        dve.scalar_tensor_tensor(res[:, t, :], both[:, t, k, :], weight[:, t, k:k + 1],
                                                 res[:, t, :], ALU.mult, ALU.add)
                    dve.drain()
                dve.drain().then_inc(z_sum, 1)

        @block.tensor
        def _(pe):
            def product(dst, lhsT, rhs, n=DC):
                for c in range(n):
                    last = pe.matmul(dst, lhsT(c), rhs(c), start=(c == 0), stop=(c == n - 1))
                return last

            def transpose_group(bank_of, tile_of):
                for j in range(G):
                    for c in range(DC):
                        last = pe.transpose(bank(bank_of(c))[:, j * P:(j + 1) * P],
                                            tile_of(j)[:, c * P:(c + 1) * P], ident[:])
                return last

            def su_step(n):
                at = bank(6 + n % 2)
                if n == 2:
                    pe.wait_ge(su_copied, 2)
                elif n == 14:
                    pe.wait_ge(su_copied, 14)
                elif n > 2:
                    pe.wait_ge(su_copied, 3 if n == 3 else n - 1)
                if n == 0:
                    for c in range(DC):
                        for b in range(B):
                            k = (c * B + b) * C
                            last = pe.transpose(at[:, k:k + C], ctx_s[:, b, c * P:(c + 1) * P], ident[0:C, 0:C])
                elif n in SU_TRANSPOSED:
                    for c in range(DC):
                        for c2 in range(DC):
                            last = pe.transpose(at[:, c2 * D + c * P:c2 * D + (c + 1) * P],
                                                raw[SU_TRANSPOSED[n]][:, c, c2 * P:(c2 + 1) * P], ident[:])
                elif n == 2:
                    for b in range(B):
                        last = product(at[0:C, b * D:(b + 1) * D], lambda c: ctxT[:, c, b, :],
                                       lambda c: raw["WT"][:, c, :])
                elif n == 3:
                    for b in range(B):
                        for c in range(DC):
                            k = (b * DC + c) * C
                            last = pe.transpose(at[:, k:k + C], tq[:, b, c * P:(c + 1) * P], ident[0:C, 0:C])
                elif n == 4:
                    pe.wait_ge(su_abs, 1)
                    last = pe.matmul(at[:, 0:2], ones, w_abs, start=True, stop=True)
                elif n == 9:
                    last = pe.transpose(at[:, 0:E * HC + DC], bias_rows, ident[0:E * HC + DC, 0:E * HC + DC])
                elif n == 10:
                    for o in range(DC):
                        last = product(at[:, o * B * C:(o + 1) * B * C],
                                       lambda c: raw["Wk2"][:, c, o * P:(o + 1) * P],
                                       lambda c: ctxT[:, c, :, :].rearrange("p b k -> p (b k)"))
                elif n == 11:
                    for b in range(B):
                        last = product(at[0:C, b * D:(b + 1) * D], lambda c: ctxT[:, c, b, :],
                                       lambda c: raw["Wv2"][:, c, :])
                elif n == 12:
                    for o in range(DC):
                        last = product(at[:, o * D:(o + 1) * D], lambda c: raw["Wq1T"][:, c, o * P:(o + 1) * P],
                                       lambda c: raw["Wk1T"][:, c, :])
                elif n == 13:
                    for o in range(DC):
                        last = product(at[:, o * B * C:(o + 1) * B * C],
                                       lambda c: raw["Wq2T"][:, c, o * P:(o + 1) * P], lambda c: K2T[:, c, :])
                elif n == 14:
                    for o in range(DC):
                        last = product(at[:, o * B * C:(o + 1) * B * C],
                                       lambda c: raw["Wv1T"][:, c, o * P:(o + 1) * P], lambda c: A2[:, c, :])
                elif n < 17:
                    c = n - 15
                    pe.wait_ge(su_tern, 1)
                    for m in range(HC):
                        last = pe.transpose(bank16(6 + n % 2)[:, m * P:(m + 1) * P],
                                            t1_s[:, m, c * P:(c + 1) * P], ident16[:])
                else:
                    pe.wait_ge(su_tern, 2)
                    for m in range(4):
                        for c in range(DC):
                            k = (4 * (n - 17) + m) * P
                            last = pe.transpose(bank16(6 + n % 2)[:, m * D + c * P:m * D + (c + 1) * P],
                                                t2_s[:, c, k:k + P], ident16[:])
                last.then_inc(su_psum, 1)

            pe.wait_ge(const_made, 1)
            pe.wait_ge(in_first, 16 * 3)
            for n in range(4):
                su_step(n)
            for g in range(NG):
                pe.wait_ge(a_h, g + 1)
                for c in range(DC):
                    at, full = a_ring.fill(pe, 0, g, "hT", c)
                    for j in range(G):
                        last = pe.transpose(at[:, j * P:(j + 1) * P], h1[:, g, j, c * P:(c + 1) * P], ident[:])
                    last.then_inc(full, 1)
            pe.wait_ge(su_copied, 4)
            for g in range(NG):
                pe.wait_ge(a_hT, g + 1)
                at, full = a_ring.fill(pe, 0, g, "scores")
                for j in range(G):
                    last = product(at[:, j * C:(j + 1) * C], lambda c: hT[:, g, c, j * P:(j + 1) * P],
                                   lambda c: tqT[:, g // GB, c, :])
                last.then_inc(full, 1)
            su_step(4)
            for g in range(NG):
                pe.wait_ge(a_probs, g + 1)
                at, full = a_ring.fill(pe, 0, g, "pT")
                for j in range(G):
                    last = pe.transpose(at[0:C, j * P:(j + 1) * P], probs[:, g, j, :], ident[:])
                last.then_inc(full, 1)
            for g in range(NG):
                pe.wait_ge(a_pT, g + 1)
                for h in range(2):
                    at, full = a_ring.fill(pe, 0, g, "att", h)
                    for j in (2 * h, 2 * h + 1):
                        last = pe.matmul(at[:, (j % 2) * D:(j % 2 + 1) * D], probsT[:, g, j * P:(j + 1) * P],
                                         tq[:, g // GB, :], start=True, stop=True)
                    last.then_inc(full, 1)
            pe.wait_ge(in_w, 16 * 8)
            for n in range(5, 19):
                su_step(n)
            for g in range(NG):
                pe.wait_ge(a_q, g + 1)
                at, full = a_ring.fill(pe, 0, g, "qT")
                for c in range(DC):
                    for j in range(G):
                        last = pe.transpose(at.bitcast(BF16)[:, (c * G + j) * P:(c * G + j + 1) * P],
                                            q1[:, g, j, c * P:(c + 1) * P], ident16[:])
                last.then_inc(full, 1)
            pe.wait_ge(a_inverse, 1)
            pe.wait_ge(su_copied, 19)
            for t in range(NT):
                last = pe.transpose(bank16(6 + t // 8)[0:9, (t % 8) * P:(t % 8 + 1) * P],
                                    inverse_parts[:, t, :, :].rearrange("p a k -> p (a k)"), ident16[:])
            last.then_inc(a_inverseT_psum, 1)
            stage_end(pe, END_1)


            q1T_tiles = q1T[:].rearrange("p g c (j n) -> p g c j n", j=G)

            def first_layer(t, u, j, reused=True):
                if reused:
                    pe.wait_ge(f_gelu, t - 1)
                for n in range(2):
                    pe.matmul(bank(2 * u + n), inverseT[:, bass.ds(t * P, P)], b1_rows[:, n * 512:(n + 1) * 512],
                              start=True, stop=False)
                for c in range(DC):
                    lhsT = q1T_flat(q1T, t, c, j, G, P, DC)
                    for n in range(2):
                        last = pe.matmul(bank(2 * u + n), lhsT, T1[:, c, n * 512:(n + 1) * 512],
                                         start=False, stop=(c == DC - 1))
                last.then_inc(f_hidden, 1)

            def transposes(t, u):
                pe.wait_ge(f_q, t + 1)
                for m in range(HC):
                    last = pe.transpose(bank16(4 + u)[:, m * P:(m + 1) * P], q2[:, u, m * P:(m + 1) * P], ident16[:])
                last.then_inc(f_qT_psum, 1)

            def second_layer(t, u):
                pe.wait_ge(f_qT, t + 1)
                for m in range(HC):
                    last = pe.matmul(bank(6 + u)[:, 0:D], q2T[:, u, m, :], T2[:, m, :],
                                     start=(m == 0), stop=(m == HC - 1))
                last.then_inc(f_y, 1)

            def stage2_tile(t, u, j, ahead):
                transposes(t, u)
                if ahead:
                    first_layer(t + 3, 1 - u, j)
                second_layer(t, u)

            def c_transposes(b, g):
                pe.wait_ge(c_n, GB * b + g + 1)
                transpose_group(lambda c: DC * g + c, lambda j: n3[:, G * g + j, :]).then_inc(c_nT_psum, 1)

            for t in range(3):
                first_layer(t, t % 2, t, t >= 2)
            stage2_tile(0, 0, 3, True)
            with pe.Fori(0, NT // G - 1) as i:
                for q in range(G):
                    stage2_tile(G * i + 1 + q, (q + 1) % 2, q, True)
            for t in range(NT - G + 1, NT):
                stage2_tile(t, t % 2, 0, False)
            for g in range(GB):
                c_transposes(0, g)
            stage_end(pe, END_2)

            pe.wait_ge(in_late, 16 * 8)

            def c_queries(b, g):
                pe.wait_ge(c_nT, GB * b + g + 1)
                if b and g == 0:
                    pe.wait_ge(c_acc, TB * b)
                for o in range(DC):
                    product(bank((4 + DC * g + o) % 5), lambda c: M1[:, c, o * P:(o + 1) * P],
                            lambda c: nT[:, c, g * 512:(g + 1) * 512]).then_inc(c_qm_psum, 1)

            def c_values(b, i):
                if 1 <= i <= 4:
                    pe.wait_ge(c_qm, DC * GB * b + i)
                elif i > 4:
                    pe.wait_ge(c_vp, TB * b + i - 4)
                product(bank((8 + i) % 5)[:, 0:DV], lambda c: nT[:, c, i * P:(i + 1) * P],
                        lambda c: WVA[:, b, c, :]).then_inc(c_vp_psum, 1)

            def c_score(b, i):
                L = (i + 1) * P
                for h in range((L + 511) // 512):
                    n = min(512, L - h * 512)
                    for c in range(DC):
                        last = pe.matmul(bank(h)[:, 0:n], QmT[:, c, i * P:(i + 1) * P],
                                         nT[:, c, h * 512:h * 512 + n], start=(c == 0),
                                         stop=(c == DC - 1 and h != i // 4))
                    if h == i // 4:
                        last = pe.matmul(bank(h)[:, (i % 4) * P:(i % 4 + 1) * P], ident[:], causal[:],
                                         start=False, stop=True)
                last.then_inc(c_scores, 1)

            def c_tile(b, i):
                pe.wait_ge(c_exp, TB * b + i + 1)
                for j in range(i + 1):
                    last = pe.transpose(bank(2 + j // 4)[:, (j % 4) * P:(j % 4 + 1) * P],
                                        Pr[:, j * P:(j + 1) * P], ident[:])
                last.then_inc(c_pT_psum, 1)
                if i + 1 < TB:
                    c_score(b, i + 1)
                pe.wait_ge(c_pT, TB * b + i + 1)
                if i:
                    pe.wait_ge(c_acc, TB * b + i)
                product(bank(4)[:, 0:DV], lambda j: PT[:, j * P:(j + 1) * P],
                        lambda j: VP[:, j, :], i + 1).then_inc(c_att, 1)

            def d_transposes(b, g, what):
                for c in range(DC):
                    at, full = d_ring(b).fill(pe, d_turn(b), g, what, c)
                    for j in range(G):
                        last = pe.transpose(at[:, j * P:(j + 1) * P], acc[:, b, g, j, c * P:(c + 1) * P],
                                            ident[:])
                    last.then_inc(full, 1)

            def d_probsT(b, g):
                pe.wait_ge(d_exp, GB * b + g + 1)
                at, full = d_ring(b).fill(pe, d_turn(b), g, "pT")
                for j in range(G):
                    last = pe.transpose(at[0:C, j * P:(j + 1) * P], s2raw[:, b, g, j, :], ident[:])
                last.then_inc(full, 1)

            def d_attention(b, g):
                pe.wait_ge(d_pT, GB * b + g + 1)
                for h in range(2):
                    at, full = d_ring(b).fill(pe, d_turn(b), g, "att", h)
                    for j in (2 * h, 2 * h + 1):
                        last = pe.matmul(at[:, (j % 2) * D:(j % 2 + 1) * D], p2T[:, g, j * P:(j + 1) * P],
                                         V2[:, b, :], start=True, stop=True)
                    last.then_inc(full, 1)

            def d_norm2T(b, g):
                pe.wait_ge(d_norm2, GB * b + g + 1)
                d_transposes(b, g, "nT")

            def d_first(b, g):
                pe.wait_ge(d_nT, GB * b + g + 1)
                for o in range(DC):
                    at, full = d_ring(b).fill(pe, d_turn(b), g, "pre", o)
                    product(at, lambda c: F1_s[:, c, o * P:(o + 1) * P], lambda c: ffT[:, g, c, :]
                            ).then_inc(full, 1)

            def d_second(b, g):
                pe.wait_ge(d_hT, GB * b + g + 1)
                for h in range(2):
                    at, full = d_ring(b).fill(pe, d_turn(b), g, "ff", h)
                    for j in (2 * h, 2 * h + 1):
                        last = product(at[:, (j % 2) * D:(j % 2 + 1) * D],
                                       lambda c: ffT[:, g, c, j * P:(j + 1) * P], lambda c: F2_s[:, c, :])
                    last.then_inc(full, 1)

            def d_norm4T(b, g):
                pe.wait_ge(d_n4, GB * b + g + 1)
                d_transposes(b, g, "n4T")

            def d_gate_logits(b, g):
                pe.wait_ge(d_n4T, GB * b + g + 1)
                at, full = d_ring(b).fill(pe, d_turn(b), g, "logits")
                for j in range(G):
                    last = product(at[:, j * E:(j + 1) * E], lambda c: ffT[:, g, c, j * P:(j + 1) * P],
                                   lambda c: Wg_s[:, c, :])
                last.then_inc(full, 1)

            for b in range(B):
                y = b - 1
                if b:
                    c_transposes(b, 0)
                    d_probsT(y, 0)
                    c_transposes(b, 1)
                c_queries(b, 0)
                if y >= 0:
                    d_probsT(y, 1)
                    d_attention(y, 0)
                c_queries(b, 1)
                for i in range(TB):
                    c_values(b, i)
                    if y >= 0 and i == 3:
                        d_attention(y, 1)
                pe.wait_ge(c_vp, TB * (b + 1))
                c_score(b, 0)
                for i in range(TB):
                    c_tile(b, i)
                    if y < 0:
                        continue
                    if i < 2:
                        d_norm2T(y, i)
                    elif i == 2:
                        d_first(y, 0)
                        d_first(y, 1)
                    elif i == 3:
                        d_second(y, 0)
                    elif i == 4:
                        d_second(y, 1)
                if y >= 0:
                    for g in range(GB):
                        d_norm4T(y, g)
                    for g in range(GB):
                        d_gate_logits(y, g)
            y = B - 1
            for part in (d_probsT, d_attention):
                for g in range(GB):
                    part(y, g)
            d_norm2T(y, 0)
            d_first(y, 0)
            d_norm2T(y, 1)
            d_second(y, 0)
            d_first(y, 1)
            d_second(y, 1)
            for g in range(GB):
                d_norm4T(y, g)
                d_gate_logits(y, g)
            stage_end(pe, END_3)

            pe.wait_ge(r_const, 1)
            pe.wait_ge(r_count, 1)
            flat_count = count[:].rearrange("p t e -> p (t e)")
            pe.matmul(bank(0)[:, 0:NT * E], strictly_lower[:], flat_count, start=True, stop=True)
            pe.matmul(bank(1)[:, 0:NT * E], ones5[:], flat_count, start=True, stop=True).then_inc(r_prefix, 1)
            pe.wait_ge(r_combine, 1)
            for t in range(NT):
                last = pe.transpose(ps[0:E, 4 + t // 4, (t % 4) * P:(t % 4 + 1) * P], combine[:, t, :], ident[:])
            last.then_inc(r_cT_psum, 1)
            pe.wait_ge(r_cT, 1)

            def second_biases(n):
                for j in range(4):
                    last = pe.matmul(bank(B2_BANKS[n] + j // 2)[:, (j % 2) * D:(j % 2 + 1) * D],
                                     combineT[:, 4 * n + j, :], e2b_s[:], start=True, stop=True)
                last.then_inc(r_b2, 1)

            second_biases(0)
            second_biases(1)
            for q in range(NTK // 8):
                pe.wait_ge(r_hot, q + 1)
                for k in range(8):
                    n = 8 * q + k
                    last = pe.matmul(bank(2)[:, 0:2 * TILES], hot_lo[:, q % 2, k, :],
                                     coded[:, n, :, :].rearrange("p a j -> p (a j)"),
                                     start=(n == 0), stop=(n == NTK - 1))
                last.then_inc(r_hot_used, 1)
                if q == NTK // 8 - 1:
                    pe.drain().then_inc(r_code, 1)
            second_biases(2)
            pe.wait_ge(r_b2_in, 1)
            second_biases(3)

            def tile_in(j, turn):
                u = j[1] % U
                pe.wait_ge(m_rows[u], 16 * (turn + 1))
                for n in range(2 * DC):
                    last = pe.transpose(bank16(6 * (j[1] % 2))[:, n * P:(n + 1) * P],
                                        rows_in[:, u, n * P:(n + 1) * P], ident16[:])
                last.then_inc(m_xT_psum, 1)

            def experts_from(first, n):
                held = pe.value_load(packed[0:1, bass.ds(first, 1)], min_val=0, max_val=(1 << 8 * BITS) - 1)
                return [((held >> BITS * k) & (1 << BITS) - 1) for k in range(n)]

            def first_chunk(j, e, m):
                u, v = j[1] % U, j[1] % 2
                dst = bank(2 + 2 * v + m // 4)[:, (m % 4) * P:(m % 4 + 1) * P]
                hi, lo = expert_w1_at(EWS, e, 0, DC, H), expert_w1_at(EWS, e, 1, DC, H)
                terms = [(w(c, m), xT[:, u, a, c, :]) for c in range(DC) for w, a in ((hi, 0), (hi, 1), (lo, 0))]
                for n, (lhsT, rhs) in enumerate(terms):
                    last = pe.matmul(dst, lhsT, rhs, start=(n == 0), stop=(n == len(terms) - 1))
                return last

            def second_chunk(j, e, m):
                v = j[1] % 2
                at = bank(1 + 6 * v)
                pe.matmul(at, hid16[:, v, 0, m, :], expert_w2_at(EWS, e, m, 2, DC, H, D), start=(m == 0),
                          stop=False)
                return pe.matmul(at[:, 0:D], hid16[:, v, 1, m, :], expert_w2_at(EWS, e, m, 1, DC, H, D),
                                 start=False, stop=(m == HC - 1))

            def products(j, e_first, e_second):
                if e_first is not None:
                    pe.wait_ge(m_xT, j[0] + 1)
                    pe.wait_ge(m_hid, j[0] - 1) if j[1] >= 2 else None
                if e_second is not None:
                    pe.wait_ge(m_hid16, j[0] - 1)
                for m in range(HC):
                    if e_first is not None:
                        last = first_chunk(j, e_first, m)
                        if m == HC - 1:
                            last.then_inc(m_hid_psum, 1)
                    if e_second is not None:
                        last = second_chunk(j, e_second, m)
                        if m == HC - 1:
                            last.then_inc(m_y_psum, 1)

            pe.wait_ge(r_expert, 1)
            pe.wait_ge(r_b2_in, 4)
            pe.wait_ge(block_split, E * EBLK)
            tile_in((0, 0), 0)
            tile_in((1, 1), 0)
            pe.wait_ge(r_packed, 1)
            e = experts_from(0, TURN)
            products((0, 0), e[0], None)
            tile_in((2, 2), 0)
            products((1, 1), e[1], None)
            for j in range(2, TURN):
                tile_in((j + 1, j + 1), (j + 1) // U)
                products((j, j), e[j], e[j - 2])
            with pe.Fori(1, TILES // TURN) as i:
                e = experts_from(TURN * i - 2, TURN + 2)
                for q in range(TURN):
                    tile_in((TURN * i + q + 1, q + TURN + 1), 2 * i + (q + 1) // U)
                    products((TURN * i + q, q + TURN), e[q + 2], e[q])
            rest = TILES // TURN * TURN
            e = experts_from(rest - 2, TILES - rest + 2)
            for j in range(rest, TILES + 2):
                if j + 1 < TILES:
                    tile_in((j + 1, j + 1), (j + 1) // U)
                products((j, j), e[j - rest + 2] if j < TILES else None, e[j - rest])
            stage_end(pe, END_5)


def count_total(ps, NT, E):
    return ps[:, 1, 0:NT * E].rearrange("p (t e) -> p t e", t=NT)


def q1T_flat(q1T, t, c, j, G, P, DC):
    flat = q1T[:].rearrange("p g c n -> p (g c n)")
    return flat[:, bass.ds((t - j) * (DC * P) + c * G * P + j * P, P)]


def expert_w1_at(EWS, e, part, DC, H):
    mine = EWS[:, bass.ds(e, 1), :].rearrange("p o n -> p (o n)")
    return lambda c, m: mine[:, part * DC * H + c * H + m * P:part * DC * H + c * H + (m + 1) * P]


def expert_w2_at(EWS, e, m, parts, DC, H, D):
    mine = EWS[:, bass.ds(e, 1), :].rearrange("p o n -> p (o n)")
    first = 2 * DC * H + 2 * m * D
    return mine[:, first:first + parts * D]


_INS = ['x', 'ctx_1024', 'g_xattn', 'g_ffn', 'L0_xattn_W', 'L0_xattn_b', 'L0_ffn_ln1_g', 'L0_ffn_ln1_b',
        'L0_ffn_w1', 'L0_ffn_b1', 'L0_ffn_ln2_g', 'L0_ffn_ln2_b', 'L0_ffn_w2', 'L0_ffn_b2',
        'L1_xattn_Wk1', 'L1_xattn_Wq1', 'L1_xattn_Wv1', 'L1_xattn_Wk2', 'L1_xattn_Wq2', 'L1_xattn_Wv2',
        'L1_xattn_W1', 'L1_xattn_b1', 'L1_xattn_W2', 'L1_xattn_b2', 'L1_xattn_gamma', 'L1_xattn_beta',
        'L1_ffn_Wg', 'L1_ffn_bg', 'L1_ffn_W1', 'L1_ffn_b1', 'L1_ffn_W2', 'L1_ffn_b2']
_OUTS = [((2, 1024, 256), 'float32')]


def kernel(**inputs):
    import numpy as _np
    import concourse.bacc as _bacc
    from concourse import mybir as _mybir
    from concourse.bass_utils import run_bass_kernel_spmd as _run

    nc = _bacc.Bacc("TRN2", target_bir_lowering=False, num_devices=1)
    arrays, args = {}, []
    for name in _INS:
        a = _np.ascontiguousarray(inputs[name])
        arrays[f"in_{name}_dram"] = a
        args.append(nc.dram_tensor(f"in_{name}_dram", a.shape, _mybir.dt.from_np(a.dtype), kind="ExternalInput").ap())
    for i, (shape, dtype) in enumerate(_OUTS):
        dt = _mybir.dt.from_np(_np.dtype(dtype))
        args.append(nc.dram_tensor(f"out_{i}_dram", shape, dt, kind="ExternalOutput").ap())
    gated_blocks_kernel(nc, *args)
    r = _run(nc, [arrays], core_ids=[0])
    got = tuple(r.results[0][f"out_{i}_dram"] for i in range(len(_OUTS)))
    return got[0]
```
